# Optimizing a Trainium2 kernel written in Bass

```python
import numpy as np
import jax
import jax.numpy as jnp

def _softmax(x, axis=-1):
    return jax.nn.softmax(x, axis=axis)

def _gelu(x):
    return jax.nn.gelu(x, approximate=True)

def _silu(x):
    return jax.nn.silu(x)

def _sigmoid(x):
    return jax.nn.sigmoid(x)

def _layernorm(x, axis=-1, eps=1e-05):
    m = jnp.mean(x, axis=axis, keepdims=True)
    v = jnp.var(x, axis=axis, keepdims=True)
    return (x - m) / jnp.sqrt(v + eps)

def _scatter_add(tgt, idx, src, axis=0):
    return tgt.at[idx].add(src)

def _segment_sum(src, seg, n):
    return jax.ops.segment_sum(src, seg, n)
kernel_name = 'mk_audio_tower_d1_tok_audfeat512_r4_9bf9b0'

def setup_inputs(seed: int=0):
    np.random.seed(seed)
    _w = jnp.asarray

    def _rec_inputs():
        import jax
        import jax.numpy as jnp
        _rk = jax.random.key(seed)
        x = 7.22013e-05 + 1.00017 * jax.random.normal(jax.random.fold_in(_rk, 1), (32, 256, 64), jnp.float32)
        return x
    x = _rec_inputs()

    def _L0_tok_setup():
        import jax, jax.numpy as jnp
        import numpy as np
        EPS = 1e-07
        C_CURV = 1.0
        LAM_HALF = 1.0 / (1.0 + EPS)
        key = jax.random.key(seed)
        k1, k2 = jax.random.split(key)
        B, L, Cin, K, F = (32, 256, 64, 9, 128)
        x = jax.random.normal(k1, (B, L, Cin), dtype=jnp.float32)
        lim = float(np.sqrt(6.0 / (K * Cin + F)))
        kernel = jax.random.uniform(k2, (K, Cin, F), dtype=jnp.float32, minval=-lim, maxval=lim)
        bias = jnp.zeros((F,), dtype=jnp.float32)
        return {'x': x, 'kernel': kernel, 'bias': bias}
    _L0_tok_all = _L0_tok_setup()
    _L0_tok_in = {k: v for k, v in _L0_tok_all.items() if k in ('kernel', 'bias')}
    del _L0_tok_all

    def _L0_attn_setup():
        import jax, jax.numpy as jnp
        import numpy as np
        from jax import lax
        D_MODEL = 128
        EXPAND = 2
        D_INNER = EXPAND * D_MODEL
        HEADDIM = 64
        NHEADS = D_INNER // HEADDIM
        D_STATE = 64
        NGROUPS = 1
        D_CONV = 4
        CONV_DIM = D_INNER + 2 * NGROUPS * D_STATE
        D_IN_PROJ = 2 * D_INNER + 2 * NGROUPS * D_STATE + NHEADS
        EPS = 1e-05

        def _mamba2(x, in_proj_w, conv_w, conv_b, dt_bias, A_log, D_skip, norm_w, out_proj_w):
            B, Lp, _ = x.shape
            zxbcdt = x @ in_proj_w
            z = zxbcdt[..., :D_INNER]
            xBC = zxbcdt[..., D_INNER:D_INNER + CONV_DIM]
            dt = zxbcdt[..., D_INNER + CONV_DIM:]
            xBC_c = lax.conv_general_dilated(xBC.transpose(0, 2, 1), conv_w, window_strides=(1,), padding=[(D_CONV - 1, 0)], feature_group_count=CONV_DIM, dimension_numbers=('NCH', 'OIH', 'NCH'))
            xBC = jax.nn.silu(xBC_c.transpose(0, 2, 1) + conv_b)
            xs = xBC[..., :D_INNER]
            Bm = xBC[..., D_INNER:D_INNER + NGROUPS * D_STATE]
            Cm = xBC[..., D_INNER + NGROUPS * D_STATE:]
            dt = jax.nn.softplus(dt + dt_bias)
            A = -jnp.exp(A_log)
            xh = xs.reshape(B, Lp, NHEADS, HEADDIM)
            decay = jnp.exp(dt * A)
            dtx = dt[..., None] * xh

            def step(h, inp):
                dec_t, dtx_t, B_t, C_t = inp
                h = dec_t[:, :, None, None] * h + dtx_t[..., None] * B_t[:, None, None, :]
                y_t = jnp.einsum('bhpn,bn->bhp', h, C_t)
                return (h, y_t)
            h0 = jnp.zeros((B, NHEADS, HEADDIM, D_STATE), x.dtype)
            _, ys = lax.scan(step, h0, (decay.transpose(1, 0, 2), dtx.transpose(1, 0, 2, 3), Bm.transpose(1, 0, 2), Cm.transpose(1, 0, 2)))
            y = ys.transpose(1, 0, 2, 3) + D_skip[None, None, :, None] * xh
            y = y.reshape(B, Lp, D_INNER)
            y = y * jax.nn.silu(z)
            y = y * lax.rsqrt(jnp.mean(y * y, axis=-1, keepdims=True) + EPS) * norm_w
            return y @ out_proj_w
        key = jax.random.key(seed)
        ks = jax.random.split(key, 8)
        x = jax.random.normal(ks[0], (4, 511, D_MODEL), jnp.float32)
        in_proj_w = jax.random.normal(ks[1], (D_MODEL, D_IN_PROJ), jnp.float32) * 0.02
        conv_w = jax.random.normal(ks[2], (CONV_DIM, 1, D_CONV), jnp.float32) * 0.2
        conv_b = jnp.zeros((CONV_DIM,), jnp.float32)
        dt_bias = jax.random.uniform(ks[3], (NHEADS,), jnp.float32, 0.0, 0.1)
        A_log = jnp.log(jax.random.uniform(ks[4], (NHEADS,), jnp.float32, 1.0, 16.0))
        D_skip = jnp.ones((NHEADS,), jnp.float32)
        norm_w = jnp.ones((D_INNER,), jnp.float32)
        out_proj_w = jax.random.normal(ks[5], (D_INNER, D_MODEL), jnp.float32) * 0.02
        return {'x': x, 'in_proj_w': in_proj_w, 'conv_w': conv_w, 'conv_b': conv_b, 'dt_bias': dt_bias, 'A_log': A_log, 'D_skip': D_skip, 'norm_w': norm_w, 'out_proj_w': out_proj_w}
    _L0_attn_all = _L0_attn_setup()
    _L0_attn_in = {k: v for k, v in _L0_attn_all.items() if k in ('in_proj_w', 'conv_w', 'conv_b', 'dt_bias', 'A_log', 'D_skip', 'norm_w', 'out_proj_w')}
    del _L0_attn_all

    def _L0_ffn_setup():
        import jax, jax.numpy as jnp
        import numpy as np
        B, S, D = (4, 256, 128)
        E = 16
        DH = 4 * D
        DS = 2 * D
        TOP_K = 2
        TEMP = 0.7
        SHARED_SCALE = 0.25
        EPS = 1e-05

        def layer_norm(x, g, b):
            mu = jnp.mean(x, axis=-1, keepdims=True)
            var = jnp.mean(jnp.square(x - mu), axis=-1, keepdims=True)
            return (x - mu) * jax.lax.rsqrt(var + EPS) * g + b
        key = jax.random.key(seed)
        ks = jax.random.split(key, 12)
        s = 0.02
        return {'x': jax.random.normal(ks[0], (B, S, D), jnp.float32), 'ln_in_g': jnp.ones((D,), jnp.float32), 'ln_in_b': jnp.zeros((D,), jnp.float32), 'router_w': jax.random.normal(ks[1], (D, E), jnp.float32) * s, 'router_b': jnp.zeros((E,), jnp.float32), 'ew1': jax.random.normal(ks[2], (E, D, DH), jnp.float32) * s, 'eb1': jnp.zeros((E, DH), jnp.float32), 'ew2': jax.random.normal(ks[3], (E, DH, D), jnp.float32) * s, 'eb2': jnp.zeros((E, D), jnp.float32), 'sw1': jax.random.normal(ks[4], (D, DS), jnp.float32) * s, 'sb1': jnp.zeros((DS,), jnp.float32), 'sw2': jax.random.normal(ks[5], (DS, D), jnp.float32) * s, 'sb2': jnp.zeros((D,), jnp.float32), 'ff_ln_g': jnp.ones((D,), jnp.float32), 'ff_ln_b': jnp.zeros((D,), jnp.float32), 'ff_w1': jax.random.normal(ks[6], (D, DH), jnp.float32) * s, 'ff_b1': jnp.zeros((DH,), jnp.float32), 'ff_w2': jax.random.normal(ks[7], (DH, D), jnp.float32) * s, 'ff_b2': jnp.zeros((D,), jnp.float32)}
    _L0_ffn_all = _L0_ffn_setup()
    _L0_ffn_in = {k: v for k, v in _L0_ffn_all.items() if k in ('ln_in_g', 'ln_in_b', 'router_w', 'router_b', 'ew1', 'eb1', 'ew2', 'eb2', 'sw1', 'sb1', 'sw2', 'sb2', 'ff_ln_g', 'ff_ln_b', 'ff_w1', 'ff_b1', 'ff_w2', 'ff_b2')}
    del _L0_ffn_all
    return {'x': x, 'L0_tok_kernel': _L0_tok_in['kernel'], 'L0_tok_bias': _L0_tok_in['bias'], 'L0_attn_in_proj_w': _L0_attn_in['in_proj_w'], 'L0_attn_conv_w': _L0_attn_in['conv_w'], 'L0_attn_conv_b': _L0_attn_in['conv_b'], 'L0_attn_dt_bias': _L0_attn_in['dt_bias'], 'L0_attn_A_log': _L0_attn_in['A_log'], 'L0_attn_D_skip': _L0_attn_in['D_skip'], 'L0_attn_norm_w': _L0_attn_in['norm_w'], 'L0_attn_out_proj_w': _L0_attn_in['out_proj_w'], 'L0_ffn_ln_in_g': _L0_ffn_in['ln_in_g'], 'L0_ffn_ln_in_b': _L0_ffn_in['ln_in_b'], 'L0_ffn_router_w': _L0_ffn_in['router_w'], 'L0_ffn_router_b': _L0_ffn_in['router_b'], 'L0_ffn_ew1': _L0_ffn_in['ew1'], 'L0_ffn_eb1': _L0_ffn_in['eb1'], 'L0_ffn_ew2': _L0_ffn_in['ew2'], 'L0_ffn_eb2': _L0_ffn_in['eb2'], 'L0_ffn_sw1': _L0_ffn_in['sw1'], 'L0_ffn_sb1': _L0_ffn_in['sb1'], 'L0_ffn_sw2': _L0_ffn_in['sw2'], 'L0_ffn_sb2': _L0_ffn_in['sb2'], 'L0_ffn_ff_ln_g': _L0_ffn_in['ff_ln_g'], 'L0_ffn_ff_ln_b': _L0_ffn_in['ff_ln_b'], 'L0_ffn_ff_w1': _L0_ffn_in['ff_w1'], 'L0_ffn_ff_b1': _L0_ffn_in['ff_b1'], 'L0_ffn_ff_w2': _L0_ffn_in['ff_w2'], 'L0_ffn_ff_b2': _L0_ffn_in['ff_b2']}

def reference(x, L0_tok_kernel, L0_tok_bias, L0_attn_in_proj_w, L0_attn_conv_w, L0_attn_conv_b, L0_attn_dt_bias, L0_attn_A_log, L0_attn_D_skip, L0_attn_norm_w, L0_attn_out_proj_w, L0_ffn_ln_in_g, L0_ffn_ln_in_b, L0_ffn_router_w, L0_ffn_router_b, L0_ffn_ew1, L0_ffn_eb1, L0_ffn_ew2, L0_ffn_eb2, L0_ffn_sw1, L0_ffn_sb1, L0_ffn_sw2, L0_ffn_sb2, L0_ffn_ff_ln_g, L0_ffn_ff_ln_b, L0_ffn_ff_w1, L0_ffn_ff_b1, L0_ffn_ff_w2, L0_ffn_ff_b2):
    import jax
    import jax.numpy as jnp

    def _L0_tok_ref(x, kernel, bias):
        import jax, jax.numpy as jnp
        import numpy as np
        EPS = 1e-07
        C_CURV = 1.0
        LAM_HALF = 1.0 / (1.0 + EPS)
        B, L, Cin = x.shape
        K, _, F = kernel.shape
        Lout = L - K + 1
        sq = jnp.sum(x * x, axis=-1)
        cs = jnp.concatenate([jnp.zeros((B, 1), x.dtype), jnp.cumsum(sq, axis=1)], axis=1)
        wsq = cs[:, K:] - cs[:, :Lout]
        wnorm = jnp.sqrt(jnp.maximum(wsq, 0.0))
        scale = jnp.where(wnorm < 1.0, 1.0, 1.0 / (wnorm + EPS))[..., None]
        conv = jax.lax.conv_general_dilated(x, kernel, window_strides=(1,), padding='VALID', dimension_numbers=('NWC', 'WIO', 'NWC'))
        v = conv * scale
        v_norm = jnp.maximum(jnp.abs(v), EPS)
        y = jnp.tanh(v_norm * LAM_HALF) * (v / v_norm)
        return jax.nn.relu(y + bias)

    def _L0_attn_ref(x, in_proj_w, conv_w, conv_b, dt_bias, A_log, D_skip, norm_w, out_proj_w):
        import jax, jax.numpy as jnp
        import numpy as np
        from jax import lax
        D_MODEL = 128
        EXPAND = 2
        D_INNER = EXPAND * D_MODEL
        HEADDIM = 64
        NHEADS = D_INNER // HEADDIM
        D_STATE = 64
        NGROUPS = 1
        D_CONV = 4
        CONV_DIM = D_INNER + 2 * NGROUPS * D_STATE
        D_IN_PROJ = 2 * D_INNER + 2 * NGROUPS * D_STATE + NHEADS
        EPS = 1e-05

        def _mamba2(x, in_proj_w, conv_w, conv_b, dt_bias, A_log, D_skip, norm_w, out_proj_w):
            B, Lp, _ = x.shape
            zxbcdt = x @ in_proj_w
            z = zxbcdt[..., :D_INNER]
            xBC = zxbcdt[..., D_INNER:D_INNER + CONV_DIM]
            dt = zxbcdt[..., D_INNER + CONV_DIM:]
            xBC_c = lax.conv_general_dilated(xBC.transpose(0, 2, 1), conv_w, window_strides=(1,), padding=[(D_CONV - 1, 0)], feature_group_count=CONV_DIM, dimension_numbers=('NCH', 'OIH', 'NCH'))
            xBC = jax.nn.silu(xBC_c.transpose(0, 2, 1) + conv_b)
            xs = xBC[..., :D_INNER]
            Bm = xBC[..., D_INNER:D_INNER + NGROUPS * D_STATE]
            Cm = xBC[..., D_INNER + NGROUPS * D_STATE:]
            dt = jax.nn.softplus(dt + dt_bias)
            A = -jnp.exp(A_log)
            xh = xs.reshape(B, Lp, NHEADS, HEADDIM)
            decay = jnp.exp(dt * A)
            dtx = dt[..., None] * xh

            def step(h, inp):
                dec_t, dtx_t, B_t, C_t = inp
                h = dec_t[:, :, None, None] * h + dtx_t[..., None] * B_t[:, None, None, :]
                y_t = jnp.einsum('bhpn,bn->bhp', h, C_t)
                return (h, y_t)
            h0 = jnp.zeros((B, NHEADS, HEADDIM, D_STATE), x.dtype)
            _, ys = lax.scan(step, h0, (decay.transpose(1, 0, 2), dtx.transpose(1, 0, 2, 3), Bm.transpose(1, 0, 2), Cm.transpose(1, 0, 2)))
            y = ys.transpose(1, 0, 2, 3) + D_skip[None, None, :, None] * xh
            y = y.reshape(B, Lp, D_INNER)
            y = y * jax.nn.silu(z)
            y = y * lax.rsqrt(jnp.mean(y * y, axis=-1, keepdims=True) + EPS) * norm_w
            return y @ out_proj_w
        L = x.shape[1]
        pad = -L % 8
        xp = jnp.pad(x, ((0, 0), (0, pad), (0, 0))) if pad else x
        out = _mamba2(xp, in_proj_w, conv_w, conv_b, dt_bias, A_log, D_skip, norm_w, out_proj_w)
        return out[:, :L, :]

    def _L0_ffn_ref(x, ln_in_g, ln_in_b, router_w, router_b, ew1, eb1, ew2, eb2, sw1, sb1, sw2, sb2, ff_ln_g, ff_ln_b, ff_w1, ff_b1, ff_w2, ff_b2):
        import jax, jax.numpy as jnp
        import numpy as np
        B, S, D = (4, 256, 128)
        E = 16
        DH = 4 * D
        DS = 2 * D
        TOP_K = 2
        TEMP = 0.7
        SHARED_SCALE = 0.25
        EPS = 1e-05

        def layer_norm(x, g, b):
            mu = jnp.mean(x, axis=-1, keepdims=True)
            var = jnp.mean(jnp.square(x - mu), axis=-1, keepdims=True)
            return (x - mu) * jax.lax.rsqrt(var + EPS) * g + b
        h = layer_norm(x, ln_in_g, ln_in_b)
        gate = jax.nn.softmax((h @ router_w + router_b) / TEMP, axis=-1)
        vals, idx = jax.lax.top_k(gate, TOP_K)
        comb = jnp.sum(jax.nn.one_hot(idx, E, dtype=h.dtype) * vals[..., None], axis=-2)
        eh = jax.nn.silu(jnp.einsum('bsd,edh->ebsh', h, ew1) + eb1[:, None, None, :])
        ey = jnp.einsum('ebsh,ehd->ebsd', eh, ew2) + eb2[:, None, None, :]
        mix = jnp.einsum('bse,ebsd->bsd', comb, ey)
        shared = (jax.nn.silu(h @ sw1 + sb1) @ sw2 + sb2) * SHARED_SCALE
        moe_out = mix + shared
        fh = layer_norm(moe_out, ff_ln_g, ff_ln_b)
        ff_out = jax.nn.silu(fh @ ff_w1 + ff_b1) @ ff_w2 + ff_b2
        return x + moe_out + ff_out
    h = _L0_tok_ref(x, L0_tok_kernel, L0_tok_bias)
    h = h + _L0_attn_ref(_layernorm(h, axis=-1), L0_attn_in_proj_w, L0_attn_conv_w, L0_attn_conv_b, L0_attn_dt_bias, L0_attn_A_log, L0_attn_D_skip, L0_attn_norm_w, L0_attn_out_proj_w)
    h = h + _L0_ffn_ref(_layernorm(h, axis=-1), L0_ffn_ln_in_g, L0_ffn_ln_in_b, L0_ffn_router_w, L0_ffn_router_b, L0_ffn_ew1, L0_ffn_eb1, L0_ffn_ew2, L0_ffn_eb2, L0_ffn_sw1, L0_ffn_sb1, L0_ffn_sw2, L0_ffn_sb2, L0_ffn_ff_ln_g, L0_ffn_ff_ln_b, L0_ffn_ff_w1, L0_ffn_ff_b1, L0_ffn_ff_w2, L0_ffn_ff_b2)
    return h

_drawn_inputs = setup_inputs


def setup_inputs(seed=0):
    import zlib

    import numpy as np

    out = dict(_drawn_inputs(seed))
    spreads = {'L0_tok_bias': (0.0, 0.1),
     'L0_attn_conv_b': (0.0, 0.1),
     'L0_attn_D_skip': (1.0, 0.2),
     'L0_attn_norm_w': (1.0, 0.2),
     'L0_ffn_ln_in_g': (1.0, 0.6),
     'L0_ffn_ln_in_b': (0.0, 0.8),
     'L0_ffn_router_b': (0.0, 0.614),
     'L0_ffn_eb1': (0.0, 0.8),
     'L0_ffn_eb2': (0.0, 0.422),
     'L0_ffn_sb1': (0.0, 0.8),
     'L0_ffn_sb2': (0.0, 0.707),
     'L0_ffn_ff_ln_g': (1.0, 0.6),
     'L0_ffn_ff_ln_b': (0.0, 2.0),
     'L0_ffn_ff_b1': (0.0, 0.506),
     'L0_ffn_ff_b2': (0.0, 0.1)}
    factors = {'L0_attn_dt_bias': 8.0,
     'L0_attn_A_log': 8.0,
     'L0_ffn_router_w': 2.874,
     'L0_ffn_ew1': 5.256,
     'L0_ffn_ew2': 5.108,
     'L0_ffn_sw1': 4.361,
     'L0_ffn_sw2': 3.9}
    for name, (base, spread) in spreads.items():
        noise = np.random.default_rng([zlib.crc32(name.encode()), seed]).standard_normal(out[name].shape)
        drawn = base * np.exp(spread * noise) if base else spread * noise
        out[name] = jnp.asarray(drawn.astype(out[name].dtype))
    for name, factor in factors.items():
        out[name] = (out[name] * factor).astype(out[name].dtype)
    return out
```

```python
import concourse.bass as bass
from concourse import mybir
from collections import namedtuple
from contextlib import ExitStack

Unit = namedtuple("Unit", "u n q")


def skewed(eng, body, units, turns=2):
    def unit(i, c):
        return Unit(turns * i + c, i + c // turns, c % turns)

    body(unit(0, 0), None, None)
    body(unit(0, 1), unit(0, 0), None)
    for c in range(turns):
        body(unit(0, c + 2), unit(0, c + 1), unit(0, c))
    rounds = (units - 2) // turns
    with eng.Fori(1, rounds) as i:
        for c in range(turns):
            body(unit(i, c + 2), unit(i, c + 1), unit(i, c))
    for c in range(rounds * turns, units - 2):
        body(unit(0, c + 2), unit(0, c + 1), unit(0, c))
    body(None, unit(0, units - 1), unit(0, units - 2))
    body(None, None, unit(0, units - 1))


def streamed(eng, step, units, turns=2):
    def unit(i, c):
        return Unit(turns * i + c, i + c // turns, c % turns)

    for c in range(turns):
        step(unit(0, c))
    with eng.Fori(1, units // turns) as i:
        for c in range(turns):
            step(unit(i, c))
    for c in range(units // turns * turns, units):
        step(unit(0, c))


def later(eng, counter, value):
    if not isinstance(value, int) or value > 0:
        eng.wait_ge(counter, value)


def audio_tower(nc, x2, tok_kernel, tok_bias, in_proj, conv_w, conv_b, dt_bias, A_log, D_skip, norm_w,
                out_proj, ln_g, ln_b, router_w, router_b, ew1, eb1, ew2, eb2, sw1, sb1, sw2, sb2,
                ffg, ffb, fw1, fb1, fw2, fb2, out):
    fp32 = mybir.dt.float32
    bf16 = mybir.dt.bfloat16
    i32 = mybir.dt.int32
    ALU = mybir.AluOpType
    ACT = mybir.ActivationFunctionType
    AX = mybir.AxisListType
    ds = bass.ds

    SEQS, LIN, CIN, TAPS = 32, 256, 64, 9
    L = LIN - TAPS + 1
    F = 128
    CH = L // 2
    UNITS = SEQS // 2
    NCH = 2 * SEQS
    UT = 2 * L
    NH, HD, NS = 4, 64, 64
    DI = NH * HD
    KC = 4
    PADL = KC - 1
    E, DH, DSH = 16, 512, 256
    NF = DH // 128
    TEMP = 0.7
    EPS = 1e-5
    TOK_EPS = 1e-7
    LAM = 1.0 / (1.0 + TOK_EPS)
    T = SEQS * L
    BLK = 128
    NBLK = (2 * T) // BLK + E
    NBLK += NBLK % 2
    SLOTS = NBLK * BLK
    CB = E + 1
    EXP1 = 2.718281828459045

    x_slots = nc.dram_tensor("x_slots", (SLOTS, F), fp32, kind="Internal").ap()
    bias_parts = nc.dram_tensor("bias_parts", (3, E, DH), bf16, kind="Internal").ap()
    y_slots = nc.dram_tensor("y_slots", (SLOTS, F), fp32, kind="Internal").ap()

    ctx = ExitStack()
    with ctx:
        def sb(name, shape, dt=fp32):
            return ctx.enter_context(nc.sbuf_tensor(name, shape, dt))

        def sem(name):
            return ctx.enter_context(nc.semaphore(name))

        ident = sb("ident", [128, 128])
        ones_col = sb("ones_col", [128, 1])
        minus_half = sb("minus_half", [128, 64])
        plus_half = sb("plus_half", [128, 64])
        euler = sb("euler", [128, 16])
        eps_row = sb("eps_row", [128, 16])
        keep = sb("keep", [CH, 4 * NH])
        wait_carrier = sb("wait_carrier", [1, 1])
        tokb = sb("tokb", [CH, F])
        cb = sb("cb", [128, 3])
        dtb = sb("dtb", [CH, NH])
        a_log = sb("a_log", [CH, NH])
        a_neg = sb("a_neg", [CH, 4, NH])
        d_col = sb("d_col", [128, 2])
        nw = sb("nw", [128, 2])
        scale = sb("scale", [CH, NCH])
        lng = sb("lng", [128, 1])
        lnb = sb("lnb", [128, 1])
        rw = sb("rw", [128, E])
        rb = sb("rb", [CH, E])
        w_s1 = sb("w_s1", [128, DSH])
        b_s1 = sb("b_s1", [128, 2])
        w_s2 = sb("w_s2", [128, 2, F])
        w_e2b = sb("w_e2b", [CB, F])
        fg = sb("fg", [128, 1])
        fbb = sb("fbb", [128, 1])
        w_f1 = sb("w_f1", [128, DH])
        b_f1 = sb("b_f1", [128, NF])
        w_f2 = sb("w_f2", [128, NF, F])
        bias3 = sb("bias3", [3, E * DH], bf16)
        ones3 = sb("ones3", [3, BLK], bf16)
        tri = sb("tri", [CH, CH], bf16)
        ones_sq = sb("ones_sq", [CH, 128], bf16)

        MV = sb("MV", [CH, NCH, 2])
        COMB = sb("COMB", [CH, NCH * CB])
        VAL = sb("VAL", [CH, 2, NCH])
        IDX = sb("IDX", [128, NCH, 2], i32)
        idx_st = [sb(f"idx_st{q}", [128, 8], i32) for q in range(2)]
        EOFF = sb("EOFF", [1, NBLK], i32)
        cumP = sb("cumP", [128, E])
        block_no = sb("block_no", [1, NBLK])
        rev_iota = sb("rev_iota", [128, E])
        st3 = sb("st3", [CH, 4, 6])
        mv3 = sb("mv3", [CH, 4, 2])
        ve3 = sb("ve3", [CH, 4])
        rs3 = sb("rs3", [CH, 4])
        b_f2 = sb("b_f2", [CH, F])
        Hb = sb("Hb", [CH, NCH * F])

        ARENA = 36300
        arena = sb("arena", [128, ARENA])

        pos = [0]

        def take(parts, *shape):
            n = 1
            for k in shape:
                n *= k
            v = arena[0:parts, pos[0]:pos[0] + n]
            pos[0] += n
            assert pos[0] <= ARENA, pos[0]
            if len(shape) == 2:
                v = v.rearrange("p (a b) -> p a b", b=shape[1])
            if len(shape) == 3:
                v = v.rearrange("p (a b c) -> p a b c", b=shape[1], c=shape[2])
            return v

        pos[0] = 0
        x_all = take(128, 2 * SEQS, CIN)
        x_sq = take(128, 2 * SEQS, CIN)
        sq = take(128, 2 * SEQS)
        wsq = take(CH, NCH)
        wnorm = take(CH, NCH)
        small = take(CH, NCH)
        wmix = take(CH, NCH)
        band = take(128, 4, CH)
        cw = take(128, 384 * KC)
        b_e1 = take(E, DH)
        b_e1f = take(E, DH)
        b_part = take(E, 3, DH // 2).bitcast(bf16)
        zero_src = take(128, 10 * F)
        iota_i = take(128, E).bitcast(i32)
        iota_b = take(1, NBLK).bitcast(i32)
        assert pos[0] <= 14800
        pos[0] = 0
        xin = [take(128, 4, 128) for _ in range(2)]
        xT = take(128, 4 * 128)
        v_s = take(CH, 4 * F)
        v_t = take(CH, 4 * F)
        v_b = take(CH, 4 * F)
        hn = take(CH, 4, F)
        Z = [take(128, 2, UT) for _ in range(2)]
        XT = [take(128, 2, UT) for _ in range(2)]
        BT = [take(64, UT) for _ in range(2)]
        CT = [take(64, UT) for _ in range(2)]
        dt = [take(CH, 4 * NH) for _ in range(2)]
        dec = [take(CH, 4, NH) for _ in range(2)]
        Xd = take(CH, 4, DI)
        L0 = take(CH, NH, L)
        L1 = take(CH, NH, CH)
        M0 = take(CH, NH, L)
        M1 = take(CH, NH, CH)
        Tg = take(128, 2, UT)
        Yg = take(128, 2, UT)
        Sq = take(128, 2, UT)
        st = take(CH, 4, 6)
        mv = take(CH, 4, 2)
        ve = take(CH, 4)
        rstd = take(CH, 4)
        ms = take(CH, 4)
        rr = take(CH, 4)
        uu = take(CH, 16)
        nab = take(CH, 16)
        ee = take(CH, 16)
        qq = take(CH, 16)
        rq = take(CH, 16)
        ss = take(CH, 16)
        s2 = take(CH, 16)
        pa = take(CH, 16)
        pb = take(CH, 16)
        tt = take(CH, 16)
        dA = take(CH, 16)
        ee2 = take(CH, 16)
        pos[0] = max(pos[0], 14800)
        diag2 = take(CH, 2, L)
        tokw = take(128, 5, F)
        w_in = take(F, 644)
        w_tap = take(F, KC, 384)
        w_out = take(128, 2, F)
        hnT = [take(128, 2, L + PADL) for _ in range(2)]
        pos[0] = 0
        XNR = take(CH, NCH * F)
        HHT = take(128, UNITS * 512)
        MOE = HHT[0:CH, :]
        w1 = take(128, E * DH)
        w2 = take(128, E * DH)
        staging_at = pos[0]
        pos[0] = staging_at - 2 * E * DH
        LG = take(CH, NCH * E)
        r12 = take(CH, NCH)
        r1p = take(CH, NCH)
        nmr = take(CH, NCH)
        v64 = [take(CH, NCH) for _ in range(4)]
        xnr = [take(CH, 4, F) for _ in range(2)]
        hhT = [take(128, UT) for _ in range(2)]
        big = [take(128, NCH * E) for _ in range(9)]
        sml = [take(128, E) for _ in range(8)]
        row = [take(CH, NCH) for _ in range(6)]
        mask = take(CH, NCH * E // 2).bitcast(bf16)
        sml_blocks = take(1, NBLK)
        assert pos[0] <= staging_at
        pos[0] = staging_at
        x_st = [take(128, 4 * F) for _ in range(2)]
        comb_st = take(CH, 4, CB)
        combT = take(CB, UT)
        SH = take(128, 2, UT)
        pos[0] = staging_at
        pos[0] = 0
        xb = [take(128, F) for _ in range(4)]
        hT = [take(128, F) for _ in range(2)]
        EH = [take(128, DH) for _ in range(2)]
        EHT = [take(128, DH) for _ in range(2)]
        YO = [take(128, F) for _ in range(4)]
        assert pos[0] <= NCH * F
        pos[0] = 0
        GY = [take(128, 8, F) for _ in range(2)]
        mo = [take(CH, 4, F) for _ in range(2)]
        fh = take(CH, 4, F)
        fhT = take(128, UT)
        FH = take(128, NF, UT)
        rest = take(CH, 4 * F)
        h_st = [take(CH, 4 * F) for _ in range(2)]
        pos[0] = staging_at
        outb = [take(CH, 4 * F) for _ in range(2)]
        rest2 = take(CH, 4 * F)

        psum = ctx.enter_context(nc.psum_tensor("psum", [128, 8, 512], fp32))

        chain_count = {}

        def link(eng, counter, ins):
            chain_count[counter.name] = chain_count.get(counter.name, 0) + 1
            ins.then_inc(counter, 1)
            eng.wait_ge(counter, chain_count[counter.name])

        ld_x = sem("ld_x")
        ld_tok = sem("ld_tok")
        ld_ssm = sem("ld_ssm")
        ld_ffn = sem("ld_ffn")
        ld_experts = sem("ld_experts")
        zeros_ready = sem("zeros_ready")
        slots_zeroed = sem("slots_zeroed")
        pool_step = sem("pool_step")
        dve_step = sem("dve_step")
        pool_turns = sem("pool_turns")
        bands_ready = sem("bands_ready")
        squares_ready = sem("squares_ready")
        row_squares_ready = sem("row_squares_ready")
        windows_ready = sem("windows_ready")
        wsq_ready = sem("wsq_ready")
        wnorm_ready = sem("wnorm_ready")
        a_ready = sem("a_ready")
        biases_split = sem("biases_split")
        bias3_ready = sem("bias3_ready")

        def rows(v, parts):
            return v.rearrange("(a n) -> a n", a=1).partition_broadcast(parts) if len(v.shape) == 1 else v

        with nc.Block() as block:
            @block.sync
            def _(sp):
                sp.dma_start(x_all, x2[:, 0:CIN].rearrange("(n p) c -> p n c", p=128)).then_inc(ld_x, 16)
                kw = tok_kernel.rearrange("k c f -> c k f")
                sp.dma_start(tokw[0:64, 0:5, :], kw[:, 0:TAPS:2, :]).then_inc(ld_tok, 16)
                sp.dma_start(tokw[64:128, 0:4, :], kw[:, 1:TAPS:2, :]).then_inc(ld_tok, 16)
                sp.dma_start(tokb[:, :], rows(tok_bias, CH)).then_inc(ld_tok, 16)
                for dst, src in ((w_in, in_proj), (cw, rows(conv_w, 128)), (cb[:, :], conv_b),
                                 (dtb[:, :], rows(dt_bias, CH)), (a_log[:, :], rows(A_log, CH)),
                                 (d_col[0:64, :], rows(D_skip[0:4:2], 64)),
                                 (d_col[64:128, :], rows(D_skip[1:4:2], 64)), (nw[:, :], norm_w),
                                 (w_out, out_proj.rearrange("(c p) f -> p c f", p=128))):
                    with nc.allow_non_contiguous_dma(reason="small vectors"):
                        sp.dma_start(dst, src).then_inc(ld_ssm, 16)
                for dst, src in ((lng[:, :], ln_g), (lnb[:, :], ln_b), (rw[:, :], router_w),
                                 (rb[:, :], rows(router_b, CH)), (w_s1[:, :], sw1), (b_s1[:, :], sb1),
                                 (w_s2[:, :, :], sw2.rearrange("(c p) f -> p c f", p=128)),
                                 (w_e2b[0:E, :], eb2), (w_e2b[E:CB, :], rows(sb2, 1)), (fg[:, :], ffg),
                                 (fbb[:, :], ffb), (w_f1[:, :], fw1), (b_f1[:, :], fb1),
                                 (w_f2[:, :, :], fw2.rearrange("(c p) f -> p c f", p=128)),
                                 (b_f2[:, :], rows(fb2, CH)), (b_e1, eb1)):
                    with nc.allow_non_contiguous_dma(reason="small vectors"):
                        sp.dma_start(dst, src).then_inc(ld_ffn, 16)
                sp.wait_ge(zeros_ready, 1)
                zr = x_slots.rearrange("(n p) f -> p n f", p=128)
                for n in range(0, NBLK, 10):
                    sp.dma_start(zr[:, n:n + 10, :], zero_src.rearrange("p (n f) -> p n f", f=F))\
                      .then_inc(slots_zeroed, 16)
                sp.wait_ge(biases_split, 3)
                sp.dma_start(bias_parts.rearrange("k e h -> e k h"), b_part).then_inc(bias3_ready, 16)
                sp.wait_ge(bias3_ready, 16)
                sp.dma_start(bias3[:, :], bias_parts.rearrange("k e h -> k (e h)")).then_inc(bias3_ready, 16)
                sp.wait_ge(bias3_ready, 32)
                sp.wait_ge(slots_zeroed, 16 * (NBLK // 10))

            @block.gpsimd
            def _(pool):
                nc.gpsimd.memset(zero_src, 0.0).then_inc(zeros_ready, 1)
                nc.gpsimd.memset(minus_half[:, :], -0.5)
                nc.gpsimd.memset(plus_half[:, :], 0.5)
                nc.gpsimd.memset(euler[:, :], EXP1)
                nc.gpsimd.memset(eps_row[:, :], EPS)
                nc.gpsimd.memset(ones_col[:, :], 1.0)
                nc.gpsimd.memset(IDX[:, :, :], 1 << 20)
                nc.gpsimd.memset(COMB[:, :], 0.25)
                nc.gpsimd.memset(ones3[:, :], 1.0)
                nc.gpsimd.memset(ones_sq[:, :], 1.0)
                nc.gpsimd.memset(band, 1.0)
                nc.gpsimd.memset(ident[:, :], 0.0)
                nc.gpsimd.memset(diag2, 0.0)
                nc.gpsimd.memset(tri[:, :], 0.0)
                link(pool, pool_step, nc.gpsimd.iota(iota_i, pattern=[[-1, E]], base=E, channel_multiplier=0))
                nc.gpsimd.tensor_copy(rev_iota[:, :], iota_i)
                link(pool, pool_step, nc.gpsimd.iota(iota_b, pattern=[[1, NBLK]], base=0,
                                                     channel_multiplier=0))
                nc.gpsimd.tensor_copy(block_no[:, :], iota_b)
                for j in range(2):
                    for c in range(2):
                        v = band[:, 2 * j + c, :]
                        nc.gpsimd.affine_select(out=v, in_=v, compare_op=ALU.is_ge, fill=0.0,
                                                base=128 * j - CH * c, pattern=[[-1, CH]],
                                                channel_multiplier=1)
                link(pool, pool_step, nc.gpsimd.affine_select(
                    out=ident[:, :], in_=ident[:, :], compare_op=ALU.not_equal, fill=1.0, base=0,
                    pattern=[[-1, 128]], channel_multiplier=1))
                for j in range(2):
                    for c in range(2):
                        v = band[:, 2 * j + c, :]
                        last = nc.gpsimd.affine_select(out=v, in_=v, compare_op=ALU.is_ge, fill=0.0,
                                                       base=TAPS - 1 - 128 * j + CH * c,
                                                       pattern=[[1, CH]], channel_multiplier=-1)
                last.then_inc(bands_ready, 1)
                nc.gpsimd.affine_select(out=diag2[:, :, 0:CH], in_=diag2[:, :, 0:CH],
                                        compare_op=ALU.not_equal, fill=1.0, base=0,
                                        pattern=[[0, 2], [-1, CH]], channel_multiplier=1)
                nc.gpsimd.affine_select(out=tri[:, :], in_=tri[:, :], compare_op=ALU.is_ge, fill=1.0,
                                        base=0, pattern=[[-1, CH]], channel_multiplier=1)
                pool.wait_ge(ld_x, 16)
                nc.gpsimd.tensor_tensor(x_sq, x_all, x_all, ALU.mult).then_inc(squares_ready, 1)
                pool.wait_ge(ld_ssm, 16 * 9)
                link(pool, pool_step, nc.gpsimd.tensor_tensor(a_neg[:, 0, :], euler[0:CH, 0:NH], a_log[:, :],
                                                              ALU.pow))
                for j in range(3, -1, -1):
                    last = nc.gpsimd.tensor_scalar(a_neg[:, j, :], a_neg[:, 0, :], -1.0, 0.0,
                                                   ALU.mult, ALU.add)
                last.then_inc(a_ready, 1)
                pool.wait_ge(wsq_ready, 1)
                nc.gpsimd.tensor_tensor(wnorm, wsq, plus_half[0:CH, :], ALU.pow).then_inc(wnorm_ready, 1)

            @block.tensor
            def _(pe):
                pe.wait_ge(row_squares_ready, 1)
                pe.wait_ge(bands_ready, 1)
                pe.wait_ge(ld_tok, 48)
                sqv = sq.rearrange("p (b j) -> p j b", j=2)
                for c in range(2):
                    for j in range(2):
                        last = nc.tensor.matmul(psum[0:CH, 0, c * SEQS:(c + 1) * SEQS],
                                                band[:, 2 * j + c, :], sqv[:, j, :],
                                                start=(j == 0), stop=(j == 1))
                last.then_inc(windows_ready, 1)

            @block.vector
            def _(dve):
                nc.vector.memset(hnT[0], 0.0)
                nc.vector.memset(keep[:, :], 1.0)
                link(dve, dve_step, nc.vector.memset(wait_carrier[:, :], 0.0))
                nc.vector.memset(keep[0:1, :].rearrange("p (b c h) -> p b c h", b=2, c=2)[:, :, 0, :], 0.0)
                nc.vector.memset(hnT[1], 0.0)
                dve.wait_ge(squares_ready, 1)
                nc.vector.tensor_reduce(sq, x_sq, AX.X, ALU.add).then_inc(row_squares_ready, 1)
                dve.wait_ge(ld_ssm, 16 * 9)
                cwv = cw.rearrange("p (c k) -> p k c", k=KC)
                for k in range(KC):
                    nc.vector.tensor_tensor(w_tap[:, k, :], w_in[:, DI:DI + 384], cwv[:, k, :], ALU.mult)
                for c in range(2):
                    nc.vector.tensor_scalar(w_out[:, c, :], w_out[:, c, :], nw[:, c:c + 1], None, ALU.mult)
                dve.wait_ge(ld_ffn, 16 * 16)
                nc.vector.tensor_scalar(w_s2[:, :, :], w_s2[:, :, :], 0.25, None, ALU.mult)
                nc.vector.tensor_copy(b_part[:, 0, :], b_e1).then_inc(biases_split, 1)
                dve.wait_ge(biases_split, 1)
                link(dve, dve_step, nc.vector.tensor_tensor(b_e1f, b_e1, b_part[:, 0, :],
                                                            ALU.subtract))
                nc.vector.tensor_copy(b_part[:, 1, :], b_e1f).then_inc(biases_split, 1)
                dve.wait_ge(biases_split, 2)
                link(dve, dve_step, nc.vector.tensor_tensor(b_e1, b_e1f, b_part[:, 1, :],
                                                            ALU.subtract))
                nc.vector.tensor_copy(b_part[:, 2, :], b_e1).then_inc(biases_split, 1)
                dve.wait_ge(windows_ready, 1)
                nc.vector.tensor_scalar(wsq.rearrange("p (b c) -> p c b", c=2),
                                        psum[0:CH, 0, 0:NCH].rearrange("p (c b) -> p c b", c=2),
                                        0.0, None, ALU.max).then_inc(wsq_ready, 1)
                dve.wait_ge(wnorm_ready, 1)
                nc.vector.tensor_scalar(wmix, wnorm, 1.0, None, ALU.is_lt)
                link(dve, dve_step, nc.vector.tensor_scalar(small, wnorm, TOK_EPS, None, ALU.add))
                link(dve, dve_step, nc.vector.reciprocal(wsq, small))
                link(dve, dve_step, nc.vector.tensor_scalar(small, wmix, -1.0, 1.0, ALU.mult, ALU.add))
                link(dve, dve_step, nc.vector.tensor_tensor(wsq, wsq, small, ALU.mult))
                link(dve, dve_step, nc.vector.tensor_tensor(wsq, wsq, wmix, ALU.add))
                link(dve, dve_step, nc.vector.tensor_scalar(scale[:, :], wsq, LAM, None, ALU.mult))

        names = ("x_in0 x_in1 xT_psum xT_ready conv_done conv_scaled tanh_done biased h_ready "
                 "stats_ready rstd_ready hn_ready hnT_psum hnT_ready pd_ready dtu_ready ip_ready ip_used "
                 "nab_ready exp_ready dt_ready dec_ready px_ready xd_ready g_ready pb_ready scan_done "
                 "m_ready y_psum t_ready yg_ready sq_ready po_ready pr_ready ms_ready rr_ready po_used "
                 "dve_link pool_link")
        s = {n: sem("a_" + n) for n in names.split()}
        S = namedtuple("S", s)(**s)
        x_in = (S.x_in0, S.x_in1)

        def stepper(eng, counter):
            at = [0]

            def begin(done):
                at[0] = done

            def step(ins):
                at[0] = at[0] + 1
                ins.then_inc(counter, 1)
                eng.wait_ge(counter, at[0])
            return begin, step

        bank_of = (2, 3, 2, 2, 3)

        with nc.Block() as block:
            x2t = x2.rearrange("(n p) c -> p n c", p=128)

            @block.sync
            def _(sp):
                def load(u):
                    later(sp, S.xT_psum, u.u - 1)
                    sp.dma_start(xin[u.q], x2t[:, ds(4 * u.u, 4), :]).then_inc(x_in[u.q], 16)
                streamed(sp, load, UNITS)

            @block.tensor
            def _(pe):
                def x_transposes(a):
                    pe.wait_ge(x_in[a.q], 16 * (a.n + 1))
                    later(pe, S.hnT_ready, a.u)
                    for j in range(4):
                        last = nc.tensor.transpose(psum[:, 0, j * 128:(j + 1) * 128], xin[a.q][:, j, :],
                                                   ident[:, :])
                    last.then_inc(S.xT_psum, 1)

                def conv(a):
                    pe.wait_ge(S.xT_ready, a.u + 1)
                    later(pe, S.conv_scaled, a.u)
                    for j in range(4):
                        t0 = LIN * (j // 2) + CH * (j % 2)
                        for k in range(5):
                            p = 128 if k < 4 else 64
                            last = nc.tensor.matmul(psum[0:CH, 1, j * F:(j + 1) * F],
                                                    xT[0:p, t0 + 2 * k:t0 + 2 * k + CH], tokw[0:p, k, :],
                                                    start=(k == 0), stop=(k == 4))
                    last.then_inc(S.conv_done, 1)

                def hn_transposes(a):
                    pe.wait_ge(S.hn_ready, a.u + 1)
                    for j in range(4):
                        last = nc.tensor.transpose(psum[:, 0, j * CH:(j + 1) * CH], hn[:, j, :],
                                                   ident[0:CH, 0:CH])
                    last.then_inc(S.hnT_psum, 1)

                def dt_projection(b):
                    pe.wait_ge(S.ip_used, 5 * b.u + 2)
                    for j in range(4):
                        t0 = PADL + CH * (j % 2)
                        last = nc.tensor.matmul(psum[0:CH, 3, 4 * j:4 * j + 4],
                                                hnT[b.q][:, j // 2, t0:t0 + CH], w_in[:, 640:644],
                                                start=True, stop=True)
                    last.then_inc(S.pd_ready, 1)

                def projection(b, k):
                    if k == 0:
                        pe.wait_ge(S.hnT_ready, b.u + 1)
                    if k == 4:
                        pe.wait_ge(S.dtu_ready, b.u + 1)
                    else:
                        later(pe, S.ip_used, 5 * b.u + (0, 0, 1, 3)[k])
                    o = psum[:, bank_of[k], 0:UT]
                    if k < 2:
                        last = nc.tensor.matmul(o, w_in[:, k * 128:(k + 1) * 128],
                                                hnT[b.q][:, :, PADL:], start=True, stop=True)
                    else:
                        for w in range(KC):
                            last = nc.tensor.matmul(o, w_tap[:, w, (k - 2) * 128:(k - 1) * 128],
                                                    hnT[b.q][:, :, w:w + L], start=(w == 0),
                                                    stop=(w == KC - 1))
                    last.then_inc(S.ip_ready, 1)

                def x_rows(c):
                    pe.wait_ge(S.ip_used, 5 * c.u + 4)
                    later(pe, S.scan_done, 2 * c.u)
                    for j in range(4):
                        for k in range(2):
                            col = j * DI + k * 128
                            last = nc.tensor.transpose(psum[0:CH, 5 + col // 512,
                                                            col % 512:col % 512 + 128],
                                                       XT[c.q][:, k, j * CH:(j + 1) * CH], ident[:, :])
                    last.then_inc(S.px_ready, 1)

                def scores(c, b):
                    w = 2 * c.u + b
                    if b == 0:
                        later(pe, S.ms_ready, c.u)
                    else:
                        pe.wait_ge(S.m_ready, w)
                    pe.wait_ge(S.ip_used, 5 * c.u + 5)
                    t0 = b * L
                    nc.tensor.matmul(psum[0:CH, 4, 0:L], BT[c.q][:, t0:t0 + CH], CT[c.q][:, t0:t0 + L],
                                     start=True, stop=True)
                    nc.tensor.matmul(psum[0:CH, 4, L:L + CH], BT[c.q][:, t0 + CH:t0 + L],
                                     CT[c.q][:, t0 + CH:t0 + L], start=True, stop=True)\
                        .then_inc(S.g_ready, 1)

                def decays(c, b):
                    w = 2 * c.u + b
                    if b == 0:
                        pe.wait_ge(S.xd_ready, c.u + 1)
                        pe.wait_ge(S.dec_ready, c.u + 1)
                    else:
                        pe.wait_ge(S.scan_done, w)
                    for h in range(NH):
                        for k in range(2):
                            col = (h % 2) * L + k * CH
                            last = nc.tensor.transpose(psum[0:CH, 5 + h // 2, col:col + CH],
                                                       dec[c.q][:, 2 * b + k, h:h + 1].to_broadcast([CH, CH]),
                                                       ident[0:CH, 0:CH])
                    last.then_inc(S.pb_ready, 1)

                def mix(c, b):
                    w = 2 * c.u + b
                    pe.wait_ge(S.m_ready, w + 1)
                    if b == 0:
                        later(pe, S.po_used, c.u)
                    else:
                        pe.wait_ge(S.t_ready, w)
                    for h in range(NH):
                        p, k = (h % 2) * 64, h // 2
                        o = psum[p:p + 64, 7, k * L:(k + 1) * L]
                        nc.tensor.matmul(o, Xd[:, 2 * b, h * HD:(h + 1) * HD], M0[:, h, :],
                                         start=True, stop=False)
                        last = nc.tensor.matmul(o[:, CH:L], Xd[:, 2 * b + 1, h * HD:(h + 1) * HD],
                                                M1[:, h, :], start=False, stop=True)
                    last.then_inc(S.y_psum, 1)

                def output(c):
                    pe.wait_ge(S.yg_ready, 2 * c.u + 2)
                    for j in range(4):
                        for k in range(2):
                            last = nc.tensor.matmul(psum[0:CH, 7, j * F:(j + 1) * F],
                                                    Yg[:, k, j * CH:(j + 1) * CH], w_out[:, k, :],
                                                    start=(k == 0), stop=(k == 1))
                    last.then_inc(S.po_ready, 1)
                    pe.wait_ge(S.sq_ready, 2 * c.u + 2)
                    pe.wait_ge(S.m_ready, 2 * c.u + 2)
                    for j in range(4):
                        for k in range(2):
                            last = nc.tensor.matmul(psum[0:CH, 4, 480 + j:481 + j],
                                                    Sq[:, k, j * CH:(j + 1) * CH], ones_col[:, :],
                                                    start=(k == 0), stop=(k == 1))
                    last.then_inc(S.pr_ready, 1)

                def body(a, b, c):
                    if c: scores(c, 0)
                    if b: projection(b, 0)
                    if c: decays(c, 0)
                    if b: projection(b, 1)
                    if a: x_transposes(a)
                    if b: projection(b, 2); dt_projection(b)
                    if c: mix(c, 0)
                    if c: scores(c, 1); decays(c, 1)
                    if a: conv(a)
                    if b: projection(b, 3)
                    if c: mix(c, 1)
                    if b: x_rows(b); projection(b, 4)
                    if c: output(c)
                    if a: hn_transposes(a)
                skewed(pe, body, UNITS)

            @block.scalar
            def _(act):
                def x_copy(a):
                    act.wait_ge(S.xT_psum, a.u + 1)
                    later(act, S.conv_done, a.u)
                    nc.scalar.activation(xT, psum[:, 0, :], ACT.Copy).then_inc(S.xT_ready, 1)

                def tanh(a):
                    act.wait_ge(S.conv_scaled, a.u + 1)
                    later(act, S.biased, a.u)
                    nc.scalar.activation(v_t, v_s, ACT.Tanh).then_inc(S.tanh_done, 1)

                def relu(a):
                    act.wait_ge(S.biased, a.u + 1)
                    nc.scalar.activation(Hb[:, ds(4 * F * a.u, 4 * F)], v_b, ACT.Relu).then_inc(S.h_ready, 1)

                def hnT_copy(a):
                    act.wait_ge(S.hnT_psum, a.u + 1)
                    later(act, S.ip_ready, 5 * (a.u - 1))
                    nc.scalar.activation(hnT[a.q][:, :, PADL:],
                                         psum[:, 0, 0:UT].rearrange("p (b t) -> p b t", b=2),
                                         ACT.Copy).then_inc(S.hnT_ready, 1)

                def silu(b, k):
                    act.wait_ge(S.ip_ready, 5 * b.u + k + 1)
                    if k == 0:
                        later(act, S.yg_ready, 2 * (b.u - 1))
                    i = psum[:, bank_of[k], 0:UT]
                    if k < 2:
                        nc.scalar.activation(Z[b.q][:, k, :], i, ACT.Silu).then_inc(S.ip_used, 1)
                    elif k < 4:
                        nc.scalar.activation(XT[b.q][:, k - 2, :], i, ACT.Silu, bias=cb[:, k - 2:k - 1])\
                            .then_inc(S.ip_used, 1)
                    else:
                        nc.scalar.activation(BT[b.q], i[0:64, :], ACT.Silu, bias=cb[0:64, 2:3])
                        nc.scalar.activation(CT[b.q], i[64:128, :], ACT.Silu, bias=cb[64:128, 2:3])\
                            .then_inc(S.ip_used, 1)

                def square(c, b):
                    act.wait_ge(S.yg_ready, 2 * c.u + b + 1)
                    if b == 0:
                        later(act, S.pr_ready, c.u)
                    nc.scalar.activation(Sq[:, :, b * L:(b + 1) * L], Yg[:, :, b * L:(b + 1) * L],
                                         ACT.Square).then_inc(S.sq_ready, 1)

                def body(a, b, c):
                    if b: silu(b, 0); silu(b, 1)
                    if a: x_copy(a)
                    if b: silu(b, 2)
                    if c: square(c, 0)
                    if a: tanh(a); relu(a)
                    if b: silu(b, 3)
                    if c: square(c, 1)
                    if b: silu(b, 4)
                    if a: hnT_copy(a)
                skewed(act, body, UNITS)

            @block.gpsimd
            def _(pool):
                own_begin, own = stepper(pool, S.pool_link)

                def add_bias(a):
                    pool.wait_ge(S.tanh_done, a.u + 1)
                    later(pool, S.h_ready, a.u)
                    nc.gpsimd.tensor_tensor(v_b.rearrange("p (j f) -> p j f", f=F),
                                            v_t.rearrange("p (j f) -> p j f", f=F),
                                            tokb[:, :].unsqueeze(1).broadcast_to([CH, 4, F]),
                                            ALU.add).then_inc(S.biased, 1)

                def exp_of(b):
                    pool.wait_ge(S.nab_ready, b.u + 1)
                    nc.gpsimd.tensor_tensor(ee, euler[0:CH, :], nab, ALU.pow).then_inc(S.exp_ready, 1)

                def decay_of(b, done):
                    own_begin(done)
                    pool.wait_ge(S.dt_ready, b.u + 1)
                    later(pool, S.pb_ready, 2 * (b.u - 1))
                    own(nc.gpsimd.tensor_tensor(dA, dt[b.q], a_neg[:, :, :].rearrange("p j h -> p (j h)"),
                                                ALU.mult))
                    own(nc.gpsimd.tensor_tensor(ee2, euler[0:CH, :], dA,
                                                ALU.pow))
                    nc.gpsimd.tensor_tensor(dec[b.q].rearrange("p j h -> p (j h)"), ee2, keep[:, :],
                                            ALU.mult).then_inc(S.dec_ready, 1)

                def gate(c, b):
                    pool.wait_ge(S.t_ready, 2 * c.u + b + 1)
                    if b == 0:
                        later(pool, S.po_ready, c.u)
                        later(pool, S.sq_ready, 2 * c.u)
                    nc.gpsimd.tensor_tensor(Yg[:, :, b * L:(b + 1) * L], Tg[:, :, b * L:(b + 1) * L],
                                            Z[c.q][:, :, b * L:(b + 1) * L], ALU.mult)\
                        .then_inc(S.yg_ready, 1)

                def rr_of(c):
                    pool.wait_ge(S.ms_ready, c.u + 1)
                    nc.gpsimd.tensor_tensor(rr, ms, minus_half[0:CH, 0:4], ALU.pow).then_inc(S.rr_ready, 1)

                def body(a, b, c):
                    if c: gate(c, 0)
                    if b: exp_of(b)
                    if a: add_bias(a)
                    if c: gate(c, 1)
                    if a:
                        own_begin(a.u + 2 * (b.u if b else 0))
                        pool.wait_ge(S.stats_ready, a.u + 1)
                        own(nc.gpsimd.tensor_tensor(ve, mv[:, :, 1], eps_row[0:CH, 0:4], ALU.add))
                        nc.gpsimd.tensor_tensor(rstd, ve, minus_half[0:CH, 0:4], ALU.pow)\
                            .then_inc(S.rstd_ready, 1)
                    if b: decay_of(b, (a.u + 1 if a else UNITS) + 2 * b.u)
                    if c: rr_of(c)
                skewed(pool, body, UNITS)

            @block.vector
            def _(dve):
                own_begin, own = stepper(dve, S.dve_link)

                def conv_scale(a):
                    dve.wait_ge(S.conv_done, a.u + 1)
                    later(dve, S.tanh_done, a.u)
                    nc.vector.tensor_tensor(v_s.rearrange("p (j f) -> p j f", f=F),
                                            psum[0:CH, 1, :].rearrange("p (j f) -> p j f", f=F),
                                            scale[:, ds(4 * a.u, 4)].unsqueeze(2).broadcast_to([CH, 4, F]),
                                            ALU.mult).then_inc(S.conv_scaled, 1)

                def stats(a):
                    dve.wait_ge(S.h_ready, a.u + 1)
                    later(dve, S.rstd_ready, a.u)
                    for j in range(4):
                        last = nc.vector.bn_stats(st[:, j, :], Hb[:, ds(4 * F * a.u + j * F, F)])
                    own(last)
                    nc.vector.memset(wait_carrier[:, :], 0.0)
                    for j in range(4):
                        last = nc.vector.bn_aggr(mv[:, j, :], st[:, j, :])
                    last.then_inc(S.stats_ready, 1)

                def norm(a):
                    dve.wait_ge(S.rstd_ready, a.u + 1)
                    later(dve, S.hnT_psum, a.u)
                    for j in range(4):
                        last = nc.vector.tensor_scalar(hn[:, j, :], Hb[:, ds(4 * F * a.u + j * F, F)],
                                                       mv[:, j, 0:1], rstd[:, j:j + 1], ALU.subtract,
                                                       ALU.mult)
                    last.then_inc(S.hn_ready, 1)

                def dt_first(b):
                    dve.wait_ge(S.pd_ready, b.u + 1)
                    ins = nc.vector.tensor_tensor(uu.rearrange("p (j h) -> p j h", h=NH),
                                                  psum[0:CH, 3, 0:16].rearrange("p (j h) -> p j h", h=NH),
                                                  dtb[:, :].unsqueeze(1).broadcast_to([CH, 4, NH]), ALU.add)
                    ins.then_inc(S.dtu_ready, 1)
                    dve.wait_ge(S.dtu_ready, b.u + 1)
                    later(dve, S.exp_ready, b.u)
                    nc.vector.scalar_tensor_tensor(nab, uu, -1.0, uu, ALU.mult, ALU.min)\
                        .then_inc(S.nab_ready, 1)

                def dt_rest(b):
                    dve.wait_ge(S.exp_ready, b.u + 1)
                    own(nc.vector.tensor_scalar(qq, ee, 2.0, None, ALU.add))
                    own(nc.vector.reciprocal(rq, qq))
                    own(nc.vector.tensor_tensor(ss, ee, rq, ALU.mult))
                    own(nc.vector.tensor_tensor(s2, ss, ss, ALU.mult))
                    own(nc.vector.tensor_scalar(pa, s2, 1.0 / 15, None, ALU.mult))
                    src, dst = pa, pb
                    for k in (13, 11, 9, 7, 5, 3):
                        own(nc.vector.scalar_tensor_tensor(dst, src, 1.0 / k, s2, ALU.add, ALU.mult))
                        src, dst = dst, src
                    own(nc.vector.scalar_tensor_tensor(tt, src, 1.0, ss, ALU.add, ALU.mult))
                    own(nc.vector.tensor_scalar(qq, uu, 0.0, None, ALU.max))
                    nc.vector.scalar_tensor_tensor(dt[b.q], tt, 2.0, qq, ALU.mult, ALU.add)\
                        .then_inc(S.dt_ready, 1)

                def x_scale(c):
                    dve.wait_ge(S.px_ready, c.u + 1)
                    dve.wait_ge(S.dt_ready, c.u + 1)
                    later(dve, S.y_psum, 2 * c.u)
                    nc.vector.tensor_tensor(Xd.rearrange("p j (h d) -> p (j h) d", d=HD),
                                            psum[0:CH, 5:7, :].rearrange("p k (g d) -> p (k g) d", d=HD),
                                            dt[c.q].unsqueeze(2).broadcast_to([CH, 4 * NH, HD]),
                                            ALU.mult).then_inc(S.xd_ready, 1)

                def scans(c, b):
                    w = 2 * c.u + b
                    dve.wait_ge(S.pb_ready, w + 1)
                    for g in range(2):
                        nc.vector.tensor_tensor_scan(
                            L0.rearrange("p h t -> p (h t)")[:, g * 2 * L:(g + 1) * 2 * L],
                            psum[0:CH, 5 + g, 0:2 * L], diag2.rearrange("p h t -> p (h t)"),
                            0.0, ALU.mult, ALU.add)
                    for h in range(NH):
                        col = (h % 2) * L + CH
                        last = nc.vector.tensor_tensor_scan(L1[:, h, :], psum[0:CH, 5 + h // 2, col:col + CH],
                                                            ident[0:CH, 0:CH], 0.0, ALU.mult, ALU.add)
                    last.then_inc(S.scan_done, 1)

                def decayed_scores(c, b):
                    w = 2 * c.u + b
                    dve.wait_ge(S.scan_done, w + 1)
                    dve.wait_ge(S.g_ready, w + 1)
                    later(dve, S.y_psum, w)
                    nc.vector.tensor_tensor(M0, L0, psum[0:CH, 4, 0:L].unsqueeze(1).broadcast_to([CH, NH, L]),
                                            ALU.mult)
                    nc.vector.tensor_tensor(M1, L1, psum[0:CH, 4, L:L + CH].unsqueeze(1)
                                            .broadcast_to([CH, NH, CH]), ALU.mult).then_inc(S.m_ready, 1)

                def skip_add(c, b):
                    w = 2 * c.u + b
                    dve.wait_ge(S.y_psum, w + 1)
                    if b == 0:
                        later(dve, S.yg_ready, 2 * c.u)
                    for k in range(2):
                        last = nc.vector.scalar_tensor_tensor(
                            Tg[:, k, b * L:(b + 1) * L], XT[c.q][:, k, b * L:(b + 1) * L], d_col[:, k:k + 1],
                            psum[:, 7, k * L:(k + 1) * L], ALU.mult, ALU.add)
                    last.then_inc(S.t_ready, 1)

                def residual(c):
                    dve.wait_ge(S.pr_ready, c.u + 1)
                    nc.vector.tensor_scalar(ms, psum[0:CH, 4, 480:484], 1.0 / DI, EPS, ALU.mult, ALU.add)\
                        .then_inc(S.ms_ready, 1)
                    dve.wait_ge(S.rr_ready, c.u + 1)
                    dve.wait_ge(S.po_ready, c.u + 1)
                    for j in range(4):
                        row = Hb[:, ds(4 * F * c.u + j * F, F)]
                        last = nc.vector.scalar_tensor_tensor(row, psum[0:CH, 7, j * F:(j + 1) * F],
                                                              rr[:, j:j + 1], row, ALU.mult, ALU.add)
                    last.then_inc(S.po_used, 1)

                def new_stats(c):
                    dve.wait_ge(S.po_used, c.u + 1)
                    nc.vector.memset(wait_carrier[:, :], 0.0)
                    for j in range(4):
                        last = nc.vector.bn_stats(st3[:, j, :], Hb[:, ds(4 * F * c.u + j * F, F)])
                    own(last)
                    nc.vector.memset(wait_carrier[:, :], 0.0)
                    for j in range(4):
                        last = nc.vector.bn_aggr(mv3[:, j, :], st3[:, j, :])
                    own(last)
                    nc.vector.tensor_copy(MV[:, ds(4 * c.u, 4), :], mv3[:, :, :])

                def body(a, b, c):
                    if c: scans(c, 0); decayed_scores(c, 0)
                    if b: dt_first(b)
                    if c: skip_add(c, 0)
                    if c: scans(c, 1); decayed_scores(c, 1)
                    if a: conv_scale(a)
                    if b:
                        own_begin((a.u if a else UNITS) + 13 * b.u + 2 * (c.u if c else 0))
                        dt_rest(b)
                    if c: skip_add(c, 1)
                    if a:
                        own_begin(a.u + 13 * (b.u + 1 if b else 0) + 2 * (c.u if c else 0))
                        stats(a)
                    if b: x_scale(b)
                    if a: norm(a)
                    if c:
                        residual(c)
                        own_begin((a.u + 1 if a else UNITS) + 13 * (b.u + 1 if b else UNITS) + 2 * c.u)
                        new_stats(c)
                skewed(dve, body, UNITS)

        names = ("var_ready r1_ready t_ready r2_ready xnr_ready xnr_used xT_psum hhT_ready hhT_copied "
                 "lg_psum lg_ready dve_own based")
        B = namedtuple("B", names)(*[sem("b_" + n) for n in names.split()])
        with nc.Block() as block:
            @block.gpsimd
            def _(pool):
                pool.wait_ge(B.var_ready, 1)
                nc.gpsimd.tensor_tensor(v64[1], v64[0], minus_half[0:CH, :], ALU.pow).then_inc(B.r1_ready, 1)
                pool.wait_ge(B.t_ready, 1)
                nc.gpsimd.tensor_tensor(v64[3], v64[2], minus_half[0:CH, :], ALU.pow).then_inc(B.r2_ready, 1)

            @block.vector
            def _(dve):
                mean, var = MV[:, :, 0], MV[:, :, 1]
                nc.vector.tensor_scalar(v64[0], var, EPS, None, ALU.add).then_inc(B.var_ready, 1)
                dve.wait_ge(B.r1_ready, 1)
                link(dve, dve_step, nc.vector.tensor_tensor(v64[2], var, v64[1], ALU.mult))
                link(dve, dve_step, nc.vector.tensor_tensor(v64[2], v64[2], v64[1], ALU.mult))
                nc.vector.tensor_scalar(v64[2], v64[2], EPS, None, ALU.add).then_inc(B.t_ready, 1)
                nc.vector.tensor_scalar(r1p, v64[1], 1.0, None, ALU.add)
                nc.vector.scalar_tensor_tensor(nmr, mean, -1.0, v64[1], ALU.mult, ALU.mult)
                dve.wait_ge(B.r2_ready, 1)
                link(dve, dve_step, nc.vector.tensor_tensor(r12, v64[1], v64[3], ALU.mult))

                def normed(a):
                    later(dve, B.xnr_used, a.u - 1)
                    later(dve, B.xT_psum, a.u - 1)
                    for j in range(4):
                        last = nc.vector.tensor_scalar(xnr[a.q][:, j, :], Hb[:, ds(4 * F * a.u + j * F, F)],
                                                       MV[:, ds(4 * a.u + j, 1), 0], r12[:, ds(4 * a.u + j, 1)],
                                                       ALU.subtract, ALU.mult)
                    last.then_inc(B.xnr_ready, 1)

                def affine(b):
                    dve.wait_ge(B.xT_psum, b.u + 1)
                    later(dve, B.hhT_copied, b.u - 1)
                    later(dve, B.lg_psum, b.u - 1)
                    nc.vector.tensor_scalar(hhT[b.q], psum[:, b.q, 0:UT], lng[:, 0:1], lnb[:, 0:1], ALU.mult,
                                            ALU.add).then_inc(B.hhT_ready, 1)

                def logits(c):
                    dve.wait_ge(B.lg_psum, c.u + 1)
                    nc.vector.tensor_tensor(LG[:, ds(4 * E * c.u, 4 * E)].rearrange("p (j e) -> p j e", e=E),
                                            psum[0:CH, 2 + c.q, 0:4 * E].rearrange("p (j e) -> p j e", e=E),
                                            rb[:, :].unsqueeze(1).broadcast_to([CH, 4, E]),
                                            ALU.add).then_inc(B.lg_ready, 1)

                def body(a, b, c):
                    if a: normed(a)
                    if b: affine(b)
                    if c: logits(c)
                skewed(dve, body, UNITS)

            @block.scalar
            def _(act):
                def body(a, b, c):
                    if a:
                        act.wait_ge(B.xnr_ready, a.u + 1)
                        nc.scalar.activation(XNR[:, ds(4 * F * a.u, 4 * F)],
                                             xnr[a.q].rearrange("p j f -> p (j f)"), ACT.Copy)\
                            .then_inc(B.xnr_used, 1)
                        for j in range(4):
                            h = Hb[:, ds(4 * F * a.u + j * F, F)]
                            nc.scalar.activation(h, h, ACT.Identity, scale=r1p[:, ds(4 * a.u + j, 1)],
                                                 bias=nmr[:, ds(4 * a.u + j, 1)])
                    if b:
                        act.wait_ge(B.hhT_ready, b.u + 1)
                        nc.scalar.activation(HHT[:, ds(512 * b.u, UT)], hhT[b.q], ACT.Copy)\
                            .then_inc(B.hhT_copied, 1)
                skewed(act, body, UNITS)

            @block.tensor
            def _(pe):
                def body(a, b, c):
                    if b:
                        pe.wait_ge(B.xnr_ready, b.u + 1)
                        later(pe, B.hhT_ready, b.u - 1)
                        for j in range(4):
                            last = nc.tensor.transpose(psum[:, b.q, j * CH:(j + 1) * CH], xnr[b.q][:, j, :],
                                                       ident[0:CH, 0:CH])
                        last.then_inc(B.xT_psum, 1)
                    if c:
                        pe.wait_ge(B.hhT_ready, c.u + 1)
                        later(pe, B.lg_ready, c.u - 1)
                        for j in range(4):
                            last = nc.tensor.matmul(psum[0:CH, 2 + c.q, j * E:(j + 1) * E],
                                                    hhT[c.q][:, j * CH:(j + 1) * CH], rw[:, :],
                                                    start=True, stop=True)
                        last.then_inc(B.lg_psum, 1)
                skewed(pe, body, UNITS)

        names = ("diff_ready exp_ready mask_ready ranks_ready pool_own lg2_ready")
        R = namedtuple("R", names)(*[sem("r_" + n) for n in names.split()])
        with nc.Block() as block:
            ge = lambda v: v.rearrange("p (g e) -> p g e", e=E)
            Dg, Ex, Key, Oh1, Lg2, Oh2, Wk, TE, CUM = [ge(v[0:CH, :]) for v in big]
            TEe = big[7].rearrange("p (e g) -> p e g", g=NCH)
            CUMe = big[8].rearrange("p (e g) -> p e g", g=NCH)
            LGg = ge(LG)
            over_e = lambda v: v.unsqueeze(2).broadcast_to([CH, NCH, E])
            each_g = lambda v: v.unsqueeze(1).broadcast_to([CH, NCH, E])
            m1, k1, m2, rs, e1, e2 = row

            @block.scalar
            def _(act):
                act.wait_ge(R.diff_ready, 1)
                nc.scalar.activation(Ex, Dg, ACT.Exp, scale=1.0 / TEMP).then_inc(R.exp_ready, 1)

            @block.tensor
            def _(pe):
                pe.wait_ge(R.mask_ready, 1)
                for k in range(2):
                    nc.tensor.matmul(psum[0:CH, k, :], tri[:, :], mask[:, k * 512:(k + 1) * 512],
                                     start=True, stop=True)
                    last = nc.tensor.matmul(psum[:, 2 + k, :], ones_sq[:, :], mask[:, k * 512:(k + 1) * 512],
                                            start=True, stop=True)
                last.then_inc(R.ranks_ready, 1)

            @block.vector
            def _(dve):
                def step(ins):
                    link(dve, dve_step, ins)

                V = nc.vector
                step(V.tensor_reduce(m1, LGg, AX.X, ALU.max))
                V.tensor_tensor(Dg, LGg, over_e(m1), ALU.subtract).then_inc(R.diff_ready, 1)
                step(V.tensor_tensor(Key, LGg, over_e(m1), ALU.is_equal))
                step(V.tensor_tensor(Key, Key, each_g(rev_iota[0:CH, :]), ALU.mult))
                step(V.tensor_reduce(k1, Key, AX.X, ALU.max))
                step(V.tensor_tensor(Oh1, each_g(rev_iota[0:CH, :]), over_e(k1), ALU.is_equal))
                step(V.scalar_tensor_tensor(Lg2, Oh1, -3.0e38, LGg, ALU.mult, ALU.add))
                step(V.tensor_reduce(m2, Lg2, AX.X, ALU.max))
                step(V.tensor_tensor(Key, Lg2, over_e(m2), ALU.is_equal))
                step(V.tensor_tensor(Key, Key, each_g(rev_iota[0:CH, :]), ALU.mult))
                step(V.tensor_reduce(k1, Key, AX.X, ALU.max))
                step(V.tensor_tensor(Oh2, each_g(rev_iota[0:CH, :]), over_e(k1), ALU.is_equal))
                V.tensor_tensor(ge(mask), Oh1, Oh2, ALU.add).then_inc(R.mask_ready, 1)
                dve.wait_ge(R.exp_ready, 1)
                step(V.tensor_reduce(rs, Ex, AX.X, ALU.add))
                step(V.reciprocal(rs, rs))
                step(V.tensor_tensor(Wk, Oh1, Ex, ALU.mult))
                step(V.tensor_reduce(e1, Wk, AX.X, ALU.add))
                step(V.tensor_tensor(VAL[:, 0, :], e1, rs, ALU.mult))
                step(V.tensor_tensor(Wk, Oh2, Ex, ALU.mult))
                step(V.tensor_reduce(e2, Wk, AX.X, ALU.add))
                step(V.tensor_tensor(VAL[:, 1, :], e2, rs, ALU.mult))
                step(V.tensor_tensor(Wk, Oh1, over_e(VAL[:, 0, :]), ALU.mult))
                step(V.tensor_tensor(Key, Oh2, over_e(VAL[:, 1, :]), ALU.mult))
                V.tensor_tensor(COMB[:, :].rearrange("p (g e) -> p g e", e=CB)[:, :, 0:E], Wk, Key, ALU.add)
                dve.wait_ge(R.ranks_ready, 1)
                step(V.tensor_copy(TEe, psum[:, 2:4, :].rearrange("p k (g e) -> p e (k g)", e=E)))
                step(V.tensor_tensor_scan(big[8], big[7], big[7], 0.0, ALU.add, ALU.max))
                prev, cnt, blocks, t0, t1, base = sml[0:6]
                ends = CUMe[:, :, NCH - 1]
                step(V.memset(prev, 0.0))
                step(V.tensor_copy(prev[:, 1:E], ends[:, 0:E - 1]))
                step(V.tensor_tensor(cnt, ends, prev, ALU.subtract))
                step(V.tensor_scalar(t0, cnt, (BLK - 1) / 2.0, 1.0 / BLK, ALU.add, ALU.mult))
                step(V.tensor_scalar(t1, t0, 8388608.0, None, ALU.add))
                step(V.tensor_scalar(blocks, t1, -8388608.0, None, ALU.add))
                step(V.tensor_tensor_scan(cumP[:, :], blocks, blocks, 0.0, ALU.add, ALU.max))
                step(V.tensor_tensor(t0, cumP[:, :], blocks, ALU.subtract))
                step(V.scalar_tensor_tensor(base, t0, float(BLK), prev, ALU.mult, ALU.subtract))
                step(V.tensor_tensor(CUMe, CUMe, TEe, ALU.subtract))
                step(V.tensor_tensor(CUMe, CUMe, base.unsqueeze(2).broadcast_to([128, E, NCH]), ALU.add))
                step(V.tensor_tensor(Lg2, psum[0:CH, 0:2, :].rearrange("p k (g e) -> p (k g) e", e=E),
                                     CUMe[0:CH].rearrange("p e g -> p g e"), ALU.add))
                step(V.tensor_tensor(Wk, Oh1, Lg2, ALU.mult))
                step(V.tensor_reduce(m1, Wk, AX.X, ALU.add))
                V.tensor_copy(IDX[0:CH, :, 0], m1)
                step(V.tensor_tensor(Key, Oh2, Lg2, ALU.mult))
                step(V.tensor_reduce(m2, Key, AX.X, ALU.add))
                V.tensor_copy(IDX[0:CH, :, 1], m2)
                blkE = arena[0:1, staging_at:staging_at + NBLK * E].rearrange("p (j e) -> p j e", e=E)
                blkN = sml_blocks
                step(V.tensor_tensor(blkE, cumP[0:1, :].unsqueeze(1).broadcast_to([1, NBLK, E]),
                                     block_no[:, :].unsqueeze(2).broadcast_to([1, NBLK, E]), ALU.is_le))
                step(V.tensor_reduce(blkN, blkE, AX.X, ALU.add))
                step(V.tensor_scalar(blkN, blkN, float(E - 1), float(DH), ALU.min, ALU.mult))
                V.tensor_copy(EOFF[:, :], blkN)

        names = ("st_ready0 st_ready1 scat0 scat1 wload up_psum up_used comb_ready comb_psum combT_ready "
                 "down_psum moe_ready")
        C = namedtuple("C", names)(*[sem("c_" + n) for n in names.split()])
        scattered = (C.scat0, C.scat1)
        staged = (C.st_ready0, C.st_ready1)
        with nc.Block() as block:
            @block.sync
            def _(sp):
                sp.dma_start(w1.rearrange("p (e h) -> p e h", e=E),
                             ew1.rearrange("e d h -> d e h")).then_inc(C.wload, 16)
                sp.dma_start(w2.rearrange("p (g d) -> p g d", d=F),
                             ew2.rearrange("e (c p) d -> p (e c) d", p=128)).then_inc(C.wload, 16)
                sp.wait_ge(C.wload, 32)

            @block.gpsimd
            def _(pool):
                nc.gpsimd.memset(x_st[0], 0.0).then_inc(C.st_ready0, 1)
                nc.gpsimd.memset(x_st[1], 0.0).then_inc(C.st_ready1, 1)

                last_slot = pool.to_reg(SLOTS - 1)

                def scatter(u):
                    pool.wait_ge(staged[u.q], u.n + 2)
                    pool.sem_inc(pool_turns)
                    for j in range(4):
                        for k in range(2):
                            nc.gpsimd.indirect_dma_start(
                                out=x_slots, out_offset=bass.IndirectOffsetOnAxis(
                                    ap=idx_st[u.q][:, 2 * j + k:2 * j + k + 1], axis=0),
                                in_=x_st[u.q][:, j * F:(j + 1) * F], in_offset=None,
                                bounds_check=last_slot, oob_is_err=False).then_inc(scattered[u.q], 16)
                streamed(pool, scatter, UNITS)
                for q in range(2):
                    pool.wait_ge(scattered[q], 16 * 8 * (UNITS // 2))

            @block.scalar
            def _(act):
                def stage(u):
                    if not isinstance(u.n, int) or u.n > 0:
                        act.wait_ge(scattered[u.q], 128 * u.n)
                    if isinstance(u.n, int) and u.n == 0:
                        act.wait_ge(staged[u.q], 1)
                    nc.scalar.activation(idx_st[u.q][:, :], IDX[:, ds(4 * u.u, 4), :]
                                         .rearrange("p j k -> p (j k)"), ACT.Copy)
                    nc.scalar.activation(x_st[u.q][0:CH, :], XNR[:, ds(4 * F * u.u, 4 * F)], ACT.Copy)\
                        .then_inc(staged[u.q], 1)

                def body(a, b, c):
                    if a: stage(a)
                    if b:
                        act.wait_ge(C.up_psum, b.u + 1)
                        later(act, C.down_psum, b.u)
                        for k in range(2):
                            last = nc.scalar.activation(SH[:, k, :], psum[:, k, 0:UT], ACT.Silu,
                                                        bias=b_s1[:, k:k + 1])
                        last.then_inc(C.up_used, 1)
                skewed(act, body, UNITS)

            @block.tensor
            def _(pe):
                def body(a, b, c):
                    if b:
                        later(pe, C.up_used, b.u)
                        for k in range(2):
                            last = nc.tensor.matmul(psum[:, k, 0:UT], w_s1[:, k * 128:(k + 1) * 128],
                                                    HHT[:, ds(512 * b.u, UT)], start=True, stop=True)
                        last.then_inc(C.up_psum, 1)
                        pe.wait_ge(C.comb_ready, b.u + 1)
                        later(pe, C.combT_ready, b.u)
                        for j in range(4):
                            last = nc.tensor.transpose(psum[0:CB, 2, j * CH:(j + 1) * CH], comb_st[:, j, :],
                                                       ident[0:CH, 0:CH])
                        last.then_inc(C.comb_psum, 1)
                        pe.wait_ge(C.up_used, b.u + 1)
                        pe.wait_ge(C.combT_ready, b.u + 1)
                        later(pe, C.moe_ready, b.u)
                        for j in range(4):
                            o = psum[0:CH, 3, j * F:(j + 1) * F]
                            t = slice(j * CH, (j + 1) * CH)
                            for k in range(2):
                                nc.tensor.matmul(o, SH[:, k, t], w_s2[:, k, :], start=(k == 0), stop=False)
                            last = nc.tensor.matmul(o, combT[:, t], w_e2b[:, :], start=False, stop=True)
                        last.then_inc(C.down_psum, 1)
                skewed(pe, body, UNITS)

            @block.vector
            def _(dve):
                def body(a, b, c):
                    if b:
                        later(dve, C.comb_psum, b.u)
                        nc.vector.tensor_copy(comb_st.rearrange("p j e -> p (j e)"),
                                              COMB[:, ds(4 * CB * b.u, 4 * CB)]).then_inc(C.comb_ready, 1)
                        dve.wait_ge(C.comb_psum, b.u + 1)
                        later(dve, C.down_psum, b.u)
                        nc.vector.tensor_copy(combT, psum[0:CB, 2, 0:UT]).then_inc(C.combT_ready, 1)
                    if c:
                        dve.wait_ge(C.down_psum, c.u + 1)
                        nc.vector.tensor_copy(MOE[:, ds(512 * c.u, 512)], psum[0:CH, 3, :])\
                            .then_inc(C.moe_ready, 1)
                skewed(dve, body, UNITS)

        names = ("xb0 xb1 xb2 xb3 xT_psum hT_ready up_psum eh_ready ehT_psum ehT_ready down_psum yo_ready "
                 "yst0 yst1 yst2 yst3")
        X = namedtuple("X", names)(*[sem("x_" + n) for n in names.split()])
        x_here = (X.xb0, X.xb1, X.xb2, X.xb3)
        y_stored = (X.yst0, X.yst1, X.yst2, X.yst3)
        with nc.Block() as block:
            @block.sync
            def _(sp):
                def load(t):
                    later(sp, X.xT_psum, t.u - 3)
                    sp.dma_start(xb[t.q], x_slots[ds(BLK * t.u, BLK), :]).then_inc(x_here[t.q], 16)
                streamed(sp, load, NBLK, 4)

            @block.tensor
            def _(pe):
                def body(a, b, c):
                    if a:
                        pe.wait_ge(x_here[a.q], 16 * (a.n + 1))
                        later(pe, X.hT_ready, a.u - 1)
                        nc.tensor.transpose(psum[:, a.q % 2, 0:BLK], xb[a.q], ident[:, :])\
                            .then_inc(X.xT_psum, 1)
                    if c:
                        pe.wait_ge(X.eh_ready, c.u + 1)
                        later(pe, X.ehT_ready, c.u - 1)
                        for k in range(NF):
                            last = nc.tensor.transpose(psum[:, 4 + c.q % 2, k * 128:(k + 1) * 128],
                                                       EH[c.q % 2][:, k * 128:(k + 1) * 128], ident[:, :])
                        last.then_inc(X.ehT_psum, 1)
                    if b:
                        at = pe.value_load(EOFF[0:1, ds(b.u, 1)], min_val=0, max_val=(E - 1) * DH)
                        pe.wait_ge(X.hT_ready, b.u + 1)
                        later(pe, X.eh_ready, b.u - 1)
                        o = psum[:, 2 + b.q % 2, :]
                        nc.tensor.matmul(o, hT[b.q % 2], w1[:, ds(at, DH)], start=True, stop=False)
                        nc.tensor.matmul(o, ones3[:, :], bias3[:, ds(at, DH)], start=False, stop=True)\
                            .then_inc(X.up_psum, 1)
                    if c:
                        at = pe.value_load(EOFF[0:1, ds(c.u, 1)], min_val=0, max_val=(E - 1) * DH)
                        pe.wait_ge(X.ehT_ready, c.u + 1)
                        later(pe, X.yo_ready, c.u - 1)
                        for k in range(NF):
                            last = nc.tensor.matmul(psum[:, 6 + c.q % 2, 0:F],
                                                    EHT[c.q % 2][:, k * 128:(k + 1) * 128],
                                                    w2[:, ds(at + k * F, F)], start=(k == 0),
                                                    stop=(k == NF - 1))
                        last.then_inc(X.down_psum, 1)
                skewed(pe, body, NBLK, 4)

            @block.scalar
            def _(act):
                def body(a, b, c):
                    if b:
                        act.wait_ge(X.up_psum, b.u + 1)
                        later(act, X.ehT_psum, b.u - 1)
                        nc.scalar.activation(EH[b.q % 2], psum[:, 2 + b.q % 2, :], ACT.Silu)\
                            .then_inc(X.eh_ready, 1)
                    if c:
                        act.wait_ge(X.down_psum, c.u + 1)
                        later(act, y_stored[c.q], 16 * c.n)
                        nc.scalar.activation(YO[c.q], psum[:, 6 + c.q % 2, 0:F], ACT.Copy)\
                            .then_inc(X.yo_ready, 1)
                        act.wait_ge(X.yo_ready, c.u + 1)
                        act.dma_start(y_slots[ds(BLK * c.u, BLK), :], YO[c.q]).then_inc(y_stored[c.q], 16)
                skewed(act, body, NBLK, 4)
                for q in range(4):
                    act.wait_ge(y_stored[q], 16 * (NBLK // 4))

            @block.vector
            def _(dve):
                def body(a, b, c):
                    if a:
                        dve.wait_ge(X.xT_psum, a.u + 1)
                        later(dve, X.up_psum, a.u - 1)
                        nc.vector.tensor_scalar(hT[a.q % 2], psum[:, a.q % 2, 0:BLK], lng[:, 0:1],
                                                lnb[:, 0:1], ALU.mult, ALU.add).then_inc(X.hT_ready, 1)
                    if c:
                        dve.wait_ge(X.ehT_psum, c.u + 1)
                        later(dve, X.down_psum, c.u - 1)
                        nc.vector.tensor_copy(EHT[c.q % 2], psum[:, 4 + c.q % 2, :]).then_inc(X.ehT_ready, 1)
                skewed(dve, body, NBLK, 4)

        names = ("idx0 idx1 gath0 gath1 mixed stats_done ve_ready rs_ready fh_ready fhT_psum fhT_ready "
                 "up_psum up_used down_psum rest_ready out_ready st0 st1 own dve_own")
        D = namedtuple("D", names)(*[sem("d_" + n) for n in names.split()])
        idx_here = (D.idx0, D.idx1)
        gathered = (D.gath0, D.gath1)
        stored = (D.st0, D.st1)
        with nc.Block() as block:
            outv = out.rearrange("(g p) f -> p g f", p=CH)

            @block.gpsimd
            def _(pool):
                last_slot = pool.to_reg(SLOTS - 1)

                def gather(u):
                    pool.wait_ge(idx_here[u.q], u.n + 1)
                    later(pool, D.mixed, u.u - 1)
                    pool.sem_inc(pool_turns)
                    for k in range(8):
                        nc.gpsimd.indirect_dma_start(
                            out=GY[u.q][:, k, :], out_offset=None, in_=y_slots,
                            in_offset=bass.IndirectOffsetOnAxis(ap=idx_st[u.q][:, k:k + 1], axis=0),
                            bounds_check=last_slot, oob_is_err=False).then_inc(gathered[u.q], 16)

                def add_rest(b):
                    pool.wait_ge(D.mixed, b.u + 1)
                    pool.wait_ge(idx_here[b.q], b.n + 1)
                    later(pool, D.out_ready, b.u)
                    own_begin(b.u)
                    own(nc.gpsimd.tensor_tensor(rest2, h_st[b.q],
                                                mo[b.q].rearrange("p j f -> p (j f)"), ALU.add))
                    nc.gpsimd.tensor_tensor(rest.rearrange("p (j f) -> p j f", f=F),
                                            rest2.rearrange("p (j f) -> p j f", f=F),
                                            b_f2[:, :].unsqueeze(1).broadcast_to([CH, 4, F]), ALU.add)\
                        .then_inc(D.rest_ready, 1)

                own_begin, own = stepper(pool, D.own)

                def body(a, b, c):
                    if b:
                        pool.wait_ge(D.ve_ready, b.u + 1)
                        nc.gpsimd.tensor_tensor(rs3[:, :], ve3[:, :], minus_half[0:CH, 0:4], ALU.pow)\
                            .then_inc(D.rs_ready, 1)
                    if a: gather(a)
                    if b: add_rest(b)
                skewed(pool, body, UNITS)

            @block.vector
            def _(dve):
                step_begin, step = stepper(dve, D.dve_own)

                def mixture(b):
                    dve.wait_ge(gathered[b.q], 128 * (b.n + 1))
                    later(dve, D.rest_ready, b.u - 1)
                    for j in range(4):
                        last = nc.vector.scalar_tensor_tensor(
                            mo[b.q][:, j, :], GY[b.q][0:CH, 2 * j, :], VAL[:, 0, ds(4 * b.u + j, 1)],
                            MOE[:, ds(512 * b.u + j * F, F)], ALU.mult, ALU.add)
                    step(last)
                    for j in range(4):
                        last = nc.vector.scalar_tensor_tensor(
                            mo[b.q][:, j, :], GY[b.q][0:CH, 2 * j + 1, :], VAL[:, 1, ds(4 * b.u + j, 1)],
                            mo[b.q][:, j, :], ALU.mult, ALU.add)
                    last.then_inc(D.mixed, 1)
                    dve.wait_ge(D.mixed, b.u + 1)
                    nc.vector.memset(wait_carrier[:, :], 0.0)
                    for j in range(4):
                        last = nc.vector.bn_stats(st3[:, j, :], mo[b.q][:, j, :])
                    step(last)
                    nc.vector.memset(wait_carrier[:, :], 0.0)
                    for j in range(4):
                        last = nc.vector.bn_aggr(mv3[:, j, :], st3[:, j, :])
                    step(last)
                    nc.vector.tensor_scalar(ve3[:, :], mv3[:, :, 1], EPS, None, ALU.add).then_inc(D.ve_ready, 1)

                def norm(b):
                    dve.wait_ge(D.rs_ready, b.u + 1)
                    later(dve, D.fhT_psum, b.u)
                    for j in range(4):
                        last = nc.vector.tensor_scalar(fh[:, j, :], mo[b.q][:, j, :], mv3[:, j, 0:1],
                                                       rs3[:, j:j + 1], ALU.subtract, ALU.mult)
                    last.then_inc(D.fh_ready, 1)

                def affine(b):
                    dve.wait_ge(D.fhT_psum, b.u + 1)
                    later(dve, D.up_psum, 4 * b.u)
                    nc.vector.tensor_scalar(fhT, psum[:, 0, 0:UT], fg[:, 0:1], fbb[:, 0:1], ALU.mult,
                                            ALU.add).then_inc(D.fhT_ready, 1)

                def final(c):
                    dve.wait_ge(D.down_psum, c.u + 1)
                    dve.wait_ge(D.rest_ready, c.u + 1)
                    later(dve, stored[c.q], 32 * c.n)
                    nc.vector.tensor_tensor(outb[c.q], psum[0:CH, 5, :], rest, ALU.add)\
                        .then_inc(D.out_ready, 1)

                def body(a, b, c):
                    if c: final(c)
                    if b:
                        step_begin(3 * b.u)
                        mixture(b)
                        norm(b)
                        affine(b)
                skewed(dve, body, UNITS)

            @block.tensor
            def _(pe):
                def body(a, b, c):
                    if b:
                        pe.wait_ge(D.fh_ready, b.u + 1)
                        later(pe, D.fhT_ready, b.u)
                        for j in range(4):
                            last = nc.tensor.transpose(psum[:, 0, j * CH:(j + 1) * CH], fh[:, j, :],
                                                       ident[0:CH, 0:CH])
                        last.then_inc(D.fhT_psum, 1)
                        pe.wait_ge(D.fhT_ready, b.u + 1)
                        for k in range(NF):
                            later(pe, D.up_used, 4 * (b.u - 1) + k + 1)
                            nc.tensor.matmul(psum[:, 1 + k, 0:UT], w_f1[:, k * 128:(k + 1) * 128], fhT,
                                             start=True, stop=True).then_inc(D.up_psum, 1)
                        pe.wait_ge(D.up_used, 4 * b.u + 4)
                        later(pe, D.out_ready, b.u)
                        for j in range(4):
                            for k in range(NF):
                                last = nc.tensor.matmul(psum[0:CH, 5, j * F:(j + 1) * F],
                                                        FH[:, k, j * CH:(j + 1) * CH], w_f2[:, k, :],
                                                        start=(k == 0), stop=(k == NF - 1))
                        last.then_inc(D.down_psum, 1)
                skewed(pe, body, UNITS)

            @block.scalar
            def _(act):
                def body(a, b, c):
                    if a:
                        later(act, gathered[a.q], 128 * a.n)
                        later(act, D.rest_ready, a.u - 1)
                        nc.scalar.activation(h_st[a.q], Hb[:, ds(4 * F * a.u, 4 * F)], ACT.Copy)
                        nc.scalar.activation(idx_st[a.q][:, :], IDX[:, ds(4 * a.u, 4), :]
                                             .rearrange("p j k -> p (j k)"), ACT.Copy)\
                            .then_inc(idx_here[a.q], 1)
                    if b:
                        for k in range(NF):
                            act.wait_ge(D.up_psum, 4 * b.u + k + 1)
                            if k == 0:
                                later(act, D.down_psum, b.u)
                            nc.scalar.activation(FH[:, k, :], psum[:, 1 + k, 0:UT], ACT.Silu,
                                                 bias=b_f1[:, k:k + 1]).then_inc(D.up_used, 1)
                skewed(act, body, UNITS)

            @block.sync
            def _(sp):
                def store(u):
                    sp.wait_ge(D.out_ready, u.u + 1)
                    for p0, p1 in ((0, 112), (112, CH)):
                        sp.dma_start(outv[p0:p1, ds(4 * u.u, 4), :],
                                     outb[u.q][p0:p1, :].rearrange("p (j f) -> p j f", f=F))\
                          .then_inc(stored[u.q], 16)
                streamed(sp, store, UNITS)
                for q in range(2):
                    sp.wait_ge(stored[q], 32 * (UNITS // 2))


def kernel(**inputs):
    import numpy as np
    import concourse.bacc as bacc
    from concourse.bass_utils import run_bass_kernel_spmd

    w = {k: np.asarray(v) for k, v in inputs.items()}
    x = w["x"].reshape(32 * 256, 64)

    def cols(v, n):
        return v.reshape(n, 128).T

    arrays = {
        "x2": np.concatenate([x, np.concatenate([x[1:], x[:1]], axis=0)], axis=1),
        "tok_kernel": w["L0_tok_kernel"], "tok_bias": w["L0_tok_bias"],
        "in_proj": w["L0_attn_in_proj_w"], "conv_w": w["L0_attn_conv_w"].reshape(384 * 4),
        "conv_b": cols(w["L0_attn_conv_b"], 3), "dt_bias": w["L0_attn_dt_bias"],
        "A_log": w["L0_attn_A_log"], "D_skip": w["L0_attn_D_skip"],
        "norm_w": cols(w["L0_attn_norm_w"], 2), "out_proj": w["L0_attn_out_proj_w"],
        "ln_g": cols(w["L0_ffn_ln_in_g"], 1), "ln_b": cols(w["L0_ffn_ln_in_b"], 1),
        "router_w": w["L0_ffn_router_w"], "router_b": w["L0_ffn_router_b"],
        "ew1": w["L0_ffn_ew1"], "eb1": w["L0_ffn_eb1"], "ew2": w["L0_ffn_ew2"], "eb2": w["L0_ffn_eb2"],
        "sw1": w["L0_ffn_sw1"], "sb1": cols(w["L0_ffn_sb1"], 2), "sw2": w["L0_ffn_sw2"],
        "sb2": w["L0_ffn_sb2"], "ffg": cols(w["L0_ffn_ff_ln_g"], 1), "ffb": cols(w["L0_ffn_ff_ln_b"], 1),
        "fw1": w["L0_ffn_ff_w1"], "fb1": cols(w["L0_ffn_ff_b1"], 4), "fw2": w["L0_ffn_ff_w2"],
        "fb2": w["L0_ffn_ff_b2"],
    }
    arrays = {"in_" + k: np.ascontiguousarray(v) for k, v in arrays.items()}
    nc = bacc.Bacc("TRN2", target_bir_lowering=False, num_devices=1)
    fp32 = mybir.dt.float32
    args = [nc.dram_tensor(k, v.shape, fp32, kind="ExternalInput").ap() for k, v in arrays.items()]
    out = nc.dram_tensor("out_tokens", (32 * 248, 128), fp32, kind="ExternalOutput").ap()
    audio_tower(nc, *args, out)
    r = run_bass_kernel_spmd(nc, [arrays], core_ids=[0])
    return r.results[0]["out_tokens"].reshape(32, 248, 128)
```

```python
import concourse.bass as bass
from concourse import mybir
from collections import namedtuple
from contextlib import ExitStack

Unit = namedtuple("Unit", "u n q")


def skewed(eng, body, units, turns=2):
    def unit(i, c):
        return Unit(turns * i + c, i + c // turns, c % turns)

    body(unit(0, 0), None, None)
    body(unit(0, 1), unit(0, 0), None)
    for c in range(turns):
        body(unit(0, c + 2), unit(0, c + 1), unit(0, c))
    rounds = (units - 2) // turns
    with eng.Fori(1, rounds) as i:
        for c in range(turns):
            body(unit(i, c + 2), unit(i, c + 1), unit(i, c))
    for c in range(rounds * turns, units - 2):
        body(unit(0, c + 2), unit(0, c + 1), unit(0, c))
    body(None, unit(0, units - 1), unit(0, units - 2))
    body(None, None, unit(0, units - 1))


def streamed(eng, step, units, turns=2):
    def unit(i, c):
        return Unit(turns * i + c, i + c // turns, c % turns)

    for c in range(turns):
        step(unit(0, c))
    with eng.Fori(1, units // turns) as i:
        for c in range(turns):
            step(unit(i, c))
    for c in range(units // turns * turns, units):
        step(unit(0, c))


def ahead(eng, front, back, units, lead, turns=2):
    def unit(i, c):
        return Unit(turns * i + c, i + c // turns, c % turns)

    for c in range(lead):
        front(unit(0, c))
    steps = units - lead
    for c in range(turns):
        front(unit(0, c + lead))
        back(unit(0, c))
    with eng.Fori(1, steps // turns) as i:
        for c in range(turns):
            front(unit(i, c + lead))
            back(unit(i, c))
    for c in range(steps // turns * turns, steps):
        front(unit(0, c + lead))
        back(unit(0, c))
    for c in range(steps, units):
        back(unit(0, c))


def later(eng, counter, value):
    if not isinstance(value, int) or value > 0:
        eng.wait_ge(counter, value)


def audio_tower(nc, x2, tok_kernel, tok_bias, in_proj, conv_w, conv_b, dt_bias, A_log, D_skip, norm_w,
                out_proj, ln_g, ln_b, router_w, router_b, ew1, eb1, ew2, eb2, sw1, sb1, sw2, sb2,
                ffg, ffb, fw1, fb1, fw2, fb2, out):
    fp32 = mybir.dt.float32
    bf16 = mybir.dt.bfloat16
    i32 = mybir.dt.int32
    ALU = mybir.AluOpType
    ACT = mybir.ActivationFunctionType
    AX = mybir.AxisListType
    ds = bass.ds

    SEQS, LIN, CIN, TAPS = 32, 256, 64, 9
    L = LIN - TAPS + 1
    F = 128
    CH = L // 2
    UNITS = SEQS // 2
    NCH = 2 * SEQS
    UT = 2 * L
    NH, HD, NS = 4, 64, 64
    DI = NH * HD
    KC = 4
    PADL = KC - 1
    E, DH, DSH = 16, 512, 256
    NF = DH // 128
    TEMP = 0.7
    EPS = 1e-5
    TOK_EPS = 1e-7
    LAM = 1.0 / (1.0 + TOK_EPS)
    T = SEQS * L
    BLK = 128
    NBLK = (2 * T) // BLK + E
    NBLK += NBLK % 2
    SLOTS = NBLK * BLK
    CB = E + 1
    NO_ROW = float(1 << 20)
    EXP1 = 2.718281828459045

    x_slots = nc.dram_tensor("x_slots", (SLOTS, F + 1), fp32, kind="Internal").ap()
    y_tokens = nc.dram_tensor("y_tokens", (CH * 2 * NCH, F), fp32, kind="Internal").ap()

    ctx = ExitStack()
    with ctx:
        def sb(name, shape, dt=fp32):
            return ctx.enter_context(nc.sbuf_tensor(name, shape, dt))

        def sem(name):
            return ctx.enter_context(nc.semaphore(name))

        ident = sb("ident", [128, 128])
        ones_col = sb("ones_col", [128, 1])
        minus_half = sb("minus_half", [128, 64])
        euler = sb("euler", [128, 16])
        eps_row = sb("eps_row", [128, 4])
        keep = sb("keep", [CH, 4 * NH])
        wait_carrier = sb("wait_carrier", [1, 1])
        tokb = sb("tokb", [CH, F])
        row_ids = tokb[:, :].bitcast(i32)
        cb = sb("cb", [128, 3])
        dtb = sb("dtb", [CH, NH])
        a_log = sb("a_log", [CH, NH])
        a_neg = sb("a_neg", [CH, 4, NH])
        d_col = sb("d_col", [128, 2])
        nw = sb("nw", [128, 2])
        scale = sb("scale", [CH, NCH])
        lng = sb("lng", [128, 1])
        lnb = sb("lnb", [128, 1])
        rw = sb("rw", [128, E])
        rb = sb("rb", [CH, E])
        w_s1 = sb("w_s1", [128, DSH])
        b_s1 = sb("b_s1", [128, 2])
        w_s2 = sb("w_s2", [128, 2, F])
        w_e2b = sb("w_e2b", [CB, F])
        fg = sb("fg", [128, 1])
        fbb = sb("fbb", [128, 1])
        w_f1 = sb("w_f1", [128, DH])
        b_f1 = sb("b_f1", [128, NF])
        w_f2 = sb("w_f2", [128, NF, F])
        b_e1 = sb("b_e1", [128, E * NF])
        tri = sb("tri", [CH, CH], bf16)
        ones_sq = sb("ones_sq", [CH, 128], bf16)

        MV = sb("MV", [CH, NCH, 2])
        COMB = sb("COMB", [CH, NCH * CB])
        VAL = sb("VAL", [CH, 2, NCH])
        IDX = sb("IDX", [128, NCH, 2], i32)
        idx_st = [sb(f"idx_st{q}", [128, 8], i32) for q in range(2)]
        EOFF = sb("EOFF", [1, NBLK], i32)
        cumP = sb("cumP", [128, E])
        block_no = sb("block_no", [1, NBLK])
        rev_iota = sb("rev_iota", [128, E])
        st3 = sb("st3", [CH, 4, 6])
        mv3 = sb("mv3", [CH, 4, 2])
        ve3 = sb("ve3", [CH, 4])
        rs3 = sb("rs3", [CH, 4])
        b_f2 = sb("b_f2", [CH, F])
        Hb = sb("Hb", [CH, NCH * F])

        ARENA = 36600
        arena = sb("arena", [128, ARENA])

        pos = [0]

        def take(parts, *shape):
            n = 1
            for k in shape:
                n *= k
            v = arena[0:parts, pos[0]:pos[0] + n]
            pos[0] += n
            assert pos[0] <= ARENA, pos[0]
            if len(shape) == 2:
                v = v.rearrange("p (a b) -> p a b", b=shape[1])
            if len(shape) == 3:
                v = v.rearrange("p (a b c) -> p a b c", b=shape[1], c=shape[2])
            return v

        pos[0] = 0
        x_all = take(128, 2 * SEQS, CIN)
        x_sq = take(128, 2 * SEQS, CIN)
        sq = take(128, 2 * SEQS)
        wsq = take(CH, NCH)
        wnorm = take(CH, NCH)
        small = take(CH, NCH)
        plus_half = take(CH, NCH)
        wmix = take(CH, NCH)
        band = take(128, 4, CH)
        cw = take(128, 384 * KC)
        zero_src = take(128, 10, F + 1)
        iota_i = take(128, E).bitcast(i32)
        iota_b = take(1, NBLK).bitcast(i32)
        assert pos[0] <= 14800
        pos[0] = 0
        xin = [take(128, 4, 128) for _ in range(2)]
        xT = take(128, 4 * 128)
        v_s = take(CH, 4 * F)
        v_t = take(CH, 4 * F)
        v_b = take(CH, 4 * F)
        hn = take(CH, 4, F)
        Z = [take(128, 2, UT) for _ in range(2)]
        XT = [take(128, 2, UT) for _ in range(2)]
        BT = [take(64, UT) for _ in range(2)]
        CT = [take(64, UT) for _ in range(2)]
        dt = [take(CH, 4 * NH) for _ in range(2)]
        dec = [take(CH, 4, NH) for _ in range(2)]
        Xd = take(CH, 4, DI)
        L0 = take(CH, NH, L)
        L1 = take(CH, NH, CH)
        M0 = take(CH, NH, L)
        M1 = take(CH, NH, CH)
        Tg = take(128, 2, UT)
        Yg = take(128, 2, UT)
        Sq = take(128, 2, UT)
        st = take(CH, 4, 6)
        mv = take(CH, 4, 2)
        ve = take(CH, 4)
        rstd = take(CH, 4)
        ms = take(CH, 4)
        rr = take(CH, 4)
        uu = take(CH, 16)
        nab = take(CH, 16)
        ee = take(CH, 16)
        qq = take(CH, 16)
        rq = take(CH, 16)
        ss = take(CH, 16)
        s2 = take(CH, 16)
        pa = take(CH, 16)
        pb = take(CH, 16)
        tt = take(CH, 16)
        dA = take(CH, 16)
        ee2 = take(CH, 16)
        pos[0] = max(pos[0], 14800)
        diag2 = take(CH, 2, L)
        tokw = take(128, 5, F)
        w_in = take(F, 644)
        w_tap = take(F, KC, 384)
        w_out = take(128, 2, F)
        hnT = [take(128, 2, L + PADL) for _ in range(2)]
        pos[0] = 0
        XNR = take(CH, NCH * F)
        HHT = take(128, UNITS * 512)
        MOE = HHT[0:CH, :]
        after_phase_a = pos[0]
        EW = DH + NF
        w1 = take(128, E * EW)
        w2 = take(128, E * EW)
        staging_at = pos[0]
        pos[0] = after_phase_a
        LG = take(CH, NCH * E)
        r12 = take(CH, NCH)
        r1p = take(CH, NCH)
        nmr = take(CH, NCH)
        v64 = [take(CH, NCH) for _ in range(4)]
        xnr = [take(CH, 4, F) for _ in range(2)]
        hhT = [take(128, UT) for _ in range(2)]
        big = [take(128, NCH * E) for _ in range(9)]
        sml = [take(128, E) for _ in range(8)]
        row = [take(CH, NCH) for _ in range(6)]
        mask = take(CH, NCH * E // 2).bitcast(bf16)
        sml_blocks = take(1, NBLK)
        assert pos[0] <= staging_at
        pos[0] = staging_at
        x_st = [take(128, 4, 2, F + 1) for _ in range(2)]
        comb_st = take(CH, 4, CB)
        combT = take(CB, UT)
        SH = take(128, 2, UT)
        pos[0] = staging_at
        pos[0] = 0
        xb = [take(128, F + 1) for _ in range(4)]
        y_row = [take(128, 1).bitcast(i32) for _ in range(4)]
        hT = [take(128, F) for _ in range(2)]
        w1_blk = [take(128, EW) for _ in range(4)]
        EHT = [take(128, DH) for _ in range(2)]
        YO = [take(128, F) for _ in range(4)]
        assert pos[0] <= NCH * F
        pos[0] = 0
        GY = [take(CH, 8, F) for _ in range(2)]
        mo = [take(CH, 4, F) for _ in range(2)]
        fh = take(CH, 4, F)
        fhT = take(128, UT)
        FH = take(128, NF, UT)
        rest = take(CH, 4 * F)
        h_st = take(CH, 4 * F)
        pos[0] = staging_at
        outb = [take(CH, 4 * F) for _ in range(2)]
        rest2 = take(CH, 4 * F)

        psum = ctx.enter_context(nc.psum_tensor("psum", [128, 8, 512], fp32))

        chain_count = {}

        def link(eng, counter, ins):
            chain_count[counter.name] = chain_count.get(counter.name, 0) + 1
            ins.then_inc(counter, 1)
            eng.wait_ge(counter, chain_count[counter.name])

        ld_x = sem("ld_x")
        ld_tok = sem("ld_tok")
        ld_ssm = sem("ld_ssm")
        ld_ffn = sem("ld_ffn")
        ld_experts = sem("ld_experts")
        zeros_ready = sem("zeros_ready")
        slots_zeroed = sem("slots_zeroed")
        pool_step = sem("pool_step")
        dve_step = sem("dve_step")
        pool_turns = sem("pool_turns")
        bands_ready = sem("bands_ready")
        squares_ready = sem("squares_ready")
        row_squares_ready = sem("row_squares_ready")
        windows_ready = sem("windows_ready")
        wsq_ready = sem("wsq_ready")
        wnorm_ready = sem("wnorm_ready")
        a_ready = sem("a_ready")

        def rows(v, parts):
            return v.rearrange("(a n) -> a n", a=1).partition_broadcast(parts) if len(v.shape) == 1 else v

        with nc.Block() as block:
            @block.sync
            def _(sp):
                sp.dma_start(x_all, x2[:, 0:CIN].rearrange("(n p) c -> p n c", p=128)).then_inc(ld_x, 16)
                kw = tok_kernel.rearrange("k c f -> c k f")
                sp.dma_start(tokw[0:64, 0:5, :], kw[:, 0:TAPS:2, :]).then_inc(ld_tok, 16)
                sp.dma_start(tokw[64:128, 0:4, :], kw[:, 1:TAPS:2, :]).then_inc(ld_tok, 16)
                sp.dma_start(tokb[:, :], rows(tok_bias, CH)).then_inc(ld_tok, 16)
                for dst, src in ((w_in, in_proj), (cw, rows(conv_w, 128)), (cb[:, :], conv_b),
                                 (dtb[:, :], rows(dt_bias, CH)), (a_log[:, :], rows(A_log, CH)),
                                 (d_col[0:64, :], rows(D_skip[0:4:2], 64)),
                                 (d_col[64:128, :], rows(D_skip[1:4:2], 64)), (nw[:, :], norm_w),
                                 (w_out, out_proj.rearrange("(c p) f -> p c f", p=128))):
                    with nc.allow_non_contiguous_dma(reason="small vectors"):
                        sp.dma_start(dst, src).then_inc(ld_ssm, 16)
                for dst, src in ((lng[:, :], ln_g), (lnb[:, :], ln_b), (rw[:, :], router_w),
                                 (rb[:, :], rows(router_b, CH)), (w_s1[:, :], sw1), (b_s1[:, :], sb1),
                                 (w_s2[:, :, :], sw2.rearrange("(c p) f -> p c f", p=128)),
                                 (w_e2b[0:E, :], eb2), (w_e2b[E:CB, :], rows(sb2, 1)), (fg[:, :], ffg),
                                 (fbb[:, :], ffb), (w_f1[:, :], fw1), (b_f1[:, :], fb1),
                                 (w_f2[:, :, :], fw2.rearrange("(c p) f -> p c f", p=128)),
                                 (b_f2[:, :], rows(fb2, CH)), (b_e1[:, :], eb1)):
                    with nc.allow_non_contiguous_dma(reason="small vectors"):
                        sp.dma_start(dst, src).then_inc(ld_ffn, 16)
                sp.wait_ge(zeros_ready, 2)
                zr = x_slots.rearrange("(n p) f -> p n f", p=128)
                for n in range(0, NBLK, 10):
                    sp.dma_start(zr[:, n:n + 10, :], zero_src)\
                      .then_inc(slots_zeroed, 16)
                sp.wait_ge(slots_zeroed, 16 * (NBLK // 10))

            @block.gpsimd
            def _(pool):
                nc.gpsimd.memset(zero_src[:, :, 0:F], 0.0).then_inc(zeros_ready, 1)
                nc.gpsimd.memset(zero_src[:, :, F:F + 1], NO_ROW).then_inc(zeros_ready, 1)
                nc.gpsimd.memset(minus_half[:, :], -0.5)
                nc.gpsimd.memset(plus_half, 0.5)
                nc.gpsimd.memset(euler[:, :], EXP1)
                nc.gpsimd.memset(eps_row[:, :], EPS)
                nc.gpsimd.memset(ones_col[:, :], 1.0)
                nc.gpsimd.memset(IDX[:, :, :], 1 << 20)
                nc.gpsimd.memset(COMB[:, :], 0.25)
                nc.gpsimd.memset(ones_sq[:, :], 1.0)
                nc.gpsimd.memset(band, 1.0)
                nc.gpsimd.memset(ident[:, :], 0.0)
                nc.gpsimd.memset(diag2, 0.0)
                nc.gpsimd.memset(tri[:, :], 0.0)
                link(pool, pool_step, nc.gpsimd.iota(iota_i, pattern=[[-1, E]], base=E, channel_multiplier=0))
                nc.gpsimd.tensor_copy(rev_iota[:, :], iota_i)
                link(pool, pool_step, nc.gpsimd.iota(iota_b, pattern=[[1, NBLK]], base=0,
                                                     channel_multiplier=0))
                nc.gpsimd.tensor_copy(block_no[:, :], iota_b)
                for j in range(2):
                    for c in range(2):
                        v = band[:, 2 * j + c, :]
                        nc.gpsimd.affine_select(out=v, in_=v, compare_op=ALU.is_ge, fill=0.0,
                                                base=128 * j - CH * c, pattern=[[-1, CH]],
                                                channel_multiplier=1)
                link(pool, pool_step, nc.gpsimd.affine_select(
                    out=ident[:, :], in_=ident[:, :], compare_op=ALU.not_equal, fill=1.0, base=0,
                    pattern=[[-1, 128]], channel_multiplier=1))
                for j in range(2):
                    for c in range(2):
                        v = band[:, 2 * j + c, :]
                        last = nc.gpsimd.affine_select(out=v, in_=v, compare_op=ALU.is_ge, fill=0.0,
                                                       base=TAPS - 1 - 128 * j + CH * c,
                                                       pattern=[[1, CH]], channel_multiplier=-1)
                last.then_inc(bands_ready, 1)
                nc.gpsimd.affine_select(out=diag2[:, :, 0:CH], in_=diag2[:, :, 0:CH],
                                        compare_op=ALU.not_equal, fill=1.0, base=0,
                                        pattern=[[0, 2], [-1, CH]], channel_multiplier=1)
                nc.gpsimd.affine_select(out=tri[:, :], in_=tri[:, :], compare_op=ALU.is_ge, fill=1.0,
                                        base=0, pattern=[[-1, CH]], channel_multiplier=1)
                pool.wait_ge(ld_x, 16)
                nc.gpsimd.tensor_tensor(x_sq, x_all, x_all, ALU.mult).then_inc(squares_ready, 1)
                pool.wait_ge(ld_ssm, 16 * 9)
                link(pool, pool_step, nc.gpsimd.tensor_tensor(a_neg[:, 0, :], euler[0:CH, 0:NH], a_log[:, :],
                                                              ALU.pow))
                for j in range(3, -1, -1):
                    last = nc.gpsimd.tensor_scalar(a_neg[:, j, :], a_neg[:, 0, :], -1.0, 0.0,
                                                   ALU.mult, ALU.add)
                last.then_inc(a_ready, 1)
                pool.wait_ge(wsq_ready, 1)
                nc.gpsimd.tensor_tensor(wnorm, wsq, plus_half, ALU.pow).then_inc(wnorm_ready, 1)

            @block.tensor
            def _(pe):
                pe.wait_ge(row_squares_ready, 1)
                pe.wait_ge(bands_ready, 1)
                pe.wait_ge(ld_tok, 48)
                sqv = sq.rearrange("p (b j) -> p j b", j=2)
                for c in range(2):
                    for j in range(2):
                        last = nc.tensor.matmul(psum[0:CH, 0, c * SEQS:(c + 1) * SEQS],
                                                band[:, 2 * j + c, :], sqv[:, j, :],
                                                start=(j == 0), stop=(j == 1))
                last.then_inc(windows_ready, 1)

            @block.vector
            def _(dve):
                nc.vector.memset(hnT[0], 0.0)
                nc.vector.memset(keep[:, :], 1.0)
                link(dve, dve_step, nc.vector.memset(wait_carrier[:, :], 0.0))
                nc.vector.memset(keep[0:1, :].rearrange("p (b c h) -> p b c h", b=2, c=2)[:, :, 0, :], 0.0)
                nc.vector.memset(hnT[1], 0.0)
                dve.wait_ge(squares_ready, 1)
                nc.vector.tensor_reduce(sq, x_sq, AX.X, ALU.add).then_inc(row_squares_ready, 1)
                dve.wait_ge(ld_ssm, 16 * 9)
                cwv = cw.rearrange("p (c k) -> p k c", k=KC)
                for k in range(KC):
                    nc.vector.tensor_tensor(w_tap[:, k, :], w_in[:, DI:DI + 384], cwv[:, k, :], ALU.mult)
                for c in range(2):
                    nc.vector.tensor_scalar(w_out[:, c, :], w_out[:, c, :], nw[:, c:c + 1], None, ALU.mult)
                dve.wait_ge(ld_ffn, 16 * 16)
                nc.vector.tensor_scalar(w_s2[:, :, :], w_s2[:, :, :], 0.25, None, ALU.mult)
                dve.wait_ge(windows_ready, 1)
                nc.vector.tensor_scalar(wsq.rearrange("p (b c) -> p c b", c=2),
                                        psum[0:CH, 0, 0:NCH].rearrange("p (c b) -> p c b", c=2),
                                        0.0, None, ALU.max).then_inc(wsq_ready, 1)
                dve.wait_ge(wnorm_ready, 1)
                nc.vector.tensor_scalar(wmix, wnorm, 1.0, None, ALU.is_lt)
                link(dve, dve_step, nc.vector.tensor_scalar(small, wnorm, TOK_EPS, None, ALU.add))
                link(dve, dve_step, nc.vector.reciprocal(wsq, small))
                link(dve, dve_step, nc.vector.tensor_scalar(small, wmix, -1.0, 1.0, ALU.mult, ALU.add))
                link(dve, dve_step, nc.vector.tensor_tensor(wsq, wsq, small, ALU.mult))
                link(dve, dve_step, nc.vector.tensor_tensor(wsq, wsq, wmix, ALU.add))
                link(dve, dve_step, nc.vector.tensor_scalar(scale[:, :], wsq, LAM, None, ALU.mult))

        names = ("x_in0 x_in1 xT_psum xT_ready conv_done conv_scaled tanh_done biased h_ready "
                 "stats_ready rstd_ready hn_ready hnT_psum hnT_ready pd_ready dtu_ready ip_ready ip_used "
                 "nab_ready exp_ready dt_ready dec_ready px_ready xd_ready g_ready pb_ready scan_done "
                 "m_ready y_psum t_ready yg_ready sq_ready po_ready pr_ready ms_ready rr_ready po_used "
                 "dve_link pool_link")
        s = {n: sem("a_" + n) for n in names.split()}
        S = namedtuple("S", s)(**s)
        x_in = (S.x_in0, S.x_in1)

        def stepper(eng, counter):
            at = [0]

            def begin(done):
                at[0] = done

            def step(ins):
                at[0] = at[0] + 1
                ins.then_inc(counter, 1)
                eng.wait_ge(counter, at[0])
            return begin, step

        bank_of = (2, 3, 2, 2, 3)

        with nc.Block() as block:
            x2t = x2.rearrange("(n p) c -> p n c", p=128)

            @block.sync
            def _(sp):
                def load(u):
                    later(sp, S.xT_psum, u.u - 1)
                    sp.dma_start(xin[u.q], x2t[:, ds(4 * u.u, 4), :]).then_inc(x_in[u.q], 16)
                streamed(sp, load, UNITS)

            @block.tensor
            def _(pe):
                def x_transposes(a):
                    pe.wait_ge(x_in[a.q], 16 * (a.n + 1))
                    later(pe, S.hnT_ready, a.u)
                    for j in range(4):
                        last = nc.tensor.transpose(psum[:, 0, j * 128:(j + 1) * 128], xin[a.q][:, j, :],
                                                   ident[:, :])
                    last.then_inc(S.xT_psum, 1)

                def conv(a):
                    pe.wait_ge(S.xT_ready, a.u + 1)
                    later(pe, S.conv_scaled, a.u)
                    for j in range(4):
                        t0 = LIN * (j // 2) + CH * (j % 2)
                        for k in range(5):
                            p = 128 if k < 4 else 64
                            last = nc.tensor.matmul(psum[0:CH, 1, j * F:(j + 1) * F],
                                                    xT[0:p, t0 + 2 * k:t0 + 2 * k + CH], tokw[0:p, k, :],
                                                    start=(k == 0), stop=(k == 4))
                    last.then_inc(S.conv_done, 1)

                def hn_transposes(a):
                    pe.wait_ge(S.hn_ready, a.u + 1)
                    for j in range(4):
                        last = nc.tensor.transpose(psum[:, 0, j * CH:(j + 1) * CH], hn[:, j, :],
                                                   ident[0:CH, 0:CH])
                    last.then_inc(S.hnT_psum, 1)

                def dt_projection(b):
                    pe.wait_ge(S.ip_used, 5 * b.u + 2)
                    for j in range(4):
                        t0 = PADL + CH * (j % 2)
                        last = nc.tensor.matmul(psum[0:CH, 3, 128 * j:128 * j + 128],
                                                hnT[b.q][:, j // 2, t0:t0 + CH], w_in[:, 516:644],
                                                start=True, stop=True)
                    last.then_inc(S.pd_ready, 1)

                def projection(b, k):
                    if k == 0:
                        pe.wait_ge(S.hnT_ready, b.u + 1)
                    if k == 4:
                        pe.wait_ge(S.dtu_ready, b.u + 1)
                    else:
                        later(pe, S.ip_used, 5 * b.u + (0, 0, 1, 3)[k])
                    o = psum[:, bank_of[k], 0:UT]
                    if k < 2:
                        last = nc.tensor.matmul(o, w_in[:, k * 128:(k + 1) * 128],
                                                hnT[b.q][:, :, PADL:], start=True, stop=True)
                    else:
                        for w in range(KC):
                            last = nc.tensor.matmul(o, w_tap[:, w, (k - 2) * 128:(k - 1) * 128],
                                                    hnT[b.q][:, :, w:w + L], start=(w == 0),
                                                    stop=(w == KC - 1))
                    last.then_inc(S.ip_ready, 1)

                def x_rows(c):
                    pe.wait_ge(S.ip_used, 5 * c.u + 4)
                    later(pe, S.scan_done, 2 * c.u)
                    for j in range(4):
                        for k in range(2):
                            col = j * DI + k * 128
                            last = nc.tensor.transpose(psum[0:CH, 5 + col // 512,
                                                            col % 512:col % 512 + 128],
                                                       XT[c.q][:, k, j * CH:(j + 1) * CH], ident[:, :])
                    last.then_inc(S.px_ready, 1)

                def scores(c, b):
                    w = 2 * c.u + b
                    if b == 0:
                        later(pe, S.ms_ready, c.u)
                    else:
                        pe.wait_ge(S.m_ready, w)
                    pe.wait_ge(S.ip_used, 5 * c.u + 5)
                    t0 = b * L
                    nc.tensor.matmul(psum[0:CH, 4, 0:L], BT[c.q][:, t0:t0 + CH], CT[c.q][:, t0:t0 + L],
                                     start=True, stop=True)
                    nc.tensor.matmul(psum[0:CH, 4, L:L + CH], BT[c.q][:, t0 + CH:t0 + L],
                                     CT[c.q][:, t0 + CH:t0 + L], start=True, stop=True)\
                        .then_inc(S.g_ready, 1)

                def decays(c, b):
                    w = 2 * c.u + b
                    if b == 0:
                        pe.wait_ge(S.xd_ready, c.u + 1)
                        pe.wait_ge(S.dec_ready, c.u + 1)
                    else:
                        pe.wait_ge(S.scan_done, w)
                    for h in range(NH):
                        for k in range(2):
                            col = (h % 2) * L + k * CH
                            last = nc.tensor.transpose(psum[0:CH, 5 + h // 2, col:col + CH],
                                                       dec[c.q][:, 2 * b + k, h:h + 1].to_broadcast([CH, CH]),
                                                       ident[0:CH, 0:CH])
                    last.then_inc(S.pb_ready, 1)

                def mix(c, b):
                    w = 2 * c.u + b
                    pe.wait_ge(S.m_ready, w + 1)
                    if b == 0:
                        later(pe, S.po_used, c.u)
                    else:
                        pe.wait_ge(S.t_ready, w)
                    for h in range(NH):
                        p, k = (h % 2) * 64, h // 2
                        o = psum[p:p + 64, 7, k * L:(k + 1) * L]
                        nc.tensor.matmul(o, Xd[:, 2 * b, h * HD:(h + 1) * HD], M0[:, h, :],
                                         start=True, stop=False)
                        last = nc.tensor.matmul(o[:, CH:L], Xd[:, 2 * b + 1, h * HD:(h + 1) * HD],
                                                M1[:, h, :], start=False, stop=True)
                    last.then_inc(S.y_psum, 1)

                def output(c):
                    pe.wait_ge(S.yg_ready, 2 * c.u + 2)
                    for j in range(4):
                        for k in range(2):
                            last = nc.tensor.matmul(psum[0:CH, 7, j * F:(j + 1) * F],
                                                    Yg[:, k, j * CH:(j + 1) * CH], w_out[:, k, :],
                                                    start=(k == 0), stop=(k == 1))
                    last.then_inc(S.po_ready, 1)
                    pe.wait_ge(S.sq_ready, 2 * c.u + 2)
                    pe.wait_ge(S.m_ready, 2 * c.u + 2)
                    for j in range(4):
                        for k in range(2):
                            last = nc.tensor.matmul(psum[0:CH, 4, 480 + j:481 + j],
                                                    Sq[:, k, j * CH:(j + 1) * CH], ones_col[:, :],
                                                    start=(k == 0), stop=(k == 1))
                    last.then_inc(S.pr_ready, 1)

                def body(a, b, c):
                    if c: scores(c, 0)
                    if b: projection(b, 0)
                    if c: decays(c, 0)
                    if b: projection(b, 1)
                    if a: x_transposes(a)
                    if b: projection(b, 2); dt_projection(b)
                    if c: mix(c, 0)
                    if c: scores(c, 1); decays(c, 1)
                    if a: conv(a)
                    if b: projection(b, 3)
                    if c: mix(c, 1)
                    if b: x_rows(b); projection(b, 4)
                    if c: output(c)
                    if a: hn_transposes(a)
                skewed(pe, body, UNITS)

            @block.scalar
            def _(act):
                def x_copy(a):
                    act.wait_ge(S.xT_psum, a.u + 1)
                    later(act, S.conv_done, a.u)
                    nc.scalar.activation(xT, psum[:, 0, :], ACT.Copy).then_inc(S.xT_ready, 1)

                def tanh(a):
                    act.wait_ge(S.conv_scaled, a.u + 1)
                    later(act, S.biased, a.u)
                    nc.scalar.activation(v_t, v_s, ACT.Tanh).then_inc(S.tanh_done, 1)

                def relu(a):
                    act.wait_ge(S.biased, a.u + 1)
                    nc.scalar.activation(Hb[:, ds(4 * F * a.u, 4 * F)], v_b, ACT.Relu).then_inc(S.h_ready, 1)

                def hnT_copy(a):
                    act.wait_ge(S.hnT_psum, a.u + 1)
                    later(act, S.ip_ready, 5 * (a.u - 1))
                    nc.scalar.activation(hnT[a.q][:, :, PADL:],
                                         psum[:, 0, 0:UT].rearrange("p (b t) -> p b t", b=2),
                                         ACT.Copy).then_inc(S.hnT_ready, 1)

                def silu(b, k):
                    act.wait_ge(S.ip_ready, 5 * b.u + k + 1)
                    if k == 0:
                        later(act, S.yg_ready, 2 * (b.u - 1))
                    i = psum[:, bank_of[k], 0:UT]
                    if k < 2:
                        nc.scalar.activation(Z[b.q][:, k, :], i, ACT.Silu).then_inc(S.ip_used, 1)
                    elif k < 4:
                        nc.scalar.activation(XT[b.q][:, k - 2, :], i, ACT.Silu, bias=cb[:, k - 2:k - 1])\
                            .then_inc(S.ip_used, 1)
                    else:
                        nc.scalar.activation(BT[b.q], i[0:64, :], ACT.Silu, bias=cb[0:64, 2:3])
                        nc.scalar.activation(CT[b.q], i[64:128, :], ACT.Silu, bias=cb[64:128, 2:3])\
                            .then_inc(S.ip_used, 1)

                def square(c, b):
                    act.wait_ge(S.yg_ready, 2 * c.u + b + 1)
                    if b == 0:
                        later(act, S.pr_ready, c.u)
                    nc.scalar.activation(Sq[:, :, b * L:(b + 1) * L], Yg[:, :, b * L:(b + 1) * L],
                                         ACT.Square).then_inc(S.sq_ready, 1)

                def body(a, b, c):
                    if b: silu(b, 0); silu(b, 1)
                    if a: x_copy(a)
                    if b: silu(b, 2)
                    if c: square(c, 0)
                    if a: tanh(a); relu(a)
                    if b: silu(b, 3)
                    if c: square(c, 1)
                    if b: silu(b, 4)
                    if a: hnT_copy(a)
                skewed(act, body, UNITS)

            @block.gpsimd
            def _(pool):
                own_begin, own = stepper(pool, S.pool_link)

                def add_bias(a):
                    pool.wait_ge(S.tanh_done, a.u + 1)
                    later(pool, S.h_ready, a.u)
                    nc.gpsimd.tensor_tensor(v_b.rearrange("p (j f) -> p j f", f=F),
                                            v_t.rearrange("p (j f) -> p j f", f=F),
                                            tokb[:, :].unsqueeze(1).broadcast_to([CH, 4, F]),
                                            ALU.add).then_inc(S.biased, 1)

                def exp_of(b):
                    pool.wait_ge(S.nab_ready, b.u + 1)
                    nc.gpsimd.tensor_tensor(ee, euler[0:CH, :], nab, ALU.pow).then_inc(S.exp_ready, 1)

                def decay_of(b, done):
                    own_begin(done)
                    pool.wait_ge(S.dt_ready, b.u + 1)
                    later(pool, S.pb_ready, 2 * (b.u - 1))
                    own(nc.gpsimd.tensor_tensor(dA, dt[b.q], a_neg[:, :, :].rearrange("p j h -> p (j h)"),
                                                ALU.mult))
                    own(nc.gpsimd.tensor_tensor(ee2, euler[0:CH, :], dA,
                                                ALU.pow))
                    nc.gpsimd.tensor_tensor(dec[b.q].rearrange("p j h -> p (j h)"), ee2, keep[:, :],
                                            ALU.mult).then_inc(S.dec_ready, 1)

                def gate(c, b):
                    pool.wait_ge(S.t_ready, 2 * c.u + b + 1)
                    if b == 0:
                        later(pool, S.po_ready, c.u)
                        later(pool, S.sq_ready, 2 * c.u)
                    nc.gpsimd.tensor_tensor(Yg[:, :, b * L:(b + 1) * L], Tg[:, :, b * L:(b + 1) * L],
                                            Z[c.q][:, :, b * L:(b + 1) * L], ALU.mult)\
                        .then_inc(S.yg_ready, 1)

                def rr_of(c):
                    pool.wait_ge(S.ms_ready, c.u + 1)
                    nc.gpsimd.tensor_tensor(rr, ms, minus_half[0:CH, 0:4], ALU.pow).then_inc(S.rr_ready, 1)

                def body(a, b, c):
                    if c: gate(c, 0)
                    if b: exp_of(b)
                    if a: add_bias(a)
                    if c: gate(c, 1)
                    if a:
                        own_begin(a.u + 2 * (b.u if b else 0))
                        pool.wait_ge(S.stats_ready, a.u + 1)
                        own(nc.gpsimd.tensor_tensor(ve, mv[:, :, 1], eps_row[0:CH, 0:4], ALU.add))
                        nc.gpsimd.tensor_tensor(rstd, ve, minus_half[0:CH, 0:4], ALU.pow)\
                            .then_inc(S.rstd_ready, 1)
                    if b: decay_of(b, (a.u + 1 if a else UNITS) + 2 * b.u)
                    if c: rr_of(c)
                skewed(pool, body, UNITS)

            @block.vector
            def _(dve):
                own_begin, own = stepper(dve, S.dve_link)

                def conv_scale(a):
                    dve.wait_ge(S.conv_done, a.u + 1)
                    later(dve, S.tanh_done, a.u)
                    nc.vector.tensor_tensor(v_s.rearrange("p (j f) -> p j f", f=F),
                                            psum[0:CH, 1, :].rearrange("p (j f) -> p j f", f=F),
                                            scale[:, ds(4 * a.u, 4)].unsqueeze(2).broadcast_to([CH, 4, F]),
                                            ALU.mult).then_inc(S.conv_scaled, 1)

                def stats(a):
                    dve.wait_ge(S.h_ready, a.u + 1)
                    later(dve, S.rstd_ready, a.u)
                    for j in range(4):
                        last = nc.vector.bn_stats(st[:, j, :], Hb[:, ds(4 * F * a.u + j * F, F)])
                    own(last)
                    nc.vector.memset(wait_carrier[:, :], 0.0)
                    for j in range(4):
                        last = nc.vector.bn_aggr(mv[:, j, :], st[:, j, :])
                    last.then_inc(S.stats_ready, 1)

                def norm(a):
                    dve.wait_ge(S.rstd_ready, a.u + 1)
                    later(dve, S.hnT_psum, a.u)
                    for j in range(4):
                        last = nc.vector.tensor_scalar(hn[:, j, :], Hb[:, ds(4 * F * a.u + j * F, F)],
                                                       mv[:, j, 0:1], rstd[:, j:j + 1], ALU.subtract,
                                                       ALU.mult)
                    last.then_inc(S.hn_ready, 1)

                def dt_first(b):
                    dve.wait_ge(S.pd_ready, b.u + 1)
                    ins = nc.vector.tensor_tensor(uu.rearrange("p (j h) -> p j h", h=NH),
                                                  psum[0:CH, 3, :].rearrange("p (j n) -> p j n", n=128)[:, :, 124:128],
                                                  dtb[:, :].unsqueeze(1).broadcast_to([CH, 4, NH]), ALU.add)
                    ins.then_inc(S.dtu_ready, 1)
                    dve.wait_ge(S.dtu_ready, b.u + 1)
                    later(dve, S.exp_ready, b.u)
                    nc.vector.scalar_tensor_tensor(nab, uu, -1.0, uu, ALU.mult, ALU.min)\
                        .then_inc(S.nab_ready, 1)

                def dt_rest(b):
                    dve.wait_ge(S.exp_ready, b.u + 1)
                    own(nc.vector.tensor_scalar(qq, ee, 2.0, None, ALU.add))
                    own(nc.vector.reciprocal(rq, qq))
                    own(nc.vector.tensor_tensor(ss, ee, rq, ALU.mult))
                    own(nc.vector.tensor_tensor(s2, ss, ss, ALU.mult))
                    own(nc.vector.tensor_scalar(pa, s2, 1.0 / 15, None, ALU.mult))
                    src, dst = pa, pb
                    for k in (13, 11, 9, 7, 5, 3):
                        own(nc.vector.scalar_tensor_tensor(dst, src, 1.0 / k, s2, ALU.add, ALU.mult))
                        src, dst = dst, src
                    own(nc.vector.scalar_tensor_tensor(tt, src, 1.0, ss, ALU.add, ALU.mult))
                    own(nc.vector.tensor_scalar(qq, uu, 0.0, None, ALU.max))
                    nc.vector.scalar_tensor_tensor(dt[b.q], tt, 2.0, qq, ALU.mult, ALU.add)\
                        .then_inc(S.dt_ready, 1)

                def x_scale(c):
                    dve.wait_ge(S.px_ready, c.u + 1)
                    dve.wait_ge(S.dt_ready, c.u + 1)
                    later(dve, S.y_psum, 2 * c.u)
                    nc.vector.tensor_tensor(Xd.rearrange("p j (h d) -> p (j h) d", d=HD),
                                            psum[0:CH, 5:7, :].rearrange("p k (g d) -> p (k g) d", d=HD),
                                            dt[c.q].unsqueeze(2).broadcast_to([CH, 4 * NH, HD]),
                                            ALU.mult).then_inc(S.xd_ready, 1)

                def scans(c, b):
                    w = 2 * c.u + b
                    dve.wait_ge(S.pb_ready, w + 1)
                    for g in range(2):
                        nc.vector.tensor_tensor_scan(
                            L0.rearrange("p h t -> p (h t)")[:, g * 2 * L:(g + 1) * 2 * L],
                            psum[0:CH, 5 + g, 0:2 * L], diag2.rearrange("p h t -> p (h t)"),
                            0.0, ALU.mult, ALU.add)
                    for h in range(NH):
                        col = (h % 2) * L + CH
                        last = nc.vector.tensor_tensor_scan(L1[:, h, :], psum[0:CH, 5 + h // 2, col:col + CH],
                                                            ident[0:CH, 0:CH], 0.0, ALU.mult, ALU.add)
                    last.then_inc(S.scan_done, 1)

                def decayed_scores(c, b):
                    w = 2 * c.u + b
                    dve.wait_ge(S.scan_done, w + 1)
                    dve.wait_ge(S.g_ready, w + 1)
                    later(dve, S.y_psum, w)
                    nc.vector.tensor_tensor(M0, L0, psum[0:CH, 4, 0:L].unsqueeze(1).broadcast_to([CH, NH, L]),
                                            ALU.mult)
                    nc.vector.tensor_tensor(M1, L1, psum[0:CH, 4, L:L + CH].unsqueeze(1)
                                            .broadcast_to([CH, NH, CH]), ALU.mult).then_inc(S.m_ready, 1)

                def skip_add(c, b):
                    w = 2 * c.u + b
                    dve.wait_ge(S.y_psum, w + 1)
                    if b == 0:
                        later(dve, S.yg_ready, 2 * c.u)
                    for k in range(2):
                        last = nc.vector.scalar_tensor_tensor(
                            Tg[:, k, b * L:(b + 1) * L], XT[c.q][:, k, b * L:(b + 1) * L], d_col[:, k:k + 1],
                            psum[:, 7, k * L:(k + 1) * L], ALU.mult, ALU.add)
                    last.then_inc(S.t_ready, 1)

                def residual(c):
                    dve.wait_ge(S.pr_ready, c.u + 1)
                    nc.vector.tensor_scalar(ms, psum[0:CH, 4, 480:484], 1.0 / DI, EPS, ALU.mult, ALU.add)\
                        .then_inc(S.ms_ready, 1)
                    dve.wait_ge(S.rr_ready, c.u + 1)
                    dve.wait_ge(S.po_ready, c.u + 1)
                    for j in range(4):
                        row = Hb[:, ds(4 * F * c.u + j * F, F)]
                        last = nc.vector.scalar_tensor_tensor(row, psum[0:CH, 7, j * F:(j + 1) * F],
                                                              rr[:, j:j + 1], row, ALU.mult, ALU.add)
                    last.then_inc(S.po_used, 1)

                def new_stats(c):
                    dve.wait_ge(S.po_used, c.u + 1)
                    nc.vector.memset(wait_carrier[:, :], 0.0)
                    for j in range(4):
                        last = nc.vector.bn_stats(st3[:, j, :], Hb[:, ds(4 * F * c.u + j * F, F)])
                    own(last)
                    nc.vector.memset(wait_carrier[:, :], 0.0)
                    for j in range(4):
                        last = nc.vector.bn_aggr(mv3[:, j, :], st3[:, j, :])
                    own(last)
                    nc.vector.tensor_copy(MV[:, ds(4 * c.u, 4), :], mv3[:, :, :])

                def body(a, b, c):
                    if c: scans(c, 0); decayed_scores(c, 0)
                    if b: dt_first(b)
                    if c: skip_add(c, 0)
                    if c: scans(c, 1); decayed_scores(c, 1)
                    if a: conv_scale(a)
                    if b:
                        own_begin((a.u if a else UNITS) + 13 * b.u + 2 * (c.u if c else 0))
                        dt_rest(b)
                    if c: skip_add(c, 1)
                    if a:
                        own_begin(a.u + 13 * (b.u + 1 if b else 0) + 2 * (c.u if c else 0))
                        stats(a)
                    if b: x_scale(b)
                    if a: norm(a)
                    if c:
                        residual(c)
                        own_begin((a.u + 1 if a else UNITS) + 13 * (b.u + 1 if b else UNITS) + 2 * c.u)
                        new_stats(c)
                skewed(dve, body, UNITS)

        names = ("var_ready r1_ready t_ready r2_ready xnr_ready xnr_used xT_psum hhT_ready hhT_copied "
                 "lg_psum lg_ready dve_own based")
        B = namedtuple("B", names)(*[sem("b_" + n) for n in names.split()])
        with nc.Block() as block:
            @block.gpsimd
            def _(pool):
                pool.wait_ge(B.var_ready, 1)
                nc.gpsimd.tensor_tensor(v64[1], v64[0], minus_half[0:CH, :], ALU.pow).then_inc(B.r1_ready, 1)
                pool.wait_ge(B.t_ready, 1)
                nc.gpsimd.tensor_tensor(v64[3], v64[2], minus_half[0:CH, :], ALU.pow).then_inc(B.r2_ready, 1)

            @block.vector
            def _(dve):
                mean, var = MV[:, :, 0], MV[:, :, 1]
                nc.vector.tensor_scalar(v64[0], var, EPS, None, ALU.add).then_inc(B.var_ready, 1)
                dve.wait_ge(B.r1_ready, 1)
                link(dve, dve_step, nc.vector.tensor_tensor(v64[2], var, v64[1], ALU.mult))
                link(dve, dve_step, nc.vector.tensor_tensor(v64[2], v64[2], v64[1], ALU.mult))
                nc.vector.tensor_scalar(v64[2], v64[2], EPS, None, ALU.add).then_inc(B.t_ready, 1)
                nc.vector.tensor_scalar(r1p, v64[1], 1.0, None, ALU.add)
                nc.vector.scalar_tensor_tensor(nmr, mean, -1.0, v64[1], ALU.mult, ALU.mult)
                dve.wait_ge(B.r2_ready, 1)
                link(dve, dve_step, nc.vector.tensor_tensor(r12, v64[1], v64[3], ALU.mult))

                def normed(a):
                    later(dve, B.xnr_used, a.u - 1)
                    later(dve, B.xT_psum, a.u - 1)
                    for j in range(4):
                        last = nc.vector.tensor_scalar(xnr[a.q][:, j, :], Hb[:, ds(4 * F * a.u + j * F, F)],
                                                       MV[:, ds(4 * a.u + j, 1), 0], r12[:, ds(4 * a.u + j, 1)],
                                                       ALU.subtract, ALU.mult)
                    last.then_inc(B.xnr_ready, 1)

                def affine(b):
                    dve.wait_ge(B.xT_psum, b.u + 1)
                    later(dve, B.hhT_copied, b.u - 1)
                    later(dve, B.lg_psum, b.u - 1)
                    nc.vector.tensor_scalar(hhT[b.q], psum[:, b.q, 0:UT], lng[:, 0:1], lnb[:, 0:1], ALU.mult,
                                            ALU.add).then_inc(B.hhT_ready, 1)

                def logits(c):
                    dve.wait_ge(B.lg_psum, c.u + 1)
                    nc.vector.tensor_tensor(LG[:, ds(4 * E * c.u, 4 * E)].rearrange("p (j e) -> p j e", e=E),
                                            psum[0:CH, 2 + c.q, 0:4 * E].rearrange("p (j e) -> p j e", e=E),
                                            rb[:, :].unsqueeze(1).broadcast_to([CH, 4, E]),
                                            ALU.add).then_inc(B.lg_ready, 1)

                def body(a, b, c):
                    if a: normed(a)
                    if b: affine(b)
                    if c: logits(c)
                skewed(dve, body, UNITS)

            @block.scalar
            def _(act):
                def body(a, b, c):
                    if a:
                        act.wait_ge(B.xnr_ready, a.u + 1)
                        nc.scalar.activation(XNR[:, ds(4 * F * a.u, 4 * F)],
                                             xnr[a.q].rearrange("p j f -> p (j f)"), ACT.Copy)\
                            .then_inc(B.xnr_used, 1)
                        for j in range(4):
                            h = Hb[:, ds(4 * F * a.u + j * F, F)]
                            nc.scalar.activation(h, h, ACT.Identity, scale=r1p[:, ds(4 * a.u + j, 1)],
                                                 bias=nmr[:, ds(4 * a.u + j, 1)])
                    if b:
                        act.wait_ge(B.hhT_ready, b.u + 1)
                        nc.scalar.activation(HHT[:, ds(512 * b.u, UT)], hhT[b.q], ACT.Copy)\
                            .then_inc(B.hhT_copied, 1)
                skewed(act, body, UNITS)

            @block.tensor
            def _(pe):
                def body(a, b, c):
                    if b:
                        pe.wait_ge(B.xnr_ready, b.u + 1)
                        later(pe, B.hhT_ready, b.u - 1)
                        for j in range(4):
                            last = nc.tensor.transpose(psum[:, b.q, j * CH:(j + 1) * CH], xnr[b.q][:, j, :],
                                                       ident[0:CH, 0:CH])
                        last.then_inc(B.xT_psum, 1)
                    if c:
                        pe.wait_ge(B.hhT_ready, c.u + 1)
                        later(pe, B.lg_ready, c.u - 1)
                        for j in range(4):
                            last = nc.tensor.matmul(psum[0:CH, 2 + c.q, j * E:(j + 1) * E],
                                                    hhT[c.q][:, j * CH:(j + 1) * CH], rw[:, :],
                                                    start=True, stop=True)
                        last.then_inc(B.lg_psum, 1)
                skewed(pe, body, UNITS)

        names = ("diff_ready exp_ready mask_ready ranks_ready pool_own lg2_ready")
        R = namedtuple("R", names)(*[sem("r_" + n) for n in names.split()])
        with nc.Block() as block:
            ge = lambda v: v.rearrange("p (g e) -> p g e", e=E)
            Dg, Ex, Key, Oh1, Lg2, Oh2, Wk, TE, CUM = [ge(v[0:CH, :]) for v in big]
            TEe = big[7].rearrange("p (e g) -> p e g", g=NCH)
            CUMe = big[8].rearrange("p (e g) -> p e g", g=NCH)
            LGg = ge(LG)
            over_e = lambda v: v.unsqueeze(2).broadcast_to([CH, NCH, E])
            each_g = lambda v: v.unsqueeze(1).broadcast_to([CH, NCH, E])
            m1, k1, m2, rs, e1, e2 = row

            @block.scalar
            def _(act):
                act.wait_ge(R.diff_ready, 1)
                nc.scalar.activation(Ex, Dg, ACT.Exp, scale=1.0 / TEMP).then_inc(R.exp_ready, 1)

            @block.tensor
            def _(pe):
                pe.wait_ge(R.mask_ready, 1)
                for k in range(2):
                    nc.tensor.matmul(psum[0:CH, k, :], tri[:, :], mask[:, k * 512:(k + 1) * 512],
                                     start=True, stop=True)
                    last = nc.tensor.matmul(psum[:, 2 + k, :], ones_sq[:, :], mask[:, k * 512:(k + 1) * 512],
                                            start=True, stop=True)
                last.then_inc(R.ranks_ready, 1)

            @block.vector
            def _(dve):
                def step(ins):
                    link(dve, dve_step, ins)

                V = nc.vector
                step(V.tensor_reduce(m1, LGg, AX.X, ALU.max))
                V.tensor_tensor(Dg, LGg, over_e(m1), ALU.subtract).then_inc(R.diff_ready, 1)
                step(V.tensor_tensor(Key, LGg, over_e(m1), ALU.is_equal))
                step(V.tensor_tensor(Key, Key, each_g(rev_iota[0:CH, :]), ALU.mult))
                step(V.tensor_reduce(k1, Key, AX.X, ALU.max))
                step(V.tensor_tensor(Oh1, each_g(rev_iota[0:CH, :]), over_e(k1), ALU.is_equal))
                step(V.scalar_tensor_tensor(Lg2, Oh1, -3.0e38, LGg, ALU.mult, ALU.add))
                step(V.tensor_reduce(m2, Lg2, AX.X, ALU.max))
                step(V.tensor_tensor(Key, Lg2, over_e(m2), ALU.is_equal))
                step(V.tensor_tensor(Key, Key, each_g(rev_iota[0:CH, :]), ALU.mult))
                step(V.tensor_reduce(k1, Key, AX.X, ALU.max))
                step(V.tensor_tensor(Oh2, each_g(rev_iota[0:CH, :]), over_e(k1), ALU.is_equal))
                V.tensor_tensor(ge(mask), Oh1, Oh2, ALU.add).then_inc(R.mask_ready, 1)
                dve.wait_ge(R.exp_ready, 1)
                step(V.tensor_reduce(rs, Ex, AX.X, ALU.add))
                step(V.reciprocal(rs, rs))
                step(V.tensor_tensor(Wk, Oh1, Ex, ALU.mult))
                step(V.tensor_reduce(e1, Wk, AX.X, ALU.add))
                step(V.tensor_tensor(VAL[:, 0, :], e1, rs, ALU.mult))
                step(V.tensor_tensor(Wk, Oh2, Ex, ALU.mult))
                step(V.tensor_reduce(e2, Wk, AX.X, ALU.add))
                step(V.tensor_tensor(VAL[:, 1, :], e2, rs, ALU.mult))
                step(V.tensor_tensor(Wk, Oh1, over_e(VAL[:, 0, :]), ALU.mult))
                step(V.tensor_tensor(Key, Oh2, over_e(VAL[:, 1, :]), ALU.mult))
                V.tensor_tensor(COMB[:, :].rearrange("p (g e) -> p g e", e=CB)[:, :, 0:E], Wk, Key, ALU.add)
                dve.wait_ge(R.ranks_ready, 1)
                step(V.tensor_copy(TEe, psum[:, 2:4, :].rearrange("p k (g e) -> p e (k g)", e=E)))
                step(V.tensor_tensor_scan(big[8], big[7], big[7], 0.0, ALU.add, ALU.max))
                prev, cnt, blocks, t0, t1, base = sml[0:6]
                ends = CUMe[:, :, NCH - 1]
                step(V.memset(prev, 0.0))
                step(V.tensor_copy(prev[:, 1:E], ends[:, 0:E - 1]))
                step(V.tensor_tensor(cnt, ends, prev, ALU.subtract))
                step(V.tensor_scalar(t0, cnt, (BLK - 1) / 2.0, 1.0 / BLK, ALU.add, ALU.mult))
                step(V.tensor_scalar(t1, t0, 8388608.0, None, ALU.add))
                step(V.tensor_scalar(blocks, t1, -8388608.0, None, ALU.add))
                step(V.tensor_tensor_scan(cumP[:, :], blocks, blocks, 0.0, ALU.add, ALU.max))
                step(V.tensor_tensor(t0, cumP[:, :], blocks, ALU.subtract))
                step(V.scalar_tensor_tensor(base, t0, float(BLK), prev, ALU.mult, ALU.subtract))
                step(V.tensor_tensor(CUMe, CUMe, TEe, ALU.subtract))
                step(V.tensor_tensor(CUMe, CUMe, base.unsqueeze(2).broadcast_to([128, E, NCH]), ALU.add))
                step(V.tensor_tensor(Lg2, psum[0:CH, 0:2, :].rearrange("p k (g e) -> p (k g) e", e=E),
                                     CUMe[0:CH].rearrange("p e g -> p g e"), ALU.add))
                step(V.tensor_tensor(Wk, Oh1, Lg2, ALU.mult))
                step(V.tensor_reduce(m1, Wk, AX.X, ALU.add))
                V.tensor_copy(IDX[0:CH, :, 0], m1)
                step(V.tensor_tensor(Key, Oh2, Lg2, ALU.mult))
                step(V.tensor_reduce(m2, Key, AX.X, ALU.add))
                V.tensor_copy(IDX[0:CH, :, 1], m2)
                blkE = arena[0:1, staging_at:staging_at + NBLK * E].rearrange("p (j e) -> p j e", e=E)
                blkN = sml_blocks
                step(V.tensor_tensor(blkE, cumP[0:1, :].unsqueeze(1).broadcast_to([1, NBLK, E]),
                                     block_no[:, :].unsqueeze(2).broadcast_to([1, NBLK, E]), ALU.is_le))
                step(V.tensor_reduce(blkN, blkE, AX.X, ALU.add))
                step(V.tensor_scalar(blkN, blkN, float(E - 1), float(EW), ALU.min, ALU.mult))
                V.tensor_copy(EOFF[:, :], blkN)

        names = ("st_ready0 st_ready1 scat0 scat1 wload up_psum up_used comb_ready comb_psum combT_ready "
                 "down_psum moe_ready ids_ready")
        C = namedtuple("C", names)(*[sem("c_" + n) for n in names.split()])
        scattered = (C.scat0, C.scat1)
        staged = (C.st_ready0, C.st_ready1)
        with nc.Block() as block:
            @block.sync
            def _(sp):
                sp.dma_start(w1.rearrange("p (e h) -> p e h", e=E)[:, :, 0:DH],
                             ew1.rearrange("e d h -> d e h")).then_inc(C.wload, 16)
                for e in range(E):
                    sp.dma_start(w2[:, e * EW:e * EW + DH].rearrange("p (c d) -> p c d", d=F),
                                 ew2[e].rearrange("(c p) d -> p c d", p=128)).then_inc(C.wload, 16)
                sp.wait_ge(C.wload, 16 * (E + 1))

            @block.gpsimd
            def _(pool):
                assert 2 * NCH <= F
                nc.gpsimd.tensor_copy(w1.rearrange("p (e h) -> p e h", e=E)[:, :, DH:EW],
                                      b_e1[:, :].rearrange("p (e k) -> p e k", e=E))
                nc.gpsimd.iota(row_ids[:, 0:2 * NCH], pattern=[[1, 2 * NCH]], base=0,
                               channel_multiplier=2 * NCH).then_inc(C.ids_ready, 1)
                for q in range(2):
                    nc.gpsimd.memset(x_st[q].rearrange("p j k f -> p (j k f)"), 0.0)\
                        .then_inc(staged[q], 1)

                last_slot = pool.to_reg(SLOTS - 1)

                def scatter(u):
                    pool.wait_ge(staged[u.q], u.n + 2)
                    pool.sem_inc(pool_turns)
                    for j in range(4):
                        for k in range(2):
                            nc.gpsimd.indirect_dma_start(
                                out=x_slots, out_offset=bass.IndirectOffsetOnAxis(
                                    ap=idx_st[u.q][:, 2 * j + k:2 * j + k + 1], axis=0),
                                in_=x_st[u.q][:, j, k, :], in_offset=None,
                                bounds_check=last_slot, oob_is_err=False).then_inc(scattered[u.q], 16)
                streamed(pool, scatter, UNITS)
                for q in range(2):
                    pool.wait_ge(scattered[q], 16 * 8 * (UNITS // 2))

            @block.scalar
            def _(act):
                def stage(u):
                    if not isinstance(u.n, int) or u.n > 0:
                        act.wait_ge(scattered[u.q], 128 * u.n)
                    if isinstance(u.n, int) and u.n == 0:
                        act.wait_ge(staged[u.q], 1)
                        act.wait_ge(C.ids_ready, 1)
                    nc.scalar.activation(idx_st[u.q][:, :], IDX[:, ds(4 * u.u, 4), :]
                                         .rearrange("p j k -> p (j k)"), ACT.Copy)
                    nc.scalar.activation(x_st[u.q][0:CH, :, :, F].rearrange("p j k -> p (j k)"),
                                         row_ids[:, ds(8 * u.u, 8)], ACT.Copy)
                    for k in range(2):
                        last = nc.scalar.activation(x_st[u.q][0:CH, :, k, 0:F],
                                                    XNR[:, ds(4 * F * u.u, 4 * F)]
                                                    .rearrange("p (j f) -> p j f", f=F), ACT.Copy)
                    last.then_inc(staged[u.q], 1)

                def body(a, b, c):
                    if a: stage(a)
                    if b:
                        act.wait_ge(C.up_psum, b.u + 1)
                        later(act, C.down_psum, b.u)
                        for k in range(2):
                            last = nc.scalar.activation(SH[:, k, :], psum[:, k, 0:UT], ACT.Silu,
                                                        bias=b_s1[:, k:k + 1])
                        last.then_inc(C.up_used, 1)
                skewed(act, body, UNITS)

            @block.tensor
            def _(pe):
                def body(a, b, c):
                    if b:
                        later(pe, C.up_used, b.u)
                        for k in range(2):
                            last = nc.tensor.matmul(psum[:, k, 0:UT], w_s1[:, k * 128:(k + 1) * 128],
                                                    HHT[:, ds(512 * b.u, UT)], start=True, stop=True)
                        last.then_inc(C.up_psum, 1)
                        pe.wait_ge(C.comb_ready, b.u + 1)
                        later(pe, C.combT_ready, b.u)
                        for j in range(4):
                            last = nc.tensor.transpose(psum[0:CB, 2, j * CH:(j + 1) * CH], comb_st[:, j, :],
                                                       ident[0:CH, 0:CH])
                        last.then_inc(C.comb_psum, 1)
                        pe.wait_ge(C.up_used, b.u + 1)
                        pe.wait_ge(C.combT_ready, b.u + 1)
                        later(pe, C.moe_ready, b.u)
                        for j in range(4):
                            o = psum[0:CH, 3, j * F:(j + 1) * F]
                            t = slice(j * CH, (j + 1) * CH)
                            for k in range(2):
                                nc.tensor.matmul(o, SH[:, k, t], w_s2[:, k, :], start=(k == 0), stop=False)
                            last = nc.tensor.matmul(o, combT[:, t], w_e2b[:, :], start=False, stop=True)
                        last.then_inc(C.down_psum, 1)
                skewed(pe, body, UNITS)

            @block.vector
            def _(dve):
                def body(a, b, c):
                    if b:
                        later(dve, C.comb_psum, b.u)
                        nc.vector.tensor_copy(comb_st.rearrange("p j e -> p (j e)"),
                                              COMB[:, ds(4 * CB * b.u, 4 * CB)]).then_inc(C.comb_ready, 1)
                        dve.wait_ge(C.comb_psum, b.u + 1)
                        later(dve, C.down_psum, b.u)
                        nc.vector.tensor_copy(combT, psum[0:CB, 2, 0:UT]).then_inc(C.combT_ready, 1)
                    if c:
                        dve.wait_ge(C.down_psum, c.u + 1)
                        nc.vector.tensor_copy(MOE[:, ds(512 * c.u, 512)], psum[0:CH, 3, :])\
                            .then_inc(C.moe_ready, 1)
                skewed(dve, body, UNITS)

        names = ("xb0 xb1 xb2 xb3 xT_psum hT_ready w1_ready up_psum eh_ready down_psum yo_ready "
                 "row_ready yst0 yst1 yst2 yst3")
        X = namedtuple("X", names)(*[sem("x_" + n) for n in names.split()])
        x_here = (X.xb0, X.xb1, X.xb2, X.xb3)
        y_stored = (X.yst0, X.yst1, X.yst2, X.yst3)
        with nc.Block() as block:
            @block.sync
            def _(sp):
                def load(t):
                    later(sp, X.xT_psum, t.u - 3)
                    later(sp, X.row_ready, t.u - 3)
                    sp.dma_start(xb[t.q], x_slots[ds(BLK * t.u, BLK), :]).then_inc(x_here[t.q], 16)
                streamed(sp, load, NBLK, 4)

            @block.tensor
            def _(pe):
                def body(a, b, c):
                    if b:
                        pe.wait_ge(X.w1_ready, b.u + 1)
                        pe.wait_ge(X.hT_ready, b.u + 1)
                        later(pe, X.eh_ready, b.u - 1)
                        for k in range(NF):
                            last = nc.tensor.matmul(psum[:, 2 + b.q % 2, k * 128:(k + 1) * 128],
                                                    w1_blk[b.q][:, k * 128:(k + 1) * 128], hT[b.q % 2],
                                                    start=True, stop=True)
                        last.then_inc(X.up_psum, 1)
                    if a:
                        pe.wait_ge(x_here[a.q], 16 * (a.n + 1))
                        later(pe, X.hT_ready, a.u - 1)
                        nc.tensor.transpose(psum[:, a.q % 2, 0:BLK], xb[a.q][:, 0:F], ident[:, :])\
                            .then_inc(X.xT_psum, 1)
                    if c:
                        at = pe.value_load(EOFF[0:1, ds(c.u, 1)], min_val=0, max_val=(E - 1) * EW)
                        pe.wait_ge(X.eh_ready, c.u + 1)
                        later(pe, X.yo_ready, c.u - 1)
                        for k in range(NF):
                            last = nc.tensor.matmul(psum[:, 4 + c.q % 2, 0:F],
                                                    EHT[c.q % 2][:, k * 128:(k + 1) * 128],
                                                    w2[:, ds(at + k * F, F)], start=(k == 0),
                                                    stop=(k == NF - 1))
                        last.then_inc(X.down_psum, 1)
                skewed(pe, body, NBLK, 4)

            @block.scalar
            def _(act):
                def body(a, b, c):
                    if b:
                        act.wait_ge(X.up_psum, b.u + 1)
                        later(act, X.down_psum, b.u - 1)
                        for k in range(NF):
                            last = nc.scalar.activation(EHT[b.q % 2][:, k * 128:(k + 1) * 128],
                                                        psum[:, 2 + b.q % 2, k * 128:(k + 1) * 128],
                                                        ACT.Silu, bias=w1_blk[b.q][:, DH + k:DH + k + 1])
                        last.then_inc(X.eh_ready, 1)
                    if c:
                        act.wait_ge(X.down_psum, c.u + 1)
                        later(act, y_stored[c.q], 16 * c.n)
                        nc.scalar.activation(YO[c.q], psum[:, 4 + c.q % 2, 0:F], ACT.Copy)\
                            .then_inc(X.yo_ready, 1)
                skewed(act, body, NBLK, 4)

            @block.gpsimd
            def _(pool):
                last_row = pool.to_reg(CH * 2 * NCH - 1)

                def scatter(t):
                    pool.wait_ge(X.row_ready, t.u + 1)
                    pool.sem_inc(pool_turns)
                    pool.wait_ge(X.yo_ready, t.u + 1)
                    pool.sem_inc(pool_turns)
                    nc.gpsimd.indirect_dma_start(
                        out=y_tokens, out_offset=bass.IndirectOffsetOnAxis(ap=y_row[t.q], axis=0),
                        in_=YO[t.q], in_offset=None, bounds_check=last_row, oob_is_err=False)\
                        .then_inc(y_stored[t.q], 16)
                streamed(pool, scatter, NBLK, 4)
                for q in range(4):
                    pool.wait_ge(y_stored[q], 16 * (NBLK // 4))

            @block.vector
            def _(dve):
                def prepare(t):
                    at = dve.value_load(EOFF[0:1, ds(t.u, 1)], min_val=0, max_val=(E - 1) * EW)
                    later(dve, X.eh_ready, t.u - 3)
                    nc.vector.tensor_copy(w1_blk[t.q], w1[:, ds(at, EW)]).then_inc(X.w1_ready, 1)
                    dve.wait_ge(X.xT_psum, t.u + 1)
                    later(dve, X.up_psum, t.u - 1)
                    nc.vector.tensor_scalar(hT[t.q % 2], psum[:, t.q % 2, 0:BLK], lng[:, 0:1],
                                            lnb[:, 0:1], ALU.mult, ALU.add).then_inc(X.hT_ready, 1)
                    later(dve, y_stored[t.q], 16 * t.n)
                    nc.vector.tensor_copy(y_row[t.q], xb[t.q][:, F:F + 1]).then_inc(X.row_ready, 1)
                streamed(dve, prepare, NBLK, 4)

        names = ("y0 y1 h_ready mixed ve_ready rs_ready fh_ready fhT_psum fhT_ready "
                 "up_psum up_used down_psum rest_ready out_ready st0 st1 own dve_own")
        D = namedtuple("D", names)(*[sem("d_" + n) for n in names.split()])
        y_here = (D.y0, D.y1)
        stored = (D.st0, D.st1)
        with nc.Block() as block:
            outv = out.rearrange("(g p) f -> p g f", p=CH)

            @block.sync
            def _(sp):
                yv = y_tokens.rearrange("(p r) f -> p r f", p=CH)

                def load(u):
                    later(sp, D.mixed, u.u - 1)
                    for p0, p1 in ((0, 112), (112, CH)):
                        sp.dma_start(GY[u.q][p0:p1, :, :], yv[p0:p1, ds(8 * u.u, 8), :])\
                          .then_inc(y_here[u.q], 16)

                def store(u):
                    sp.wait_ge(D.out_ready, u.u + 1)
                    for p0, p1 in ((0, 112), (112, CH)):
                        sp.dma_start(outv[p0:p1, ds(4 * u.u, 4), :],
                                     outb[u.q][p0:p1, :].rearrange("p (j f) -> p j f", f=F))\
                          .then_inc(stored[u.q], 16)

                ahead(sp, load, store, UNITS, 3)
                for q in range(2):
                    sp.wait_ge(stored[q], 32 * (UNITS // 2))

            @block.gpsimd
            def _(pool):
                own_begin, own = stepper(pool, D.own)

                def body(a, b, c):
                    if a:
                        pool.wait_ge(D.ve_ready, a.u + 1)
                        nc.gpsimd.tensor_tensor(rs3[:, :], ve3[:, :], minus_half[0:CH, 0:4], ALU.pow)\
                            .then_inc(D.rs_ready, 1)
                    if b:
                        pool.wait_ge(D.mixed, b.u + 1)
                        pool.wait_ge(D.h_ready, b.u + 1)
                        later(pool, D.out_ready, b.u)
                        own_begin(b.u)
                        own(nc.gpsimd.tensor_tensor(rest2, h_st, mo[b.q].rearrange("p j f -> p (j f)"), ALU.add))
                        nc.gpsimd.tensor_tensor(rest.rearrange("p (j f) -> p j f", f=F),
                                                rest2.rearrange("p (j f) -> p j f", f=F),
                                                b_f2[:, :].unsqueeze(1).broadcast_to([CH, 4, F]), ALU.add)\
                            .then_inc(D.rest_ready, 1)
                skewed(pool, body, UNITS)

            @block.vector
            def _(dve):
                step_begin, step = stepper(dve, D.dve_own)

                def mixture(a):
                    dve.wait_ge(y_here[a.q], 32 * (a.n + 1))
                    later(dve, D.rest_ready, a.u - 1)
                    for j in range(4):
                        last = nc.vector.scalar_tensor_tensor(
                            mo[a.q][:, j, :], GY[a.q][:, 2 * j, :], VAL[:, 0, ds(4 * a.u + j, 1)],
                            MOE[:, ds(512 * a.u + j * F, F)], ALU.mult, ALU.add)
                    step(last)
                    for j in range(4):
                        last = nc.vector.scalar_tensor_tensor(
                            mo[a.q][:, j, :], GY[a.q][:, 2 * j + 1, :], VAL[:, 1, ds(4 * a.u + j, 1)],
                            mo[a.q][:, j, :], ALU.mult, ALU.add)
                    last.then_inc(D.mixed, 1)
                    dve.wait_ge(D.mixed, a.u + 1)
                    nc.vector.memset(wait_carrier[:, :], 0.0)
                    for j in range(4):
                        last = nc.vector.bn_stats(st3[:, j, :], mo[a.q][:, j, :])
                    step(last)
                    nc.vector.memset(wait_carrier[:, :], 0.0)
                    for j in range(4):
                        last = nc.vector.bn_aggr(mv3[:, j, :], st3[:, j, :])
                    step(last)
                    nc.vector.tensor_scalar(ve3[:, :], mv3[:, :, 1], EPS, None, ALU.add).then_inc(D.ve_ready, 1)

                def norm(a):
                    dve.wait_ge(D.rs_ready, a.u + 1)
                    later(dve, D.fhT_psum, a.u)
                    for j in range(4):
                        last = nc.vector.tensor_scalar(fh[:, j, :], mo[a.q][:, j, :], mv3[:, j, 0:1],
                                                       rs3[:, j:j + 1], ALU.subtract, ALU.mult)
                    last.then_inc(D.fh_ready, 1)

                def affine(b):
                    dve.wait_ge(D.fhT_psum, b.u + 1)
                    later(dve, D.up_psum, 4 * b.u)
                    nc.vector.tensor_scalar(fhT, psum[:, 0, 0:UT], fg[:, 0:1], fbb[:, 0:1], ALU.mult,
                                            ALU.add).then_inc(D.fhT_ready, 1)

                def final(c):
                    dve.wait_ge(D.down_psum, c.u + 1)
                    dve.wait_ge(D.rest_ready, c.u + 1)
                    later(dve, stored[c.q], 32 * c.n)
                    nc.vector.tensor_tensor(outb[c.q], psum[0:CH, 5, :], rest, ALU.add)\
                        .then_inc(D.out_ready, 1)

                def body(a, b, c):
                    if b: affine(b)
                    if a:
                        step_begin(3 * a.u)
                        mixture(a)
                        norm(a)
                    if c: final(c)
                skewed(dve, body, UNITS)

            @block.tensor
            def _(pe):
                def body(a, b, c):
                    if b:
                        pe.wait_ge(D.fh_ready, b.u + 1)
                        later(pe, D.fhT_ready, b.u)
                        for j in range(4):
                            last = nc.tensor.transpose(psum[:, 0, j * CH:(j + 1) * CH], fh[:, j, :],
                                                       ident[0:CH, 0:CH])
                        last.then_inc(D.fhT_psum, 1)
                    if c:
                        pe.wait_ge(D.up_used, 4 * c.u + 4)
                        later(pe, D.out_ready, c.u)
                        for j in range(4):
                            for k in range(NF):
                                last = nc.tensor.matmul(psum[0:CH, 5, j * F:(j + 1) * F],
                                                        FH[:, k, j * CH:(j + 1) * CH], w_f2[:, k, :],
                                                        start=(k == 0), stop=(k == NF - 1))
                        last.then_inc(D.down_psum, 1)
                    if b:
                        pe.wait_ge(D.fhT_ready, b.u + 1)
                        for k in range(NF):
                            nc.tensor.matmul(psum[:, 1 + k, 0:UT], w_f1[:, k * 128:(k + 1) * 128], fhT,
                                             start=True, stop=True).then_inc(D.up_psum, 1)
                skewed(pe, body, UNITS)

            @block.scalar
            def _(act):
                def body(a, b, c):
                    if b:
                        later(act, D.rest_ready, b.u)
                        nc.scalar.activation(h_st, Hb[:, ds(4 * F * b.u, 4 * F)], ACT.Copy)\
                            .then_inc(D.h_ready, 1)
                        for k in range(NF):
                            act.wait_ge(D.up_psum, 4 * b.u + k + 1)
                            if k == 0:
                                later(act, D.down_psum, b.u)
                            nc.scalar.activation(FH[:, k, :], psum[:, 1 + k, 0:UT], ACT.Silu,
                                                 bias=b_f1[:, k:k + 1]).then_inc(D.up_used, 1)
                skewed(act, body, UNITS)


def kernel(**inputs):
    import numpy as np
    import concourse.bacc as bacc
    from concourse.bass_utils import run_bass_kernel_spmd

    w = {k: np.asarray(v) for k, v in inputs.items()}
    x = w["x"].reshape(32 * 256, 64)

    def cols(v, n):
        return v.reshape(n, 128).T

    arrays = {
        "x2": np.concatenate([x, np.concatenate([x[1:], x[:1]], axis=0)], axis=1),
        "tok_kernel": w["L0_tok_kernel"], "tok_bias": w["L0_tok_bias"],
        "in_proj": w["L0_attn_in_proj_w"], "conv_w": w["L0_attn_conv_w"].reshape(384 * 4),
        "conv_b": cols(w["L0_attn_conv_b"], 3), "dt_bias": w["L0_attn_dt_bias"],
        "A_log": w["L0_attn_A_log"], "D_skip": w["L0_attn_D_skip"],
        "norm_w": cols(w["L0_attn_norm_w"], 2), "out_proj": w["L0_attn_out_proj_w"],
        "ln_g": cols(w["L0_ffn_ln_in_g"], 1), "ln_b": cols(w["L0_ffn_ln_in_b"], 1),
        "router_w": w["L0_ffn_router_w"], "router_b": w["L0_ffn_router_b"],
        "ew1": w["L0_ffn_ew1"], "eb1": cols(w["L0_ffn_eb1"], 64), "ew2": w["L0_ffn_ew2"], "eb2": w["L0_ffn_eb2"],
        "sw1": w["L0_ffn_sw1"], "sb1": cols(w["L0_ffn_sb1"], 2), "sw2": w["L0_ffn_sw2"],
        "sb2": w["L0_ffn_sb2"], "ffg": cols(w["L0_ffn_ff_ln_g"], 1), "ffb": cols(w["L0_ffn_ff_ln_b"], 1),
        "fw1": w["L0_ffn_ff_w1"], "fb1": cols(w["L0_ffn_ff_b1"], 4), "fw2": w["L0_ffn_ff_w2"],
        "fb2": w["L0_ffn_ff_b2"],
    }
    arrays = {"in_" + k: np.ascontiguousarray(v) for k, v in arrays.items()}
    nc = bacc.Bacc("TRN2", target_bir_lowering=False, num_devices=1)
    fp32 = mybir.dt.float32
    args = [nc.dram_tensor(k, v.shape, fp32, kind="ExternalInput").ap() for k, v in arrays.items()]
    out = nc.dram_tensor("out_tokens", (32 * 248, 128), fp32, kind="ExternalOutput").ap()
    audio_tower(nc, *args, out)
    r = run_bass_kernel_spmd(nc, [arrays], core_ids=[0])
    return r.results[0]["out_tokens"].reshape(32, 248, 128)
```

```python
import concourse.bass as bass
from concourse import mybir
from collections import namedtuple
from contextlib import ExitStack

Unit = namedtuple("Unit", "u n q")


def skewed(eng, body, units, turns=2):
    def unit(i, c):
        return Unit(turns * i + c, i + c // turns, c % turns)

    body(unit(0, 0), None, None)
    body(unit(0, 1), unit(0, 0), None)
    for c in range(turns):
        body(unit(0, c + 2), unit(0, c + 1), unit(0, c))
    rounds = (units - 2) // turns
    with eng.Fori(1, rounds) as i:
        for c in range(turns):
            body(unit(i, c + 2), unit(i, c + 1), unit(i, c))
    for c in range(rounds * turns, units - 2):
        body(unit(0, c + 2), unit(0, c + 1), unit(0, c))
    body(None, unit(0, units - 1), unit(0, units - 2))
    body(None, None, unit(0, units - 1))


def streamed(eng, step, units, turns=2):
    def unit(i, c):
        return Unit(turns * i + c, i + c // turns, c % turns)

    for c in range(turns):
        step(unit(0, c))
    with eng.Fori(1, units // turns) as i:
        for c in range(turns):
            step(unit(i, c))
    for c in range(units // turns * turns, units):
        step(unit(0, c))


def ahead(eng, front, back, units, lead, turns=2):
    def unit(i, c):
        return Unit(turns * i + c, i + c // turns, c % turns)

    def both(i, c):
        back(unit(i, c))
        front(unit(i, c + lead))

    for c in range(lead):
        front(unit(0, c))
    steps = units - lead
    for c in range(turns):
        both(0, c)
    with eng.Fori(1, steps // turns) as i:
        for c in range(turns):
            both(i, c)
    for c in range(steps // turns * turns, steps):
        both(0, c)
    for c in range(steps, units):
        back(unit(0, c))


def later(eng, counter, value):
    if not isinstance(value, int) or value > 0:
        eng.wait_ge(counter, value)


def audio_tower(nc, x2, tok_kernel, tok_bias, in_proj, conv_w, conv_b, dt_bias, A_log, D_skip, norm_w,
                out_proj, ln_g, ln_b, router_w, router_b, ew1, eb1, ew2, eb2, sw1, sb1, sw2, sb2,
                ffg, ffb, fw1, fb1, fw2, fb2, out):
    fp32 = mybir.dt.float32
    bf16 = mybir.dt.bfloat16
    i32 = mybir.dt.int32
    ALU = mybir.AluOpType
    ACT = mybir.ActivationFunctionType
    AX = mybir.AxisListType
    ds = bass.ds

    SEQS, LIN, CIN, TAPS = 32, 256, 64, 9
    L = LIN - TAPS + 1
    F = 128
    CH = L // 2
    UNITS = SEQS // 2
    NCH = 2 * SEQS
    UT = 2 * L
    NH, HD, NS = 4, 64, 64
    DI = NH * HD
    KC = 4
    PADL = KC - 1
    E, DH, DSH = 16, 512, 256
    NF = DH // 128
    TEMP = 0.7
    EPS = 1e-5
    TOK_EPS = 1e-7
    LAM = 1.0 / (1.0 + TOK_EPS)
    T = SEQS * L
    BLK = 128
    NBLK = (2 * T) // BLK + E
    NBLK += NBLK % 2
    SLOTS = NBLK * BLK
    CB = E + 1
    NO_ROW = float(1 << 20)
    EXP1 = 2.718281828459045

    x_slots = nc.dram_tensor("x_slots", (SLOTS, F + 1), fp32, kind="Internal").ap()
    y_tokens = nc.dram_tensor("y_tokens", (CH * 2 * NCH, F), fp32, kind="Internal").ap()

    ctx = ExitStack()
    with ctx:
        def sb(name, shape, dt=fp32):
            return ctx.enter_context(nc.sbuf_tensor(name, shape, dt))

        def sem(name):
            return ctx.enter_context(nc.semaphore(name))

        ident = sb("ident", [128, 128])
        ones_col = sb("ones_col", [128, 1])
        minus_half = sb("minus_half", [128, 64])
        euler = sb("euler", [128, 16])
        eps_row = sb("eps_row", [128, 4])
        keep = sb("keep", [CH, 4 * NH])
        wait_carrier = sb("wait_carrier", [1, 1])
        tokb = sb("tokb", [CH, F])
        row_ids = tokb[:, :].bitcast(i32)
        cb = sb("cb", [128, 3])
        dtb = sb("dtb", [CH, NH])
        a_log = sb("a_log", [CH, NH])
        a_neg = sb("a_neg", [CH, 4, NH])
        d_col = sb("d_col", [128, 2])
        nw = sb("nw", [128, 2])
        scale = sb("scale", [CH, NCH])
        lng = sb("lng", [128, 1])
        lnb = sb("lnb", [128, 1])
        rw = sb("rw", [128, 128])
        rb = sb("rb", [CH, E])
        w_s1 = sb("w_s1", [128, DSH])
        b_s1 = sb("b_s1", [128, 2])
        w_s2 = sb("w_s2", [128, 2, F])
        w_e2b = sb("w_e2b", [CB, F])
        fg = sb("fg", [128, 1])
        fbb = sb("fbb", [128, 1])
        w_f1 = sb("w_f1", [128, DH])
        b_f1 = sb("b_f1", [128, NF])
        w_f2 = sb("w_f2", [128, NF, F])
        b_e1 = sb("b_e1", [128, E * NF])
        tri = sb("tri", [CH, CH], bf16)
        ones_sq = sb("ones_sq", [CH, 128], bf16)

        MV = sb("MV", [CH, NCH, 2])
        COMB = sb("COMB", [CH, NCH * CB])
        VAL = sb("VAL", [CH, 2, NCH])
        IDX = sb("IDX", [128, NCH, 2], i32)
        idx_st = [sb(f"idx_st{q}", [128, 8], i32) for q in range(4)]
        EOFF = sb("EOFF", [1, NBLK], i32)
        cumP = sb("cumP", [128, E])
        block_no = sb("block_no", [1, NBLK])
        rev_iota = sb("rev_iota", [128, E])
        st3 = sb("st3", [CH, 4, 6])
        mv3 = sb("mv3", [CH, 4, 2])
        ve3 = sb("ve3", [CH, 4])
        rs3 = sb("rs3", [CH, 4])
        b_f2 = sb("b_f2", [CH, F])
        Hb = sb("Hb", [CH, NCH * F])

        ARENA = 38800
        arena_at = nc.sbuf_base
        arena = sb("arena", [128, ARENA])

        pos = [0]

        def take(parts, *shape):
            n = 1
            for k in shape:
                n *= k
            v = arena[0:parts, pos[0]:pos[0] + n]
            pos[0] += n
            assert pos[0] <= ARENA, pos[0]
            if len(shape) == 2:
                v = v.rearrange("p (a b) -> p a b", b=shape[1])
            if len(shape) == 3:
                v = v.rearrange("p (a b c) -> p a b c", b=shape[1], c=shape[2])
            return v

        def take_pair(name, shape):
            n = 1
            for k in shape[1:]:
                n *= k
            pair = []
            for part in ("hi", "lo"):
                pos[0] += pos[0] % 8 and 8 - pos[0] % 8
                pair.append(nc.alloc_sbuf_tensor_at(f"{name}_{part}", shape, mybir.dt.float32r,
                                                    offset=arena_at + 4 * pos[0]))
                pos[0] += n
                assert pos[0] <= ARENA, pos[0]
            return pair

        pos[0] = 0
        weights_at = 14800
        x_all = take(128, 2 * SEQS, CIN)
        x_sq = take(128, 2 * SEQS, CIN)
        sq = take(128, 2 * SEQS)
        wsq = take(CH, NCH)
        wnorm = take(CH, NCH)
        small = take(CH, NCH)
        wmix = take(CH, NCH)
        band = take(128, 4, CH)
        cw = take(128, 384 * KC)
        iota_i = take(128, E).bitcast(i32)
        iota_b = take(1, NBLK).bitcast(i32)
        assert pos[0] <= weights_at
        pos[0] = 0
        xin = [take(128, 4, 128) for _ in range(2)]
        v_s = take(CH, 4 * F)
        v_t = take(CH, 4 * F)
        v_b = take(CH, 4 * F)
        hn = take(CH, 4, F)
        Z = [take(128, 2, UT) for _ in range(2)]
        XT = [take(128, 2, UT) for _ in range(2)]
        BT = [take(64, UT) for _ in range(2)]
        CT = [take(64, UT) for _ in range(2)]
        dt = [take(CH, 4 * NH) for _ in range(2)]
        dec = [take(CH, 4, NH) for _ in range(2)]
        Xd = take(CH, 4, DI)
        L0 = take(CH, NH, L)
        L1 = take(CH, NH, CH)
        M0 = take(CH, NH, L)
        M1 = take(CH, NH, CH)
        Tg = take(128, 2, UT)
        Yg = take(128, 2, UT)
        Sq = take(128, 2, UT)
        st = take(CH, 4, 6)
        mv = take(CH, 4, 2)
        ve = take(CH, 4)
        rstd = take(CH, 4)
        ms = take(CH, 4)
        rr = take(CH, 4)
        uu = take(CH, 16)
        nab = take(CH, 16)
        ee = take(CH, 16)
        qq = take(CH, 16)
        rq = take(CH, 16)
        ss = take(CH, 16)
        s2 = take(CH, 16)
        pa = take(CH, 16)
        pb = take(CH, 16)
        tt = take(CH, 16)
        dA = take(CH, 16)
        ee2 = take(CH, 16)
        pos[0] = max(pos[0], weights_at)
        diag2 = take(CH, 2, L)
        tokw = take(128, 5, F)
        w_in = take(F, 644)
        w_tap = take(F, KC, 384)
        w_out = take(128, 2, F)
        xT = take(128, 4 * 128)
        w_in2 = take_pair("w_in", [F, 644])
        w_tap2 = take_pair("w_tap", [F, KC, 384])
        hnT2 = [take_pair(f"hnT{q}", [128, 2, L + PADL]) for q in range(2)]
        zero_src = take(128, 10, F + 1)
        pos[0] = 0
        XNR = take(CH, NCH * F)
        HHT = take(128, UNITS * 512)
        MOE = HHT[0:CH, :]
        after_phase_a = pos[0]
        EW = DH + NF
        w1 = take(128, E * EW)
        w2 = take(128, E * EW)
        staging_at = pos[0]
        pos[0] = after_phase_a
        LG = take(CH, NCH * E)
        r12 = take(CH, NCH)
        v64 = [take(CH, NCH) for _ in range(4)]
        xnr = [take(CH, 4, F) for _ in range(2)]
        hhT = [take(128, UT) for _ in range(2)]
        big_at = pos[0]
        big = [take(128, NCH * E) for _ in range(9)]
        sml = [take(128, E) for _ in range(8)]
        row = [take(CH, NCH) for _ in range(6)]
        mask = take(CH, NCH * E // 2).bitcast(bf16)
        sml_blocks = take(1, NBLK)
        assert pos[0] <= staging_at
        pos[0] = staging_at
        x_st = [take(128, 4, 2, F + 1) for _ in range(4)]
        comb_st = take(CH, 4, CB)
        combT = take(CB, UT)
        SH = take(128, 2, UT)
        r1p = take(CH, NCH)
        nmr = take(CH, NCH)
        pos[0] = 0
        xb = [take(128, F + 1) for _ in range(4)]
        y_row = [take(128, 1).bitcast(i32) for _ in range(4)]
        hT = [take(128, F) for _ in range(2)]
        w1_blk = [take(128, EW) for _ in range(4)]
        EHT = [take(128, DH) for _ in range(2)]
        YO = [take(128, F) for _ in range(4)]
        assert pos[0] <= NCH * F
        pos[0] = 0
        GY = [take(CH, 8, F) for _ in range(2)]
        mo = [take(CH, 4, F) for _ in range(2)]
        fh = take(CH, 4, F)
        fhT = take(128, UT)
        FH = take(128, NF, UT)
        rest = [take(CH, 4 * F) for _ in range(2)]
        h_st = take(CH, 4 * F)
        pos[0] = staging_at
        outb = [take(CH, 4 * F) for _ in range(2)]
        rest2 = take(CH, 4 * F)

        psum = ctx.enter_context(nc.psum_tensor("psum", [128, 8, 512], fp32))

        chain_count = {}

        def link(eng, counter, ins):
            chain_count[counter.name] = chain_count.get(counter.name, 0) + 1
            ins.then_inc(counter, 1)
            eng.wait_ge(counter, chain_count[counter.name])

        XPARTS = 4
        ld_x = [sem(f"ld_x{n}") for n in range(XPARTS)]
        ld_tok = sem("ld_tok")
        ld_ssm = sem("ld_ssm")
        ld_ffn = sem("ld_ffn")
        zeros_ready = sem("zeros_ready")
        slots_zeroed = sem("slots_zeroed")
        pool_step = sem("pool_step")
        dve_step = sem("dve_step")
        pool_turns = sem("pool_turns")
        bands_ready = sem("bands_ready")
        squares_ready = sem("squares_ready")
        row_squares_ready = sem("row_squares_ready")
        windows_ready = sem("windows_ready")
        wsq_ready = sem("wsq_ready")
        wnorm_ready = sem("wnorm_ready")
        folded = sem("folded")
        hi_ready = sem("hi_ready")
        a_ready = sem("a_ready")

        splits = [(w_in, [v[:, :] for v in w_in2]), (w_tap, [v[:, :, :] for v in w_tap2])]

        def rows(v, parts):
            return v.rearrange("(a n) -> a n", a=1).partition_broadcast(parts) if len(v.shape) == 1 else v

        with nc.Block() as block:
            @block.sync
            def _(sp):
                for n in range(XPARTS):
                    g = slice(n * NCH // XPARTS, (n + 1) * NCH // XPARTS)
                    sp.dma_start(x_all[:, g, :], x2[:, 0:CIN].rearrange("(n p) c -> p n c", p=128)[:, g, :])\
                        .then_inc(ld_x[n], 16)
                kw = tok_kernel.rearrange("k c f -> c k f")
                sp.dma_start(tokw[0:64, 0:5, :], kw[:, 0:TAPS:2, :]).then_inc(ld_tok, 16)
                sp.dma_start(tokw[64:128, 0:4, :], kw[:, 1:TAPS:2, :]).then_inc(ld_tok, 16)
                sp.dma_start(tokb[:, :], rows(tok_bias, CH)).then_inc(ld_tok, 16)
                for dst, src in ((w_in, in_proj), (cw, rows(conv_w, 128)), (cb[:, :], conv_b),
                                 (dtb[:, :], rows(dt_bias, CH)), (a_log[:, :], rows(A_log, CH)),
                                 (d_col[0:64, :], rows(D_skip[0:4:2], 64)),
                                 (d_col[64:128, :], rows(D_skip[1:4:2], 64)), (nw[:, :], norm_w),
                                 (w_out, out_proj.rearrange("(c p) f -> p c f", p=128))):
                    with nc.allow_non_contiguous_dma(reason="small vectors"):
                        sp.dma_start(dst, src).then_inc(ld_ssm, 16)

            @block.gpsimd
            def _(pool):
                nc.gpsimd.memset(zero_src[:, :, 0:F], 0.0).then_inc(zeros_ready, 1)
                nc.gpsimd.memset(zero_src[:, :, F:F + 1], NO_ROW).then_inc(zeros_ready, 1)
                nc.gpsimd.memset(minus_half[:, :], -0.5)
                nc.gpsimd.memset(rw[:, :], 0.0).then_inc(zeros_ready, 1)
                nc.gpsimd.memset(euler[:, :], EXP1)
                nc.gpsimd.memset(eps_row[:, :], EPS)
                nc.gpsimd.memset(ones_col[:, :], 1.0)
                nc.gpsimd.memset(IDX[:, :, :], 1 << 20)
                nc.gpsimd.memset(COMB[:, :], 0.25)
                nc.gpsimd.memset(ones_sq[:, :], 1.0)
                nc.gpsimd.memset(band, 1.0)
                nc.gpsimd.memset(ident[:, :], 0.0)
                nc.gpsimd.memset(diag2, 0.0)
                nc.gpsimd.memset(tri[:, :], 0.0)
                link(pool, pool_step, nc.gpsimd.iota(iota_i, pattern=[[-1, E]], base=E, channel_multiplier=0))
                nc.gpsimd.tensor_copy(rev_iota[:, :], iota_i)
                link(pool, pool_step, nc.gpsimd.iota(iota_b, pattern=[[1, NBLK]], base=0,
                                                     channel_multiplier=0))
                nc.gpsimd.tensor_copy(block_no[:, :], iota_b)
                for j in range(2):
                    for c in range(2):
                        v = band[:, 2 * j + c, :]
                        nc.gpsimd.affine_select(out=v, in_=v, compare_op=ALU.is_ge, fill=0.0,
                                                base=128 * j - CH * c, pattern=[[-1, CH]],
                                                channel_multiplier=1)
                link(pool, pool_step, nc.gpsimd.affine_select(
                    out=ident[:, :], in_=ident[:, :], compare_op=ALU.not_equal, fill=1.0, base=0,
                    pattern=[[-1, 128]], channel_multiplier=1))
                for j in range(2):
                    for c in range(2):
                        v = band[:, 2 * j + c, :]
                        last = nc.gpsimd.affine_select(out=v, in_=v, compare_op=ALU.is_ge, fill=0.0,
                                                       base=TAPS - 1 - 128 * j + CH * c,
                                                       pattern=[[1, CH]], channel_multiplier=-1)
                last.then_inc(bands_ready, 1)
                nc.gpsimd.affine_select(out=diag2[:, :, 0:CH], in_=diag2[:, :, 0:CH],
                                        compare_op=ALU.not_equal, fill=1.0, base=0,
                                        pattern=[[0, 2], [-1, CH]], channel_multiplier=1)
                nc.gpsimd.affine_select(out=tri[:, :], in_=tri[:, :], compare_op=ALU.is_ge, fill=1.0,
                                        base=0, pattern=[[-1, CH]], channel_multiplier=1)
                pool.wait_ge(ld_ssm, 16 * 9)
                link(pool, pool_step, nc.gpsimd.tensor_tensor(a_neg[:, 0, :], euler[0:CH, 0:NH], a_log[:, :],
                                                              ALU.pow))
                for j in range(3, -1, -1):
                    last = nc.gpsimd.tensor_scalar(a_neg[:, j, :], a_neg[:, 0, :], -1.0, 0.0,
                                                   ALU.mult, ALU.add)
                last.then_inc(a_ready, 1)

            @block.scalar
            def _(act):
                for n in range(XPARTS):
                    g = slice(n * NCH // XPARTS, (n + 1) * NCH // XPARTS)
                    act.wait_ge(ld_x[n], 16)
                    nc.scalar.activation(x_sq[:, g, :], x_all[:, g, :], ACT.Square).then_inc(squares_ready, 1)
                act.wait_ge(wsq_ready, 1)
                nc.scalar.activation(wnorm, wsq, ACT.Sqrt).then_inc(wnorm_ready, 1)
                act.wait_ge(ld_ssm, 16 * 9)
                act.wait_ge(folded, 1)
                for full, (hi, lo) in splits:
                    nc.scalar.activation(hi, full, ACT.Copy).then_inc(hi_ready, 1)

            @block.tensor
            def _(pe):
                pe.wait_ge(row_squares_ready, 1)
                pe.wait_ge(bands_ready, 1)
                pe.wait_ge(ld_tok, 48)
                sqv = sq.rearrange("p (b j) -> p j b", j=2)
                for c in range(2):
                    for j in range(2):
                        last = nc.tensor.matmul(psum[0:CH, 0, c * SEQS:(c + 1) * SEQS],
                                                band[:, 2 * j + c, :], sqv[:, j, :],
                                                start=(j == 0), stop=(j == 1))
                last.then_inc(windows_ready, 1)

            @block.vector
            def _(dve):
                nc.vector.memset(keep[:, :], 1.0)
                link(dve, dve_step, nc.vector.memset(wait_carrier[:, :], 0.0))
                nc.vector.memset(keep[0:1, :].rearrange("p (b c h) -> p b c h", b=2, c=2)[:, :, 0, :], 0.0)
                for q in range(2):
                    for part in hnT2[q]:
                        nc.vector.memset(part[:, :, 0:PADL].bitcast(fp32), 0.0)
                for n in range(XPARTS):
                    g = slice(n * NCH // XPARTS, (n + 1) * NCH // XPARTS)
                    dve.wait_ge(squares_ready, n + 1)
                    last = nc.vector.tensor_reduce(sq[:, g], x_sq[:, g, :], AX.X, ALU.add)
                last.then_inc(row_squares_ready, 1)
                dve.wait_ge(ld_ssm, 16 * 9)
                cwv = cw.rearrange("p (c k) -> p k c", k=KC)
                for k in range(KC):
                    last = nc.vector.tensor_tensor(w_tap[:, k, :], w_in[:, DI:DI + 384], cwv[:, k, :],
                                                   ALU.mult)
                last.then_inc(folded, 1)
                for c in range(2):
                    nc.vector.tensor_scalar(w_out[:, c, :], w_out[:, c, :], nw[:, c:c + 1], None, ALU.mult)
                dve.wait_ge(windows_ready, 1)
                nc.vector.tensor_scalar(wsq.rearrange("p (b c) -> p c b", c=2),
                                        psum[0:CH, 0, 0:NCH].rearrange("p (c b) -> p c b", c=2),
                                        0.0, None, ALU.max).then_inc(wsq_ready, 1)
                dve.wait_ge(wnorm_ready, 1)
                nc.vector.tensor_scalar(wmix, wnorm, 1.0, None, ALU.is_lt)
                link(dve, dve_step, nc.vector.tensor_scalar(small, wnorm, TOK_EPS, None, ALU.add))
                link(dve, dve_step, nc.vector.reciprocal(wsq, small))
                link(dve, dve_step, nc.vector.tensor_scalar(small, wmix, -1.0, 1.0, ALU.mult, ALU.add))
                link(dve, dve_step, nc.vector.tensor_tensor(wsq, wsq, small, ALU.mult))
                link(dve, dve_step, nc.vector.tensor_tensor(wsq, wsq, wmix, ALU.add))
                link(dve, dve_step, nc.vector.tensor_scalar(scale[:, :], wsq, LAM, None, ALU.mult))
                for n, (full, (hi, lo)) in enumerate(splits):
                    dve.wait_ge(hi_ready, n + 1)
                    nc.vector.tensor_tensor(lo, full, hi.bitcast(fp32), ALU.subtract)

        names = ("x_in0 x_in1 xT_psum hn_hi_ready xT_ready conv_done conv_scaled tanh_done biased h_ready "
                 "stats_ready rstd_ready hn_ready hnT_psum hnT_ready pd_ready dtu_ready ip_ready ip_used "
                 "nab_ready exp_ready dt_ready dec_ready px_ready xd_ready g_ready pb_ready scan_done "
                 "m_ready y_psum t_ready yg_ready sq_ready sq_summed po_ready pr_ready ms_ready rr_ready "
                 "po_used dve_link pool_link")
        s = {n: sem("a_" + n) for n in names.split()}
        S = namedtuple("S", s)(**s)
        x_in = (S.x_in0, S.x_in1)

        def stepper(eng, counter):
            at = [0]

            def begin(done):
                at[0] = done

            def step(ins):
                at[0] = at[0] + 1
                ins.then_inc(counter, 1)
                eng.wait_ge(counter, at[0])
            return begin, step

        chunks = (("z", 0, 3, 0), ("x", 0, 2, -2), ("x", 1, 2, 2), ("z", 1, 3, 1), ("bc", 2, 3, 4))

        with nc.Block() as block:
            x2t = x2.rearrange("(n p) c -> p n c", p=128)

            @block.sync
            def _(sp):
                def load(u):
                    later(sp, S.xT_psum, u.u - 1)
                    sp.dma_start(xin[u.q], x2t[:, ds(4 * u.u, 4), :]).then_inc(x_in[u.q], 16)

                zr = x_slots.rearrange("(n p) f -> p n f", p=128)
                fills = NBLK // 10

                def load_and_fill(u):
                    load(u)
                    sp.dma_start(zr[:, ds(10 * u.u, 10), :], zero_src).then_inc(slots_zeroed, 16)
                sp.wait_ge(zeros_ready, 3)
                streamed(sp, load_and_fill, fills)
                for u in range(fills, UNITS):
                    load(Unit(u, u // 2, u % 2))
                for dst, src in ((lng[:, :], ln_g), (lnb[:, :], ln_b), (rw[:, 0:E], router_w),
                                 (rb[:, :], rows(router_b, CH)), (w_s1[:, :], sw1), (b_s1[:, :], sb1),
                                 (w_s2[:, :, :], sw2.rearrange("(c p) f -> p c f", p=128)),
                                 (w_e2b[0:E, :], eb2), (w_e2b[E:CB, :], rows(sb2, 1)), (fg[:, :], ffg),
                                 (fbb[:, :], ffb), (w_f1[:, :], fw1), (b_f1[:, :], fb1),
                                 (w_f2[:, :, :], fw2.rearrange("(c p) f -> p c f", p=128)),
                                 (b_f2[:, :], rows(fb2, CH)), (b_e1[:, :], eb1)):
                    with nc.allow_non_contiguous_dma(reason="small vectors"):
                        sp.dma_start(dst, src).then_inc(ld_ffn, 16)
                sp.wait_ge(ld_ffn, 16 * 16)
                sp.wait_ge(slots_zeroed, 16 * fills)

            @block.tensor
            def _(pe):
                def product(o, stationary, moving, start, stop):
                    nc.tensor.matmul(o, stationary[0], moving[0], start=start, stop=False)
                    nc.tensor.matmul(o, stationary[0], moving[1], start=False, stop=False)
                    return nc.tensor.matmul(o, stationary[1], moving[0], start=False, stop=stop)

                def x_transposes(a):
                    pe.wait_ge(x_in[a.q], 16 * (a.n + 1))
                    later(pe, S.hnT_ready, a.u)
                    for j in range(4):
                        last = nc.tensor.transpose(psum[:, 0, j * 128:(j + 1) * 128], xin[a.q][:, j, :],
                                                   ident[:, :])
                    last.then_inc(S.xT_psum, 1)

                def conv(a):
                    pe.wait_ge(S.xT_ready, a.u + 1)
                    later(pe, S.dtu_ready, a.u)
                    for j in range(4):
                        t0 = LIN * (j // 2) + CH * (j % 2)
                        for k in range(5):
                            p = 128 if k < 4 else 64
                            last = nc.tensor.matmul(psum[0:CH, 1, j * F:(j + 1) * F],
                                                    xT[0:p, t0 + 2 * k:t0 + 2 * k + CH], tokw[0:p, k, :],
                                                    start=(k == 0), stop=(k == 4))
                    last.then_inc(S.conv_done, 1)

                def hn_transposes(a):
                    pe.wait_ge(S.hn_ready, a.u + 1)
                    for j in range(4):
                        last = nc.tensor.transpose(psum[:, 0, j * CH:(j + 1) * CH], hn[:, j, :],
                                                   ident[0:CH, 0:CH])
                    last.then_inc(S.hnT_psum, 1)

                def dt_projection(b):
                    pe.wait_ge(S.hnT_ready, b.u + 1)
                    pe.wait_ge(S.conv_scaled, b.u + 1)
                    for j in range(4):
                        t0 = PADL + CH * (j % 2)
                        last = product(psum[0:CH, 1, 128 * j:128 * j + 128],
                                       [v[:, j // 2, t0:t0 + CH] for v in hnT2[b.q]],
                                       [v[:, 516:644] for v in w_in2], True, True)
                    last.then_inc(S.pd_ready, 1)

                def projection(b, k):
                    what, part, bank, used = chunks[k]
                    later(pe, S.ip_used, 5 * b.u + used)
                    o = psum[:, bank, 0:UT]
                    if what == "z":
                        last = product(o, [v[:, part * 128:(part + 1) * 128] for v in w_in2],
                                       [v[:, :, PADL:] for v in hnT2[b.q]], True, True)
                    else:
                        for w in range(KC):
                            last = product(o, [v[:, w, part * 128:(part + 1) * 128] for v in w_tap2],
                                           [v[:, :, w:w + L] for v in hnT2[b.q]], w == 0, w == KC - 1)
                    last.then_inc(S.ip_ready, 1)

                def x_rows(c):
                    pe.wait_ge(S.ip_used, 5 * c.u + 3)
                    later(pe, S.scan_done, 2 * c.u)
                    for j in range(4):
                        for k in range(2):
                            col = j * DI + k * 128
                            last = nc.tensor.transpose(psum[0:CH, 5 + col // 512,
                                                            col % 512:col % 512 + 128],
                                                       XT[c.q][:, k, j * CH:(j + 1) * CH], ident[:, :])
                    last.then_inc(S.px_ready, 1)

                def scores(c, b):
                    w = 2 * c.u + b
                    if b == 0:
                        later(pe, S.ms_ready, c.u)
                    else:
                        pe.wait_ge(S.m_ready, w)
                    pe.wait_ge(S.ip_used, 5 * c.u + 5)
                    t0 = b * L
                    nc.tensor.matmul(psum[0:CH, 4, 0:L], BT[c.q][:, t0:t0 + CH], CT[c.q][:, t0:t0 + L],
                                     start=True, stop=True)
                    nc.tensor.matmul(psum[0:CH, 4, L:L + CH], BT[c.q][:, t0 + CH:t0 + L],
                                     CT[c.q][:, t0 + CH:t0 + L], start=True, stop=True)\
                        .then_inc(S.g_ready, 1)

                def decays(c, b):
                    w = 2 * c.u + b
                    if b == 0:
                        pe.wait_ge(S.xd_ready, c.u + 1)
                        pe.wait_ge(S.dec_ready, c.u + 1)
                    else:
                        pe.wait_ge(S.scan_done, w)
                    for h in range(NH):
                        for k in range(2):
                            col = (h % 2) * L + k * CH
                            last = nc.tensor.transpose(psum[0:CH, 5 + h // 2, col:col + CH],
                                                       dec[c.q][:, 2 * b + k, h:h + 1].to_broadcast([CH, CH]),
                                                       ident[0:CH, 0:CH])
                    last.then_inc(S.pb_ready, 1)

                def mix(c, b):
                    w = 2 * c.u + b
                    pe.wait_ge(S.m_ready, w + 1)
                    if b == 0:
                        later(pe, S.po_used, c.u)
                    else:
                        pe.wait_ge(S.t_ready, w)
                    for h in range(NH):
                        p, k = (h % 2) * 64, h // 2
                        o = psum[p:p + 64, 7, k * L:(k + 1) * L]
                        nc.tensor.matmul(o, Xd[:, 2 * b, h * HD:(h + 1) * HD], M0[:, h, :],
                                         start=True, stop=False)
                        last = nc.tensor.matmul(o[:, CH:L], Xd[:, 2 * b + 1, h * HD:(h + 1) * HD],
                                                M1[:, h, :], start=False, stop=True)
                    last.then_inc(S.y_psum, 1)

                def output(c):
                    pe.wait_ge(S.yg_ready, 2 * c.u + 2)
                    for j in range(4):
                        for k in range(2):
                            last = nc.tensor.matmul(psum[0:CH, 7, j * F:(j + 1) * F],
                                                    Yg[:, k, j * CH:(j + 1) * CH], w_out[:, k, :],
                                                    start=(k == 0), stop=(k == 1))
                    last.then_inc(S.po_ready, 1)
                    pe.wait_ge(S.sq_summed, c.u + 1)
                    pe.wait_ge(S.m_ready, 2 * c.u + 2)
                    for j in range(4):
                        last = nc.tensor.matmul(psum[0:CH, 4, 480 + j:481 + j],
                                                Sq[:, 0, j * CH:(j + 1) * CH], ones_col[:, :],
                                                start=True, stop=True)
                    last.then_inc(S.pr_ready, 1)

                def body(a, b, c):
                    if c: scores(c, 0); decays(c, 0)
                    if b: dt_projection(b); projection(b, 0)
                    if a: x_transposes(a)
                    if b: projection(b, 1)
                    if a: conv(a)
                    if c: mix(c, 0); scores(c, 1); decays(c, 1)
                    if b: projection(b, 2); projection(b, 3); x_rows(b)
                    if c: mix(c, 1)
                    if b: projection(b, 4)
                    if c: output(c)
                    if a: hn_transposes(a)
                skewed(pe, body, UNITS)

            @block.scalar
            def _(act):
                def x_copy(a):
                    act.wait_ge(S.xT_psum, a.u + 1)
                    later(act, S.conv_done, a.u)
                    nc.scalar.activation(xT, psum[:, 0, :], ACT.Copy).then_inc(S.xT_ready, 1)

                def tanh(a):
                    act.wait_ge(S.conv_scaled, a.u + 1)
                    later(act, S.biased, a.u)
                    nc.scalar.activation(v_t, v_s, ACT.Tanh).then_inc(S.tanh_done, 1)

                def relu(a):
                    act.wait_ge(S.biased, a.u + 1)
                    nc.scalar.activation(Hb[:, ds(4 * F * a.u, 4 * F)], v_b, ACT.Relu).then_inc(S.h_ready, 1)

                def hnT_copy(a):
                    act.wait_ge(S.hnT_psum, a.u + 1)
                    later(act, S.ip_ready, 5 * (a.u - 1))
                    nc.scalar.activation(hnT2[a.q][0][:, :, PADL:],
                                         psum[:, 0, 0:UT].rearrange("p (b t) -> p b t", b=2),
                                         ACT.Copy).then_inc(S.hn_hi_ready, 1)

                def silu(b, k):
                    act.wait_ge(S.ip_ready, 5 * b.u + k + 1)
                    if k == 0:
                        later(act, S.yg_ready, 2 * (b.u - 1))
                    what, part, bank, _ = chunks[k]
                    i = psum[:, bank, 0:UT]
                    if what == "z":
                        nc.scalar.activation(Z[b.q][:, part, :], i, ACT.Silu).then_inc(S.ip_used, 1)
                    elif what == "x":
                        nc.scalar.activation(XT[b.q][:, part, :], i, ACT.Silu, bias=cb[:, part:part + 1])\
                            .then_inc(S.ip_used, 1)
                    else:
                        nc.scalar.activation(BT[b.q], i[0:64, :], ACT.Silu, bias=cb[0:64, 2:3])
                        nc.scalar.activation(CT[b.q], i[64:128, :], ACT.Silu, bias=cb[64:128, 2:3])\
                            .then_inc(S.ip_used, 1)

                def square(c, b):
                    act.wait_ge(S.yg_ready, 2 * c.u + b + 1)
                    if b == 0:
                        later(act, S.pr_ready, c.u)
                    nc.scalar.activation(Sq[:, :, b * L:(b + 1) * L], Yg[:, :, b * L:(b + 1) * L],
                                         ACT.Square).then_inc(S.sq_ready, 1)

                def body(a, b, c):
                    if b: silu(b, 0)
                    if a: x_copy(a)
                    if b: silu(b, 1)
                    if a: tanh(a); relu(a)
                    if b: silu(b, 2)
                    if c: square(c, 0)
                    if b: silu(b, 3)
                    if c: square(c, 1)
                    if b: silu(b, 4)
                    if a: hnT_copy(a)
                skewed(act, body, UNITS)

            @block.gpsimd
            def _(pool):
                own_begin, own = stepper(pool, S.pool_link)

                def add_bias(a):
                    pool.wait_ge(S.tanh_done, a.u + 1)
                    later(pool, S.h_ready, a.u)
                    nc.gpsimd.tensor_tensor(v_b.rearrange("p (j f) -> p j f", f=F),
                                            v_t.rearrange("p (j f) -> p j f", f=F),
                                            tokb[:, :].unsqueeze(1).broadcast_to([CH, 4, F]),
                                            ALU.add).then_inc(S.biased, 1)

                def exp_of(b):
                    pool.wait_ge(S.nab_ready, b.u + 1)
                    nc.gpsimd.tensor_tensor(ee, euler[0:CH, :], nab, ALU.pow).then_inc(S.exp_ready, 1)

                def rstd_of(a, done):
                    own_begin(done)
                    pool.wait_ge(S.stats_ready, a.u + 1)
                    own(nc.gpsimd.tensor_tensor(ve, mv[:, :, 1], eps_row[0:CH, 0:4], ALU.add))
                    nc.gpsimd.tensor_tensor(rstd, ve, minus_half[0:CH, 0:4], ALU.pow)\
                        .then_inc(S.rstd_ready, 1)

                def decay_of(b, done):
                    own_begin(done)
                    pool.wait_ge(S.dt_ready, b.u + 1)
                    later(pool, S.pb_ready, 2 * (b.u - 1))
                    own(nc.gpsimd.tensor_tensor(dA, dt[b.q], a_neg[:, :, :].rearrange("p j h -> p (j h)"),
                                                ALU.mult))
                    own(nc.gpsimd.tensor_tensor(ee2, euler[0:CH, :], dA,
                                                ALU.pow))
                    nc.gpsimd.tensor_tensor(dec[b.q].rearrange("p j h -> p (j h)"), ee2, keep[:, :],
                                            ALU.mult).then_inc(S.dec_ready, 1)

                def gate(c, b):
                    pool.wait_ge(S.t_ready, 2 * c.u + b + 1)
                    if b == 0:
                        later(pool, S.po_ready, c.u)
                        later(pool, S.sq_ready, 2 * c.u)
                    nc.gpsimd.tensor_tensor(Yg[:, :, b * L:(b + 1) * L], Tg[:, :, b * L:(b + 1) * L],
                                            Z[c.q][:, :, b * L:(b + 1) * L], ALU.mult)\
                        .then_inc(S.yg_ready, 1)

                def rr_of(c):
                    pool.wait_ge(S.ms_ready, c.u + 1)
                    nc.gpsimd.tensor_tensor(rr, ms, minus_half[0:CH, 0:4], ALU.pow).then_inc(S.rr_ready, 1)

                def body(a, b, c):
                    if b: exp_of(b)
                    if a: add_bias(a)
                    if c: gate(c, 0)
                    if b: decay_of(b, (a.u if a else UNITS) + 2 * b.u)
                    if a: rstd_of(a, a.u + 2 * (b.u + 1 if b else 0))
                    if c: gate(c, 1); rr_of(c)
                skewed(pool, body, UNITS)

            @block.vector
            def _(dve):
                own_begin, own = stepper(dve, S.dve_link)

                def hn_rest(a):
                    dve.wait_ge(S.hn_hi_ready, a.u + 1)
                    nc.vector.tensor_tensor(hnT2[a.q][1][:, :, PADL:],
                                            psum[:, 0, 0:UT].rearrange("p (b t) -> p b t", b=2),
                                            hnT2[a.q][0][:, :, PADL:].bitcast(fp32),
                                            ALU.subtract).then_inc(S.hnT_ready, 1)

                def conv_scale(a):
                    dve.wait_ge(S.conv_done, a.u + 1)
                    later(dve, S.tanh_done, a.u)
                    nc.vector.tensor_tensor(v_s.rearrange("p (j f) -> p j f", f=F),
                                            psum[0:CH, 1, :].rearrange("p (j f) -> p j f", f=F),
                                            scale[:, ds(4 * a.u, 4)].unsqueeze(2).broadcast_to([CH, 4, F]),
                                            ALU.mult).then_inc(S.conv_scaled, 1)

                def stats(a):
                    dve.wait_ge(S.h_ready, a.u + 1)
                    later(dve, S.rstd_ready, a.u)
                    for j in range(4):
                        last = nc.vector.bn_stats(st[:, j, :], Hb[:, ds(4 * F * a.u + j * F, F)])
                    own(last)
                    nc.vector.memset(wait_carrier[:, :], 0.0)
                    for j in range(4):
                        last = nc.vector.bn_aggr(mv[:, j, :], st[:, j, :])
                    last.then_inc(S.stats_ready, 1)

                def norm(a):
                    dve.wait_ge(S.rstd_ready, a.u + 1)
                    later(dve, S.hnT_psum, a.u)
                    for j in range(4):
                        last = nc.vector.tensor_scalar(hn[:, j, :], Hb[:, ds(4 * F * a.u + j * F, F)],
                                                       mv[:, j, 0:1], rstd[:, j:j + 1], ALU.subtract,
                                                       ALU.mult)
                    last.then_inc(S.hn_ready, 1)

                def dt_first(b):
                    dve.wait_ge(S.pd_ready, b.u + 1)
                    ins = nc.vector.tensor_tensor(uu.rearrange("p (j h) -> p j h", h=NH),
                                                  psum[0:CH, 1, :].rearrange("p (j n) -> p j n", n=128)
                                                  [:, :, 124:128],
                                                  dtb[:, :].unsqueeze(1).broadcast_to([CH, 4, NH]), ALU.add)
                    ins.then_inc(S.dtu_ready, 1)
                    dve.wait_ge(S.dtu_ready, b.u + 1)
                    later(dve, S.exp_ready, b.u)
                    nc.vector.scalar_tensor_tensor(nab, uu, -1.0, uu, ALU.mult, ALU.min)\
                        .then_inc(S.nab_ready, 1)

                def dt_rest(b):
                    dve.wait_ge(S.exp_ready, b.u + 1)
                    own(nc.vector.tensor_scalar(qq, ee, 2.0, None, ALU.add))
                    own(nc.vector.reciprocal(rq, qq))
                    own(nc.vector.tensor_tensor(ss, ee, rq, ALU.mult))
                    own(nc.vector.tensor_tensor(s2, ss, ss, ALU.mult))
                    own(nc.vector.tensor_scalar(pa, s2, 1.0 / 15, None, ALU.mult))
                    src, dst = pa, pb
                    for k in (13, 11, 9, 7, 5, 3):
                        own(nc.vector.scalar_tensor_tensor(dst, src, 1.0 / k, s2, ALU.add, ALU.mult))
                        src, dst = dst, src
                    own(nc.vector.scalar_tensor_tensor(tt, src, 1.0, ss, ALU.add, ALU.mult))
                    own(nc.vector.tensor_scalar(qq, uu, 0.0, None, ALU.max))
                    nc.vector.scalar_tensor_tensor(dt[b.q], tt, 2.0, qq, ALU.mult, ALU.add)\
                        .then_inc(S.dt_ready, 1)

                def x_scale(c):
                    dve.wait_ge(S.px_ready, c.u + 1)
                    dve.wait_ge(S.dt_ready, c.u + 1)
                    later(dve, S.y_psum, 2 * c.u)
                    nc.vector.tensor_tensor(Xd.rearrange("p j (h d) -> p (j h) d", d=HD),
                                            psum[0:CH, 5:7, :].rearrange("p k (g d) -> p (k g) d", d=HD),
                                            dt[c.q].unsqueeze(2).broadcast_to([CH, 4 * NH, HD]),
                                            ALU.mult).then_inc(S.xd_ready, 1)

                def scans(c, b):
                    w = 2 * c.u + b
                    dve.wait_ge(S.pb_ready, w + 1)
                    for g in range(2):
                        nc.vector.tensor_tensor_scan(
                            L0.rearrange("p h t -> p (h t)")[:, g * 2 * L:(g + 1) * 2 * L],
                            psum[0:CH, 5 + g, 0:2 * L], diag2.rearrange("p h t -> p (h t)"),
                            0.0, ALU.mult, ALU.add)
                    for h in range(NH):
                        col = (h % 2) * L + CH
                        last = nc.vector.tensor_tensor_scan(L1[:, h, :], psum[0:CH, 5 + h // 2, col:col + CH],
                                                            ident[0:CH, 0:CH], 0.0, ALU.mult, ALU.add)
                    last.then_inc(S.scan_done, 1)

                def decayed_scores(c, b):
                    w = 2 * c.u + b
                    dve.wait_ge(S.scan_done, w + 1)
                    dve.wait_ge(S.g_ready, w + 1)
                    later(dve, S.y_psum, w)
                    nc.vector.tensor_tensor(M0, L0, psum[0:CH, 4, 0:L].unsqueeze(1).broadcast_to([CH, NH, L]),
                                            ALU.mult)
                    nc.vector.tensor_tensor(M1, L1, psum[0:CH, 4, L:L + CH].unsqueeze(1)
                                            .broadcast_to([CH, NH, CH]), ALU.mult).then_inc(S.m_ready, 1)

                def skip_add(c, b):
                    w = 2 * c.u + b
                    dve.wait_ge(S.y_psum, w + 1)
                    if b == 0:
                        later(dve, S.yg_ready, 2 * c.u)
                    for k in range(2):
                        last = nc.vector.scalar_tensor_tensor(
                            Tg[:, k, b * L:(b + 1) * L], XT[c.q][:, k, b * L:(b + 1) * L], d_col[:, k:k + 1],
                            psum[:, 7, k * L:(k + 1) * L], ALU.mult, ALU.add)
                    last.then_inc(S.t_ready, 1)

                def sum_squares(c):
                    dve.wait_ge(S.sq_ready, 2 * c.u + 2)
                    nc.vector.tensor_tensor(Sq[:, 0, :], Sq[:, 0, :], Sq[:, 1, :], ALU.add)\
                        .then_inc(S.sq_summed, 1)

                def mean_squares(c):
                    dve.wait_ge(S.pr_ready, c.u + 1)
                    nc.vector.tensor_scalar(ms, psum[0:CH, 4, 480:484], 1.0 / DI, EPS, ALU.mult, ALU.add)\
                        .then_inc(S.ms_ready, 1)

                def residual(c):
                    dve.wait_ge(S.rr_ready, c.u + 1)
                    dve.wait_ge(S.po_ready, c.u + 1)
                    for j in range(4):
                        row = Hb[:, ds(4 * F * c.u + j * F, F)]
                        last = nc.vector.scalar_tensor_tensor(row, psum[0:CH, 7, j * F:(j + 1) * F],
                                                              rr[:, j:j + 1], row, ALU.mult, ALU.add)
                    last.then_inc(S.po_used, 1)

                def new_stats(c):
                    dve.wait_ge(S.po_used, c.u + 1)
                    nc.vector.memset(wait_carrier[:, :], 0.0)
                    for j in range(4):
                        last = nc.vector.bn_stats(st3[:, j, :], Hb[:, ds(4 * F * c.u + j * F, F)])
                    own(last)
                    nc.vector.memset(wait_carrier[:, :], 0.0)
                    for j in range(4):
                        last = nc.vector.bn_aggr(mv3[:, j, :], st3[:, j, :])
                    own(last)
                    nc.vector.tensor_copy(MV[:, ds(4 * c.u, 4), :], mv3[:, :, :])

                def body(a, b, c):
                    if b: dt_first(b)
                    if c: scans(c, 0); decayed_scores(c, 0)
                    if b:
                        own_begin((a.u if a else UNITS) + 13 * b.u + 2 * (c.u if c else 0))
                        dt_rest(b)
                    if a: conv_scale(a)
                    if c: skip_add(c, 0); scans(c, 1); decayed_scores(c, 1)
                    if a:
                        own_begin(a.u + 13 * (b.u + 1 if b else 0) + 2 * (c.u if c else 0))
                        stats(a)
                    if c: skip_add(c, 1)
                    if a: norm(a)
                    if b: x_scale(b)
                    if c: sum_squares(c); mean_squares(c)
                    if a: hn_rest(a)
                    if c:
                        residual(c)
                        own_begin((a.u + 1 if a else UNITS) + 13 * (b.u + 1 if b else UNITS) + 2 * c.u)
                        new_stats(c)
                skewed(dve, body, UNITS)

        names = ("var_ready r1_ready t_ready r2_ready xnr_ready xnr_used xT_psum hhT_ready hhT_copied "
                 "lg_psum lg_ready dve_own")
        B = namedtuple("B", names)(*[sem("b_" + n) for n in names.split()])
        with nc.Block() as block:
            @block.gpsimd
            def _(pool):
                def keep_rows(u):
                    pool.wait_ge(B.xnr_ready, u.u + 1)
                    pool.sem_inc(pool_turns)
                    rows_of = xnr[u.q].rearrange("p j f -> p (j f)")
                    nc.gpsimd.tensor_tensor(XNR[:, ds(4 * F * u.u, 4 * F)], rows_of,
                                            ones_col[0:CH, :].broadcast_to([CH, 4 * F]), ALU.mult)\
                        .then_inc(B.xnr_used, 1)
                streamed(pool, keep_rows, UNITS)

            @block.vector
            def _(dve):
                mean, var = MV[:, :, 0], MV[:, :, 1]
                nc.vector.tensor_scalar(v64[0], var, EPS, None, ALU.add).then_inc(B.var_ready, 1)
                dve.wait_ge(B.r1_ready, 1)
                link(dve, dve_step, nc.vector.reciprocal(v64[1], v64[1]))
                link(dve, dve_step, nc.vector.tensor_tensor(v64[2], var, v64[1], ALU.mult))
                link(dve, dve_step, nc.vector.tensor_tensor(v64[2], v64[2], v64[1], ALU.mult))
                nc.vector.tensor_scalar(v64[2], v64[2], EPS, None, ALU.add).then_inc(B.t_ready, 1)
                nc.vector.tensor_scalar(w_s2[:, :, :], w_s2[:, :, :], 0.25, None, ALU.mult)
                nc.vector.tensor_scalar(r1p, v64[1], 1.0, None, ALU.add)
                nc.vector.scalar_tensor_tensor(nmr, mean, -1.0, v64[1], ALU.mult, ALU.mult)
                dve.wait_ge(B.r2_ready, 1)
                link(dve, dve_step, nc.vector.reciprocal(v64[3], v64[3]))
                link(dve, dve_step, nc.vector.tensor_tensor(r12, v64[1], v64[3], ALU.mult))

                def normed(a):
                    later(dve, B.xnr_used, a.u - 1)
                    later(dve, B.xT_psum, a.u - 1)
                    for j in range(4):
                        last = nc.vector.tensor_scalar(xnr[a.q][:, j, :], Hb[:, ds(4 * F * a.u + j * F, F)],
                                                       MV[:, ds(4 * a.u + j, 1), 0], r12[:, ds(4 * a.u + j, 1)],
                                                       ALU.subtract, ALU.mult)
                    last.then_inc(B.xnr_ready, 1)

                def logits(c):
                    dve.wait_ge(B.lg_psum, c.u + 1)
                    nc.vector.tensor_tensor(LG[:, ds(4 * E * c.u, 4 * E)].rearrange("p (j e) -> p j e", e=E),
                                            psum[0:CH, 2 + c.q, :].rearrange("p (j n) -> p j n", j=4)
                                            [:, :, 0:E],
                                            rb[:, :].unsqueeze(1).broadcast_to([CH, 4, E]),
                                            ALU.add).then_inc(B.lg_ready, 1)

                def body(a, b, c):
                    if a: normed(a)
                    if c: logits(c)
                skewed(dve, body, UNITS)

            @block.scalar
            def _(act):
                act.wait_ge(B.var_ready, 1)
                nc.scalar.activation(v64[1], v64[0], ACT.Sqrt).then_inc(B.r1_ready, 1)
                act.wait_ge(B.t_ready, 1)
                nc.scalar.activation(v64[3], v64[2], ACT.Sqrt).then_inc(B.r2_ready, 1)

                def body(a, b, c):
                    if b:
                        act.wait_ge(B.xT_psum, b.u + 1)
                        later(act, B.lg_psum, b.u - 1)
                        later(act, B.hhT_copied, b.u - 1)
                        nc.scalar.activation(hhT[b.q], psum[:, b.q, 0:UT], ACT.Identity, scale=lng[:, 0:1],
                                             bias=lnb[:, 0:1]).then_inc(B.hhT_ready, 1)
                    if c:
                        act.wait_ge(B.hhT_ready, c.u + 1)
                        nc.scalar.activation(HHT[:, ds(512 * c.u, UT)], hhT[c.q], ACT.Copy)\
                            .then_inc(B.hhT_copied, 1)
                skewed(act, body, UNITS)

            @block.tensor
            def _(pe):
                def body(a, b, c):
                    if b:
                        pe.wait_ge(B.xnr_ready, b.u + 1)
                        later(pe, B.hhT_ready, b.u - 1)
                        for j in range(4):
                            last = nc.tensor.transpose(psum[:, b.q, j * CH:(j + 1) * CH], xnr[b.q][:, j, :],
                                                       ident[0:CH, 0:CH])
                        last.then_inc(B.xT_psum, 1)
                    if c:
                        pe.wait_ge(B.hhT_ready, c.u + 1)
                        later(pe, B.lg_ready, c.u - 1)
                        for j in range(4):
                            last = nc.tensor.matmul(psum[0:CH, 2 + c.q, j * 128:(j + 1) * 128],
                                                    hhT[c.q][:, j * CH:(j + 1) * CH], rw[:, :],
                                                    start=True, stop=True)
                        last.then_inc(B.lg_psum, 1)
                skewed(pe, body, UNITS)

        names = ("diff_ready exp_ready mask_ready ranks_ready")
        R = namedtuple("R", names)(*[sem("r_" + n) for n in names.split()])
        with nc.Block() as block:
            ge = lambda v: v.rearrange("p (g e) -> p g e", e=E)
            Dg, Ex, Key, Oh1, Lg2, Oh2, Wk, TE, CUM = [ge(v[0:CH, :]) for v in big]
            TEe = big[7].rearrange("p (e g) -> p e g", g=NCH)
            CUMe = big[8].rearrange("p (e g) -> p e g", g=NCH)
            LGg = ge(LG)
            over_e = lambda v: v.unsqueeze(2).broadcast_to([CH, NCH, E])
            each_g = lambda v: v.unsqueeze(1).broadcast_to([CH, NCH, E])
            m1, k1, m2, rs, e1, e2 = row

            @block.gpsimd
            def _(pool):
                assert 2 * NCH <= F
                nc.gpsimd.iota(row_ids[:, 0:2 * NCH], pattern=[[1, 2 * NCH]], base=0,
                               channel_multiplier=2 * NCH)
                for q in range(4):
                    nc.gpsimd.memset(x_st[q].rearrange("p j k f -> p (j k f)"), 0.0)

            @block.scalar
            def _(act):
                act.wait_ge(R.diff_ready, 1)
                nc.scalar.activation(Ex, Dg, ACT.Exp, scale=1.0 / TEMP).then_inc(R.exp_ready, 1)

            @block.tensor
            def _(pe):
                pe.wait_ge(R.mask_ready, 1)
                for k in range(2):
                    nc.tensor.matmul(psum[0:CH, k, :], tri[:, :], mask[:, k * 512:(k + 1) * 512],
                                     start=True, stop=True)
                    last = nc.tensor.matmul(psum[:, 2 + k, :], ones_sq[:, :], mask[:, k * 512:(k + 1) * 512],
                                            start=True, stop=True)
                last.then_inc(R.ranks_ready, 1)

            @block.vector
            def _(dve):
                def step(ins):
                    link(dve, dve_step, ins)

                V = nc.vector
                step(V.tensor_reduce(m1, LGg, AX.X, ALU.max))
                V.tensor_tensor(Dg, LGg, over_e(m1), ALU.subtract).then_inc(R.diff_ready, 1)
                step(V.tensor_tensor(Key, LGg, over_e(m1), ALU.is_equal))
                step(V.tensor_tensor(Key, Key, each_g(rev_iota[0:CH, :]), ALU.mult))
                step(V.tensor_reduce(k1, Key, AX.X, ALU.max))
                step(V.tensor_tensor(Oh1, each_g(rev_iota[0:CH, :]), over_e(k1), ALU.is_equal))
                step(V.scalar_tensor_tensor(Lg2, Oh1, -3.0e38, LGg, ALU.mult, ALU.add))
                step(V.tensor_reduce(m2, Lg2, AX.X, ALU.max))
                step(V.tensor_tensor(Key, Lg2, over_e(m2), ALU.is_equal))
                step(V.tensor_tensor(Key, Key, each_g(rev_iota[0:CH, :]), ALU.mult))
                step(V.tensor_reduce(k1, Key, AX.X, ALU.max))
                step(V.tensor_tensor(Oh2, each_g(rev_iota[0:CH, :]), over_e(k1), ALU.is_equal))
                V.tensor_tensor(ge(mask), Oh1, Oh2, ALU.add).then_inc(R.mask_ready, 1)
                dve.wait_ge(R.ranks_ready, 1)
                step(V.tensor_copy(TEe, psum[:, 2:4, :].rearrange("p k (g e) -> p e (k g)", e=E)))
                step(V.tensor_tensor_scan(big[8], big[7], big[7], 0.0, ALU.add, ALU.max))
                prev, cnt, blocks, t0, t1, base = sml[0:6]
                ends = CUMe[:, :, NCH - 1]
                step(V.memset(prev, 0.0))
                step(V.tensor_copy(prev[:, 1:E], ends[:, 0:E - 1]))
                step(V.tensor_tensor(cnt, ends, prev, ALU.subtract))
                step(V.tensor_scalar(t0, cnt, (BLK - 1) / 2.0, 1.0 / BLK, ALU.add, ALU.mult))
                step(V.tensor_scalar(t1, t0, 8388608.0, None, ALU.add))
                step(V.tensor_scalar(blocks, t1, -8388608.0, None, ALU.add))
                step(V.tensor_tensor_scan(cumP[:, :], blocks, blocks, 0.0, ALU.add, ALU.max))
                step(V.tensor_tensor(t0, cumP[:, :], blocks, ALU.subtract))
                step(V.scalar_tensor_tensor(base, t0, float(BLK), prev, ALU.mult, ALU.subtract))
                step(V.tensor_tensor(CUMe, CUMe, TEe, ALU.subtract))
                step(V.tensor_tensor(CUMe, CUMe, base.unsqueeze(2).broadcast_to([128, E, NCH]), ALU.add))
                step(V.tensor_tensor(Lg2, psum[0:CH, 0:2, :].rearrange("p k (g e) -> p (k g) e", e=E),
                                     CUMe[0:CH].rearrange("p e g -> p g e"), ALU.add))
                step(V.tensor_tensor(Wk, Oh1, Lg2, ALU.mult))
                step(V.tensor_reduce(m1, Wk, AX.X, ALU.add))
                V.tensor_copy(IDX[0:CH, :, 0], m1)
                step(V.tensor_tensor(Key, Oh2, Lg2, ALU.mult))
                step(V.tensor_reduce(m2, Key, AX.X, ALU.add))
                V.tensor_copy(IDX[0:CH, :, 1], m2)

        names = ("st_ready0 st_ready1 st_ready2 st_ready3 scat0 scat1 scat2 scat3 wload up_psum "
                 "up_used comb_ready comb_psum combT_ready "
                 "down_psum moe_ready experts_known")
        C = namedtuple("C", names)(*[sem("c_" + n) for n in names.split()])
        scattered = (C.scat0, C.scat1, C.scat2, C.scat3)
        staged = (C.st_ready0, C.st_ready1, C.st_ready2, C.st_ready3)
        with nc.Block() as block:
            @block.sync
            def _(sp):
                sp.wait_ge(C.experts_known, 1)
                sp.dma_start(w1.rearrange("p (e h) -> p e h", e=E)[:, :, 0:DH],
                             ew1.rearrange("e d h -> d e h")).then_inc(C.wload, 16)
                for e in range(E):
                    sp.dma_start(w2[:, e * EW:e * EW + DH].rearrange("p (c d) -> p c d", d=F),
                                 ew2[e].rearrange("(c p) d -> p c d", p=128)).then_inc(C.wload, 16)
                sp.wait_ge(C.wload, 16 * (E + 1))

            @block.gpsimd
            def _(pool):
                last_slot = pool.to_reg(SLOTS - 1)

                def scatter(u):
                    pool.wait_ge(staged[u.q], u.n + 1)
                    pool.sem_inc(pool_turns)
                    for j in range(4):
                        for k in range(2):
                            nc.gpsimd.indirect_dma_start(
                                out=x_slots, out_offset=bass.IndirectOffsetOnAxis(
                                    ap=idx_st[u.q][:, 2 * j + k:2 * j + k + 1], axis=0),
                                in_=x_st[u.q][:, j, k, :], in_offset=None,
                                bounds_check=last_slot, oob_is_err=False).then_inc(scattered[u.q], 16)
                streamed(pool, scatter, UNITS, 4)
                for q in range(4):
                    pool.wait_ge(scattered[q], 16 * 8 * (UNITS // 4))

            @block.scalar
            def _(act):
                def stage(u):
                    if not isinstance(u.n, int) or u.n > 0:
                        act.wait_ge(scattered[u.q], 128 * u.n)
                    nc.scalar.activation(idx_st[u.q][:, :], IDX[:, ds(4 * u.u, 4), :]
                                         .rearrange("p j k -> p (j k)"), ACT.Copy)
                    nc.scalar.activation(x_st[u.q][0:CH, :, :, F].rearrange("p j k -> p (j k)"),
                                         row_ids[:, ds(8 * u.u, 8)], ACT.Copy)
                    for k in range(2):
                        last = nc.scalar.activation(x_st[u.q][0:CH, :, k, 0:F],
                                                    XNR[:, ds(4 * F * u.u, 4 * F)]
                                                    .rearrange("p (j f) -> p j f", f=F), ACT.Copy)
                    last.then_inc(staged[u.q], 1)

                def shared(b):
                    act.wait_ge(C.up_psum, b.u + 1)
                    later(act, C.down_psum, b.u)
                    for k in range(2):
                        last = nc.scalar.activation(SH[:, k, :], psum[:, k, 0:UT], ACT.Silu,
                                                    bias=b_s1[:, k:k + 1])
                    last.then_inc(C.up_used, 1)
                    for j in range(4):
                        h = Hb[:, ds(4 * F * b.u + j * F, F)]
                        nc.scalar.activation(h, h, ACT.Identity, scale=r1p[:, ds(4 * b.u + j, 1)],
                                             bias=nmr[:, ds(4 * b.u + j, 1)])
                ahead(act, stage, shared, UNITS, 4, 4)

            @block.tensor
            def _(pe):
                def body(a, b, c):
                    if b:
                        later(pe, C.up_used, b.u)
                        for k in range(2):
                            last = nc.tensor.matmul(psum[:, k, 0:UT], w_s1[:, k * 128:(k + 1) * 128],
                                                    HHT[:, ds(512 * b.u, UT)], start=True, stop=True)
                        last.then_inc(C.up_psum, 1)
                        pe.wait_ge(C.comb_ready, b.u + 1)
                        later(pe, C.combT_ready, b.u)
                        for j in range(4):
                            last = nc.tensor.transpose(psum[0:CB, 2, j * CH:(j + 1) * CH], comb_st[:, j, :],
                                                       ident[0:CH, 0:CH])
                        last.then_inc(C.comb_psum, 1)
                        pe.wait_ge(C.up_used, b.u + 1)
                        pe.wait_ge(C.combT_ready, b.u + 1)
                        later(pe, C.moe_ready, b.u)
                        for j in range(4):
                            o = psum[0:CH, 3, j * F:(j + 1) * F]
                            t = slice(j * CH, (j + 1) * CH)
                            for k in range(2):
                                nc.tensor.matmul(o, SH[:, k, t], w_s2[:, k, :], start=(k == 0), stop=False)
                            last = nc.tensor.matmul(o, combT[:, t], w_e2b[:, :], start=False, stop=True)
                        last.then_inc(C.down_psum, 1)
                skewed(pe, body, UNITS)

            @block.vector
            def _(dve):
                def step(ins):
                    link(dve, dve_step, ins)

                V = nc.vector
                rs, e1, e2 = row[3:6]
                step(V.tensor_reduce(rs, Ex, AX.X, ALU.add))
                step(V.reciprocal(rs, rs))
                step(V.tensor_tensor(Wk, Oh1, Ex, ALU.mult))
                step(V.tensor_reduce(e1, Wk, AX.X, ALU.add))
                step(V.tensor_tensor(VAL[:, 0, :], e1, rs, ALU.mult))
                step(V.tensor_tensor(Wk, Oh2, Ex, ALU.mult))
                step(V.tensor_reduce(e2, Wk, AX.X, ALU.add))
                step(V.tensor_tensor(VAL[:, 1, :], e2, rs, ALU.mult))
                step(V.tensor_tensor(Wk, Oh1, over_e(VAL[:, 0, :]), ALU.mult))
                step(V.tensor_tensor(Key, Oh2, over_e(VAL[:, 1, :]), ALU.mult))
                step(V.tensor_tensor(COMB[:, :].rearrange("p (g e) -> p g e", e=CB)[:, :, 0:E], Wk, Key,
                                     ALU.add))
                blkE = arena[0:1, big_at:big_at + NBLK * E].rearrange("p (j e) -> p j e", e=E)
                blkN = sml_blocks
                step(V.tensor_tensor(blkE, cumP[0:1, :].unsqueeze(1).broadcast_to([1, NBLK, E]),
                                     block_no[:, :].unsqueeze(2).broadcast_to([1, NBLK, E]), ALU.is_le))
                step(V.tensor_reduce(blkN, blkE, AX.X, ALU.add))
                step(V.tensor_scalar(blkN, blkN, float(E - 1), float(EW), ALU.min, ALU.mult))
                step(V.tensor_copy(EOFF[:, :], blkN))
                nc.vector.tensor_copy(w1.rearrange("p (e h) -> p e h", e=E)[:, :, DH:EW],
                                      b_e1[:, :].rearrange("p (e k) -> p e k", e=E))\
                    .then_inc(C.experts_known, 1)

                def body(a, b, c):
                    if b:
                        later(dve, C.comb_psum, b.u)
                        nc.vector.tensor_copy(comb_st.rearrange("p j e -> p (j e)"),
                                              COMB[:, ds(4 * CB * b.u, 4 * CB)]).then_inc(C.comb_ready, 1)
                        dve.wait_ge(C.comb_psum, b.u + 1)
                        later(dve, C.down_psum, b.u)
                        nc.vector.tensor_copy(combT, psum[0:CB, 2, 0:UT]).then_inc(C.combT_ready, 1)
                    if c:
                        dve.wait_ge(C.down_psum, c.u + 1)
                        nc.vector.tensor_copy(MOE[:, ds(512 * c.u, 512)], psum[0:CH, 3, :])\
                            .then_inc(C.moe_ready, 1)
                skewed(dve, body, UNITS)

        names = ("xb0 xb1 xb2 xb3 xT_psum hT_ready w1_ready up_psum eh_ready down_psum yo_ready "
                 "row_ready yst0 yst1 yst2 yst3")
        X = namedtuple("X", names)(*[sem("x_" + n) for n in names.split()])
        x_here = (X.xb0, X.xb1, X.xb2, X.xb3)
        y_stored = (X.yst0, X.yst1, X.yst2, X.yst3)
        with nc.Block() as block:
            @block.sync
            def _(sp):
                def load(t):
                    later(sp, X.xT_psum, t.u - 3)
                    later(sp, X.row_ready, t.u - 3)
                    sp.dma_start(xb[t.q], x_slots[ds(BLK * t.u, BLK), :]).then_inc(x_here[t.q], 16)
                streamed(sp, load, NBLK, 4)

            @block.tensor
            def _(pe):
                def body(a, b, c):
                    if c:
                        at = pe.value_load(EOFF[0:1, ds(c.u, 1)], min_val=0, max_val=(E - 1) * EW)
                    if b:
                        pe.wait_ge(X.w1_ready, b.u + 1)
                        pe.wait_ge(X.hT_ready, b.u + 1)
                        later(pe, X.eh_ready, b.u - 1)
                        for k in range(NF):
                            last = nc.tensor.matmul(psum[:, 2 + b.q % 2, k * 128:(k + 1) * 128],
                                                    w1_blk[b.q][:, k * 128:(k + 1) * 128], hT[b.q % 2],
                                                    start=True, stop=True)
                        last.then_inc(X.up_psum, 1)
                    if a:
                        pe.wait_ge(x_here[a.q], 16 * (a.n + 1))
                        later(pe, X.hT_ready, a.u - 1)
                        nc.tensor.transpose(psum[:, a.q % 2, 0:BLK], xb[a.q][:, 0:F], ident[:, :])\
                            .then_inc(X.xT_psum, 1)
                    if c:
                        pe.wait_ge(X.eh_ready, c.u + 1)
                        later(pe, X.yo_ready, c.u - 1)
                        for k in range(NF):
                            last = nc.tensor.matmul(psum[:, 4 + c.q % 2, 0:F],
                                                    EHT[c.q % 2][:, k * 128:(k + 1) * 128],
                                                    w2[:, ds(at + k * F, F)], start=(k == 0),
                                                    stop=(k == NF - 1))
                        last.then_inc(X.down_psum, 1)
                skewed(pe, body, NBLK, 4)

            @block.scalar
            def _(act):
                def body(a, b, c):
                    if b:
                        act.wait_ge(X.up_psum, b.u + 1)
                        later(act, X.down_psum, b.u - 1)
                        for k in range(NF):
                            last = nc.scalar.activation(EHT[b.q % 2][:, k * 128:(k + 1) * 128],
                                                        psum[:, 2 + b.q % 2, k * 128:(k + 1) * 128],
                                                        ACT.Silu, bias=w1_blk[b.q][:, DH + k:DH + k + 1])
                        last.then_inc(X.eh_ready, 1)
                    if c:
                        act.wait_ge(X.down_psum, c.u + 1)
                        later(act, y_stored[c.q], 16 * c.n)
                        nc.scalar.activation(YO[c.q], psum[:, 4 + c.q % 2, 0:F], ACT.Copy)\
                            .then_inc(X.yo_ready, 1)
                skewed(act, body, NBLK, 4)

            @block.gpsimd
            def _(pool):
                last_row = pool.to_reg(CH * 2 * NCH - 1)

                def scatter(t):
                    pool.wait_ge(X.row_ready, t.u + 1)
                    pool.sem_inc(pool_turns)
                    pool.wait_ge(X.yo_ready, t.u + 1)
                    pool.sem_inc(pool_turns)
                    nc.gpsimd.indirect_dma_start(
                        out=y_tokens, out_offset=bass.IndirectOffsetOnAxis(ap=y_row[t.q], axis=0),
                        in_=YO[t.q], in_offset=None, bounds_check=last_row, oob_is_err=False)\
                        .then_inc(y_stored[t.q], 16)
                streamed(pool, scatter, NBLK, 4)
                for q in range(4):
                    pool.wait_ge(y_stored[q], 16 * (NBLK // 4))

            @block.vector
            def _(dve):
                def prepare(t):
                    at = dve.value_load(EOFF[0:1, ds(t.u, 1)], min_val=0, max_val=(E - 1) * EW)
                    later(dve, X.eh_ready, t.u - 3)
                    nc.vector.tensor_copy(w1_blk[t.q], w1[:, ds(at, EW)]).then_inc(X.w1_ready, 1)
                    dve.wait_ge(X.xT_psum, t.u + 1)
                    later(dve, X.up_psum, t.u - 1)
                    nc.vector.tensor_scalar(hT[t.q % 2], psum[:, t.q % 2, 0:BLK], lng[:, 0:1],
                                            lnb[:, 0:1], ALU.mult, ALU.add).then_inc(X.hT_ready, 1)
                    later(dve, y_stored[t.q], 16 * t.n)
                    nc.vector.tensor_copy(y_row[t.q], xb[t.q][:, F:F + 1]).then_inc(X.row_ready, 1)
                streamed(dve, prepare, NBLK, 4)

        names = ("y0 y1 h_ready mixed ve_ready rs_ready fh_ready fhT_psum fhT_ready "
                 "up_psum up_used down_psum rest_ready out_ready st0 st1 own dve_own")
        D = namedtuple("D", names)(*[sem("d_" + n) for n in names.split()])
        y_here = (D.y0, D.y1)
        stored = (D.st0, D.st1)
        with nc.Block() as block:
            outv = out.rearrange("(g p) f -> p g f", p=CH)

            @block.sync
            def _(sp):
                yv = y_tokens.rearrange("(p r) f -> p r f", p=CH)

                def load(u):
                    later(sp, D.mixed, u.u - 1)
                    for p0, p1 in ((0, 112), (112, CH)):
                        sp.dma_start(GY[u.q][p0:p1, :, :], yv[p0:p1, ds(8 * u.u, 8), :])\
                          .then_inc(y_here[u.q], 16)

                def store(u):
                    sp.wait_ge(D.out_ready, u.u + 1)
                    for p0, p1 in ((0, 112), (112, CH)):
                        sp.dma_start(outv[p0:p1, ds(4 * u.u, 4), :],
                                     outb[u.q][p0:p1, :].rearrange("p (j f) -> p j f", f=F))\
                          .then_inc(stored[u.q], 16)

                ahead(sp, load, store, UNITS, 4)
                for q in range(2):
                    sp.wait_ge(stored[q], 32 * (UNITS // 2))

            @block.gpsimd
            def _(pool):
                own_begin, own = stepper(pool, D.own)

                def body(a, b, c):
                    if a:
                        pool.wait_ge(D.ve_ready, a.u + 1)
                        nc.gpsimd.tensor_tensor(rs3[:, :], ve3[:, :], minus_half[0:CH, 0:4], ALU.pow)\
                            .then_inc(D.rs_ready, 1)
                    if b:
                        pool.wait_ge(D.mixed, b.u + 1)
                        pool.wait_ge(D.h_ready, b.u + 1)
                        later(pool, D.out_ready, b.u - 1)
                        own_begin(b.u)
                        own(nc.gpsimd.tensor_tensor(rest2, h_st, mo[b.q].rearrange("p j f -> p (j f)"),
                                                    ALU.add))
                        nc.gpsimd.tensor_tensor(rest[b.q].rearrange("p (j f) -> p j f", f=F),
                                                rest2.rearrange("p (j f) -> p j f", f=F),
                                                b_f2[:, :].unsqueeze(1).broadcast_to([CH, 4, F]), ALU.add)\
                            .then_inc(D.rest_ready, 1)
                skewed(pool, body, UNITS)

            @block.vector
            def _(dve):
                step_begin, step = stepper(dve, D.dve_own)

                def mixture(a):
                    dve.wait_ge(y_here[a.q], 32 * (a.n + 1))
                    later(dve, D.rest_ready, a.u - 1)
                    for j in range(4):
                        last = nc.vector.scalar_tensor_tensor(
                            mo[a.q][:, j, :], GY[a.q][:, 2 * j, :], VAL[:, 0, ds(4 * a.u + j, 1)],
                            MOE[:, ds(512 * a.u + j * F, F)], ALU.mult, ALU.add)
                    step(last)
                    for j in range(4):
                        last = nc.vector.scalar_tensor_tensor(
                            mo[a.q][:, j, :], GY[a.q][:, 2 * j + 1, :], VAL[:, 1, ds(4 * a.u + j, 1)],
                            mo[a.q][:, j, :], ALU.mult, ALU.add)
                    last.then_inc(D.mixed, 1)
                    dve.wait_ge(D.mixed, a.u + 1)
                    nc.vector.memset(wait_carrier[:, :], 0.0)
                    for j in range(4):
                        last = nc.vector.bn_stats(st3[:, j, :], mo[a.q][:, j, :])
                    step(last)
                    nc.vector.memset(wait_carrier[:, :], 0.0)
                    for j in range(4):
                        last = nc.vector.bn_aggr(mv3[:, j, :], st3[:, j, :])
                    step(last)
                    nc.vector.tensor_scalar(ve3[:, :], mv3[:, :, 1], EPS, None, ALU.add).then_inc(D.ve_ready, 1)

                def norm(a):
                    dve.wait_ge(D.rs_ready, a.u + 1)
                    later(dve, D.fhT_psum, a.u)
                    for j in range(4):
                        last = nc.vector.tensor_scalar(fh[:, j, :], mo[a.q][:, j, :], mv3[:, j, 0:1],
                                                       rs3[:, j:j + 1], ALU.subtract, ALU.mult)
                    last.then_inc(D.fh_ready, 1)

                def final(c):
                    dve.wait_ge(D.down_psum, c.u + 1)
                    dve.wait_ge(D.rest_ready, c.u + 1)
                    later(dve, stored[c.q], 32 * c.n)
                    nc.vector.tensor_tensor(outb[c.q], psum[0:CH, 5, :], rest[c.q], ALU.add)\
                        .then_inc(D.out_ready, 1)

                def body(a, b, c):
                    if a:
                        step_begin(3 * a.u)
                        mixture(a)
                        norm(a)
                    if c: final(c)
                skewed(dve, body, UNITS)

            @block.tensor
            def _(pe):
                def body(a, b, c):
                    if b:
                        pe.wait_ge(D.fh_ready, b.u + 1)
                        later(pe, D.fhT_ready, b.u)
                        for j in range(4):
                            last = nc.tensor.transpose(psum[:, 0, j * CH:(j + 1) * CH], fh[:, j, :],
                                                       ident[0:CH, 0:CH])
                        last.then_inc(D.fhT_psum, 1)
                    if c:
                        pe.wait_ge(D.up_used, 4 * c.u + 4)
                        later(pe, D.out_ready, c.u)
                        for j in range(4):
                            for k in range(NF):
                                last = nc.tensor.matmul(psum[0:CH, 5, j * F:(j + 1) * F],
                                                        FH[:, k, j * CH:(j + 1) * CH], w_f2[:, k, :],
                                                        start=(k == 0), stop=(k == NF - 1))
                        last.then_inc(D.down_psum, 1)
                    if b:
                        pe.wait_ge(D.fhT_ready, b.u + 1)
                        for k in range(NF):
                            nc.tensor.matmul(psum[:, 1 + k, 0:UT], w_f1[:, k * 128:(k + 1) * 128], fhT,
                                             start=True, stop=True).then_inc(D.up_psum, 1)
                skewed(pe, body, UNITS)

            @block.scalar
            def _(act):
                def body(a, b, c):
                    if b:
                        act.wait_ge(D.fhT_psum, b.u + 1)
                        later(act, D.up_psum, 4 * b.u)
                        nc.scalar.activation(fhT, psum[:, 0, 0:UT], ACT.Identity, scale=fg[:, 0:1],
                                             bias=fbb[:, 0:1]).then_inc(D.fhT_ready, 1)
                        later(act, D.rest_ready, b.u)
                        nc.scalar.activation(h_st, Hb[:, ds(4 * F * b.u, 4 * F)], ACT.Copy)\
                            .then_inc(D.h_ready, 1)
                        for k in range(NF):
                            act.wait_ge(D.up_psum, 4 * b.u + k + 1)
                            if k == 0:
                                later(act, D.down_psum, b.u)
                            nc.scalar.activation(FH[:, k, :], psum[:, 1 + k, 0:UT], ACT.Silu,
                                                 bias=b_f1[:, k:k + 1]).then_inc(D.up_used, 1)
                skewed(act, body, UNITS)


def kernel(**inputs):
    import numpy as np
    import concourse.bacc as bacc
    from concourse.bass_utils import run_bass_kernel_spmd

    w = {k: np.asarray(v) for k, v in inputs.items()}
    x = w["x"].reshape(32 * 256, 64)

    def cols(v, n):
        return v.reshape(n, 128).T

    arrays = {
        "x2": np.concatenate([x, np.concatenate([x[1:], x[:1]], axis=0)], axis=1),
        "tok_kernel": w["L0_tok_kernel"], "tok_bias": w["L0_tok_bias"],
        "in_proj": w["L0_attn_in_proj_w"], "conv_w": w["L0_attn_conv_w"].reshape(384 * 4),
        "conv_b": cols(w["L0_attn_conv_b"], 3), "dt_bias": w["L0_attn_dt_bias"],
        "A_log": w["L0_attn_A_log"], "D_skip": w["L0_attn_D_skip"],
        "norm_w": cols(w["L0_attn_norm_w"], 2), "out_proj": w["L0_attn_out_proj_w"],
        "ln_g": cols(w["L0_ffn_ln_in_g"], 1), "ln_b": cols(w["L0_ffn_ln_in_b"], 1),
        "router_w": w["L0_ffn_router_w"], "router_b": w["L0_ffn_router_b"],
        "ew1": w["L0_ffn_ew1"], "eb1": cols(w["L0_ffn_eb1"], 64), "ew2": w["L0_ffn_ew2"],
        "eb2": w["L0_ffn_eb2"],
        "sw1": w["L0_ffn_sw1"], "sb1": cols(w["L0_ffn_sb1"], 2), "sw2": w["L0_ffn_sw2"],
        "sb2": w["L0_ffn_sb2"], "ffg": cols(w["L0_ffn_ff_ln_g"], 1), "ffb": cols(w["L0_ffn_ff_ln_b"], 1),
        "fw1": w["L0_ffn_ff_w1"], "fb1": cols(w["L0_ffn_ff_b1"], 4), "fw2": w["L0_ffn_ff_w2"],
        "fb2": w["L0_ffn_ff_b2"],
    }
    arrays = {"in_" + k: np.ascontiguousarray(v) for k, v in arrays.items()}
    nc = bacc.Bacc("TRN2", target_bir_lowering=False, num_devices=1)
    fp32 = mybir.dt.float32
    args = [nc.dram_tensor(k, v.shape, fp32, kind="ExternalInput").ap() for k, v in arrays.items()]
    out = nc.dram_tensor("out_tokens", (32 * 248, 128), fp32, kind="ExternalOutput").ap()
    audio_tower(nc, *args, out)
    r = run_bass_kernel_spmd(nc, [arrays], core_ids=[0])
    return r.results[0]["out_tokens"].reshape(32, 248, 128)
```
